# Optimizing a Trainium2 kernel written in Bass

```python
import numpy as np
import jax
import jax.numpy as jnp

def _softmax(x, axis=-1):
    return jax.nn.softmax(x, axis=axis)

def _gelu(x):
    return jax.nn.gelu(x, approximate=True)

def _silu(x):
    return jax.nn.silu(x)

def _sigmoid(x):
    return jax.nn.sigmoid(x)

def _layernorm(x, axis=-1, eps=1e-05):
    m = jnp.mean(x, axis=axis, keepdims=True)
    v = jnp.var(x, axis=axis, keepdims=True)
    return (x - m) / jnp.sqrt(v + eps)

def _scatter_add(tgt, idx, src, axis=0):
    return tgt.at[idx].add(src)

def _segment_sum(src, seg, n):
    return jax.ops.segment_sum(src, seg, n)
kernel_name = 'mk_gnn_preln_d4_gnn_r64_dcde18'

def setup_inputs(seed: int=0):
    np.random.seed(seed)
    _w = jnp.asarray

    def _rec_inputs():
        import jax
        import jax.numpy as jnp
        _gk = jax.random.key(seed)
        x = 7.22e-05 + 1 * jax.random.normal(jax.random.fold_in(_gk, 1), (256, 512), jnp.float32)
        src = jax.random.randint(jax.random.fold_in(_gk, 2), (8192,), 0, 256, jnp.int32)
        dst = jax.random.randint(jax.random.fold_in(_gk, 3), (8192,), 0, 256, jnp.int32)
        _o = jnp.argsort(dst, stable=True)
        src = src[_o]
        dst = dst[_o]
        edge_attr_512 = -8.16379e-05 + 0.999858 * jax.random.normal(jax.random.fold_in(_gk, 13), (8192, 512), jnp.float32)
        node_vec1 = jax.random.uniform(jax.random.fold_in(_gk, 15), (256, 1), jnp.float32, 0.0, 0.999957)
        return (x, src, dst, edge_attr_512, node_vec1)
    x, src, dst, edge_attr_512, node_vec1 = _rec_inputs()

    def _L0_gnn_setup():
        import jax, jax.numpy as jnp
        import numpy as np
        N, E, H, L, G = (256, 2500, 512, 7, 128)
        LN_EPS = 1e-05
        EPS = 1e-07

        def _ln(x, g, b):
            m = jnp.mean(x, axis=-1, keepdims=True)
            v = jnp.var(x, axis=-1, keepdims=True)
            return (x - m) * jax.lax.rsqrt(v + LN_EPS) * g + b

        def _genconv(h, src, dst, W, b):
            msg = jax.nn.relu(h[src]) + EPS
            mmax = jax.ops.segment_max(msg, dst, num_segments=N)
            ex = jnp.exp(msg - mmax[dst])
            denom = jax.ops.segment_sum(ex, dst, num_segments=N)
            agg = jax.ops.segment_sum(msg * ex, dst, num_segments=N) / jnp.where(denom > 0, denom, 1.0)
            return (h + agg) @ W + b
        key = jax.random.key(seed)
        ks = jax.random.split(key, 8)
        s = 1.0 / np.sqrt(H)
        return {'x': jax.random.normal(ks[0], (N, H), jnp.float32), 'edge_index': jax.random.randint(ks[1], (2, E), 0, N), 'batch': jnp.sort(jax.random.randint(ks[2], (N,), 0, G)), 'gcn_W': jax.random.uniform(ks[3], (L, H, H), jnp.float32, -s, s), 'gcn_b': jnp.zeros((L, H), jnp.float32), 'norm_g': jnp.ones((L, H), jnp.float32), 'norm_b': jnp.zeros((L, H), jnp.float32), 'vn_emb': jnp.zeros((H,), jnp.float32), 'vn_W1': jax.random.uniform(ks[4], (L - 1, H, H), jnp.float32, -s, s), 'vn_b1': jnp.zeros((L - 1, H), jnp.float32), 'vn_g': jnp.ones((L - 1, H), jnp.float32), 'vn_beta': jnp.zeros((L - 1, H), jnp.float32), 'vn_W2': jax.random.uniform(ks[5], (L - 1, H, H), jnp.float32, -s, s), 'vn_b2': jnp.zeros((L - 1, H), jnp.float32)}
    _L0_gnn_all = _L0_gnn_setup()
    _L0_gnn_in = {k: v for k, v in _L0_gnn_all.items() if k in ('gcn_W', 'gcn_b', 'norm_g', 'norm_b', 'vn_emb', 'vn_W1', 'vn_b1', 'vn_g', 'vn_beta', 'vn_W2', 'vn_b2')}
    del _L0_gnn_all

    def _L1_gnn_setup():
        import jax, jax.numpy as jnp
        import numpy as np
        N_NODES = 40962
        LATENT_DIM = 512
        N_EDGES = 655392
        NUM_BLOCKS = 4
        NUM_HEADS = 4
        NUM_FREQ = 32
        BASE_PERIOD = 16
        NOISE_EMB_DIM = 16
        EPS = 1e-05

        def _cond_layer_norm(x, cond, sw, sb, bw, bb):
            mu = jnp.mean(x, axis=-1, keepdims=True)
            var = jnp.var(x, axis=-1, keepdims=True)
            xn = (x - mu) * jax.lax.rsqrt(var + EPS)
            scale = cond @ sw + sb
            bias = cond @ bw + bb
            return xn * (1.0 + scale) + bias

        def _sparse_attention(x, src, dst, wq, bq, wk, bk, wv, bv, wo, bo):
            N, D = x.shape
            H, Dh = (NUM_HEADS, D // NUM_HEADS)
            q = (x @ wq + bq).reshape(N, H, Dh) * Dh ** (-0.5)
            k = (x @ wk + bk).reshape(N, H, Dh)
            v = (x @ wv + bv).reshape(N, H, Dh)
            scores = jnp.einsum('ehd,ehd->eh', q[src], k[dst])
            smax = jax.ops.segment_max(scores, src, num_segments=N)
            ex = jnp.exp(scores - smax[src])
            denom = jax.ops.segment_sum(ex, src, num_segments=N)
            attn = ex / denom[src]
            out = jax.ops.segment_sum(attn[:, :, None] * v[dst], src, num_segments=N)
            return out.reshape(N, D) @ wo + bo

        def _forward(x, edge_index, noise_levels, f_w1, f_b1, f_w2, f_b2, s1_w, s1_b, b1_w, b1_b, wq, bq, wk, bk, wv, bv, wo, bo, s2_w, s2_b, b2_w, b2_b, m_w1, m_b1, m_w2, m_b2):
            src, dst = (edge_index[0], edge_index[1])
            freqs = jnp.arange(1, NUM_FREQ + 1, dtype=x.dtype) * (2.0 * np.pi / BASE_PERIOD)
            ph = noise_levels * freqs
            emb = jnp.concatenate([jnp.sin(ph), jnp.cos(ph)], axis=-1)
            cond = jax.nn.silu(emb @ f_w1 + f_b1) @ f_w2 + f_b2
            for i in range(NUM_BLOCKS):
                y = _cond_layer_norm(x, cond, s1_w[i], s1_b[i], b1_w[i], b1_b[i])
                y = _sparse_attention(y, src, dst, wq[i], bq[i], wk[i], bk[i], wv[i], bv[i], wo[i], bo[i])
                x = x + y
                y = _cond_layer_norm(x, cond, s2_w[i], s2_b[i], b2_w[i], b2_b[i])
                y = jax.nn.relu(y @ m_w1[i] + m_b1[i]) @ m_w2[i] + m_b2[i]
                x = x + y
            return x
        key = jax.random.key(seed)
        ks = jax.random.split(key, 20)

        def w(k, shape, s=0.02):
            return jax.random.normal(k, shape, dtype=jnp.float32) * s
        D, B, C = (LATENT_DIM, NUM_BLOCKS, NOISE_EMB_DIM)
        z = lambda *s: jnp.zeros(s, jnp.float32)
        return {'latent_mesh_nodes': jax.random.normal(ks[0], (N_NODES, D), dtype=jnp.float32), 'edge_index': jax.random.randint(ks[1], (2, N_EDGES), 0, N_NODES, dtype=jnp.int32), 'noise_levels': jax.random.uniform(ks[2], (N_NODES, 1), dtype=jnp.float32), 'f_w1': w(ks[3], (2 * NUM_FREQ, C)), 'f_b1': z(C), 'f_w2': w(ks[4], (C, C)), 'f_b2': z(C), 's1_w': w(ks[5], (B, C, D)), 's1_b': z(B, D), 'b1_w': w(ks[6], (B, C, D)), 'b1_b': z(B, D), 'wq': w(ks[7], (B, D, D)), 'bq': z(B, D), 'wk': w(ks[8], (B, D, D)), 'bk': z(B, D), 'wv': w(ks[9], (B, D, D)), 'bv': z(B, D), 'wo': w(ks[10], (B, D, D)), 'bo': z(B, D), 's2_w': w(ks[11], (B, C, D)), 's2_b': z(B, D), 'b2_w': w(ks[12], (B, C, D)), 'b2_b': z(B, D), 'm_w1': w(ks[13], (B, D, D)), 'm_b1': z(B, D), 'm_w2': w(ks[14], (B, D, D)), 'm_b2': z(B, D)}
    _L1_gnn_all = _L1_gnn_setup()
    _L1_gnn_in = {k: v for k, v in _L1_gnn_all.items() if k in ('f_w1', 'f_b1', 'f_w2', 'f_b2', 's1_w', 's1_b', 'b1_w', 'b1_b', 'wq', 'bq', 'wk', 'bk', 'wv', 'bv', 'wo', 'bo', 's2_w', 's2_b', 'b2_w', 'b2_b', 'm_w1', 'm_b1', 'm_w2', 'm_b2')}
    del _L1_gnn_all

    def _L2_gnn_setup():
        import jax, jax.numpy as jnp
        import numpy as np
        N = 50000
        IN_CH = 512
        OUT_CH = 512
        DEG = 32
        E = N * DEG
        key = jax.random.key(seed)
        kx, kwc, kwn, kb, ke = jax.random.split(key, 5)
        x = jax.random.normal(kx, (N, IN_CH), dtype=jnp.float32)
        bound = 1.0 / np.sqrt(IN_CH)
        wc = jax.random.uniform(kwc, (IN_CH, OUT_CH), minval=-bound, maxval=bound, dtype=jnp.float32)
        wn = jax.random.uniform(kwn, (IN_CH, OUT_CH), minval=-bound, maxval=bound, dtype=jnp.float32)
        bias = jax.random.uniform(kb, (OUT_CH,), minval=-bound, maxval=bound, dtype=jnp.float32)
        src = jnp.repeat(jnp.arange(N, dtype=jnp.int64), DEG)
        dst = jax.random.randint(ke, (E,), 0, N, dtype=jnp.int64)
        edge_index = jnp.stack([src, dst], axis=0)
        return {'x': x, 'wc': wc, 'wn': wn, 'bias': bias, 'edge_index': edge_index}
    _L2_gnn_all = _L2_gnn_setup()
    _L2_gnn_in = {k: v for k, v in _L2_gnn_all.items() if k in ('wc', 'wn', 'bias')}
    del _L2_gnn_all

    def _L3_gnn_setup():
        import jax, jax.numpy as jnp
        import numpy as np
        N_NODES = 20000
        N_EDGES = 3125
        N_SEG = 16
        EXTENT = 32
        N_PATHS = 64
        OP_SIZE = N_SEG * EXTENT
        key = jax.random.key(seed)
        k1, k2, k3, k4, k5, k6 = jax.random.split(key, 6)
        x_nodes = jax.random.normal(k1, (N_NODES, OP_SIZE), dtype=jnp.float32)
        x_edges = jax.random.normal(k2, (N_EDGES, OP_SIZE), dtype=jnp.float32)
        path_coeffs = jax.random.normal(k3, (N_PATHS,), dtype=jnp.float32)
        src = jax.random.randint(k4, (N_EDGES,), 0, N_NODES, dtype=jnp.int64)
        dst = jax.random.randint(k5, (N_EDGES,), 0, N_NODES, dtype=jnp.int64)
        path_indices = jax.random.randint(k6, (N_PATHS, 3), 0, N_SEG, dtype=jnp.int64)
        return {'x_nodes': x_nodes, 'x_edges': x_edges, 'path_coeffs': path_coeffs, 'src': src, 'dst': dst, 'path_indices': path_indices}
    _L3_gnn_all = _L3_gnn_setup()
    _L3_gnn_in = {k: v for k, v in _L3_gnn_all.items() if k in ('path_coeffs', 'path_indices')}
    del _L3_gnn_all
    return {'x': x, 'src': src, 'dst': dst, 'edge_attr_512': edge_attr_512, 'node_vec1': node_vec1, 'L0_gnn_gcn_W': _L0_gnn_in['gcn_W'], 'L0_gnn_gcn_b': _L0_gnn_in['gcn_b'], 'L0_gnn_norm_g': _L0_gnn_in['norm_g'], 'L0_gnn_norm_b': _L0_gnn_in['norm_b'], 'L0_gnn_vn_emb': _L0_gnn_in['vn_emb'], 'L0_gnn_vn_W1': _L0_gnn_in['vn_W1'], 'L0_gnn_vn_b1': _L0_gnn_in['vn_b1'], 'L0_gnn_vn_g': _L0_gnn_in['vn_g'], 'L0_gnn_vn_beta': _L0_gnn_in['vn_beta'], 'L0_gnn_vn_W2': _L0_gnn_in['vn_W2'], 'L0_gnn_vn_b2': _L0_gnn_in['vn_b2'], 'L1_gnn_f_w1': _L1_gnn_in['f_w1'], 'L1_gnn_f_b1': _L1_gnn_in['f_b1'], 'L1_gnn_f_w2': _L1_gnn_in['f_w2'], 'L1_gnn_f_b2': _L1_gnn_in['f_b2'], 'L1_gnn_s1_w': _L1_gnn_in['s1_w'], 'L1_gnn_s1_b': _L1_gnn_in['s1_b'], 'L1_gnn_b1_w': _L1_gnn_in['b1_w'], 'L1_gnn_b1_b': _L1_gnn_in['b1_b'], 'L1_gnn_wq': _L1_gnn_in['wq'], 'L1_gnn_bq': _L1_gnn_in['bq'], 'L1_gnn_wk': _L1_gnn_in['wk'], 'L1_gnn_bk': _L1_gnn_in['bk'], 'L1_gnn_wv': _L1_gnn_in['wv'], 'L1_gnn_bv': _L1_gnn_in['bv'], 'L1_gnn_wo': _L1_gnn_in['wo'], 'L1_gnn_bo': _L1_gnn_in['bo'], 'L1_gnn_s2_w': _L1_gnn_in['s2_w'], 'L1_gnn_s2_b': _L1_gnn_in['s2_b'], 'L1_gnn_b2_w': _L1_gnn_in['b2_w'], 'L1_gnn_b2_b': _L1_gnn_in['b2_b'], 'L1_gnn_m_w1': _L1_gnn_in['m_w1'], 'L1_gnn_m_b1': _L1_gnn_in['m_b1'], 'L1_gnn_m_w2': _L1_gnn_in['m_w2'], 'L1_gnn_m_b2': _L1_gnn_in['m_b2'], 'L2_gnn_wc': _L2_gnn_in['wc'], 'L2_gnn_wn': _L2_gnn_in['wn'], 'L2_gnn_bias': _L2_gnn_in['bias'], 'L3_gnn_path_coeffs': _L3_gnn_in['path_coeffs'], 'L3_gnn_path_indices': _L3_gnn_in['path_indices']}

def reference(x, src, dst, edge_attr_512, node_vec1, L0_gnn_gcn_W, L0_gnn_gcn_b, L0_gnn_norm_g, L0_gnn_norm_b, L0_gnn_vn_emb, L0_gnn_vn_W1, L0_gnn_vn_b1, L0_gnn_vn_g, L0_gnn_vn_beta, L0_gnn_vn_W2, L0_gnn_vn_b2, L1_gnn_f_w1, L1_gnn_f_b1, L1_gnn_f_w2, L1_gnn_f_b2, L1_gnn_s1_w, L1_gnn_s1_b, L1_gnn_b1_w, L1_gnn_b1_b, L1_gnn_wq, L1_gnn_bq, L1_gnn_wk, L1_gnn_bk, L1_gnn_wv, L1_gnn_bv, L1_gnn_wo, L1_gnn_bo, L1_gnn_s2_w, L1_gnn_s2_b, L1_gnn_b2_w, L1_gnn_b2_b, L1_gnn_m_w1, L1_gnn_m_b1, L1_gnn_m_w2, L1_gnn_m_b2, L2_gnn_wc, L2_gnn_wn, L2_gnn_bias, L3_gnn_path_coeffs, L3_gnn_path_indices):
    import jax
    import jax.numpy as jnp

    def _L0_gnn_ref(x, edge_index, batch, gcn_W, gcn_b, norm_g, norm_b, vn_emb, vn_W1, vn_b1, vn_g, vn_beta, vn_W2, vn_b2):
        import jax, jax.numpy as jnp
        import numpy as np
        N, E, H, L, G = (256, 2500, 512, 7, 128)
        LN_EPS = 1e-05
        EPS = 1e-07

        def _ln(x, g, b):
            m = jnp.mean(x, axis=-1, keepdims=True)
            v = jnp.var(x, axis=-1, keepdims=True)
            return (x - m) * jax.lax.rsqrt(v + LN_EPS) * g + b

        def _genconv(h, src, dst, W, b):
            msg = jax.nn.relu(h[src]) + EPS
            mmax = jax.ops.segment_max(msg, dst, num_segments=N)
            ex = jnp.exp(msg - mmax[dst])
            denom = jax.ops.segment_sum(ex, dst, num_segments=N)
            agg = jax.ops.segment_sum(msg * ex, dst, num_segments=N) / jnp.where(denom > 0, denom, 1.0)
            return (h + agg) @ W + b
        src, dst = (edge_index[0], edge_index[1])
        vn = jnp.broadcast_to(vn_emb, (G, H))
        h = x + vn[batch]
        h = _genconv(h, src, dst, gcn_W[0], gcn_b[0])
        for l in range(1, L):
            h2 = jax.nn.relu(_ln(h, norm_g[l - 1], norm_b[l - 1]))
            vn_tmp = jax.ops.segment_sum(h2, batch, num_segments=G) + vn
            vn_hid = jax.nn.relu(_ln(vn_tmp @ vn_W1[l - 1] + vn_b1[l - 1], vn_g[l - 1], vn_beta[l - 1]))
            vn = vn_hid @ vn_W2[l - 1] + vn_b2[l - 1]
            h2 = h2 + vn[batch]
            h = _genconv(h2, src, dst, gcn_W[l], gcn_b[l]) + h
        h = _ln(h, norm_g[L - 1], norm_b[L - 1])
        return h

    def _L1_gnn_ref(latent_mesh_nodes, edge_index, noise_levels, f_w1, f_b1, f_w2, f_b2, s1_w, s1_b, b1_w, b1_b, wq, bq, wk, bk, wv, bv, wo, bo, s2_w, s2_b, b2_w, b2_b, m_w1, m_b1, m_w2, m_b2):
        import jax, jax.numpy as jnp
        import numpy as np
        N_NODES = 40962
        LATENT_DIM = 512
        N_EDGES = 655392
        NUM_BLOCKS = 4
        NUM_HEADS = 4
        NUM_FREQ = 32
        BASE_PERIOD = 16
        NOISE_EMB_DIM = 16
        EPS = 1e-05

        def _cond_layer_norm(x, cond, sw, sb, bw, bb):
            mu = jnp.mean(x, axis=-1, keepdims=True)
            var = jnp.var(x, axis=-1, keepdims=True)
            xn = (x - mu) * jax.lax.rsqrt(var + EPS)
            scale = cond @ sw + sb
            bias = cond @ bw + bb
            return xn * (1.0 + scale) + bias

        def _sparse_attention(x, src, dst, wq, bq, wk, bk, wv, bv, wo, bo):
            N, D = x.shape
            H, Dh = (NUM_HEADS, D // NUM_HEADS)
            q = (x @ wq + bq).reshape(N, H, Dh) * Dh ** (-0.5)
            k = (x @ wk + bk).reshape(N, H, Dh)
            v = (x @ wv + bv).reshape(N, H, Dh)
            scores = jnp.einsum('ehd,ehd->eh', q[src], k[dst])
            smax = jax.ops.segment_max(scores, src, num_segments=N)
            ex = jnp.exp(scores - smax[src])
            denom = jax.ops.segment_sum(ex, src, num_segments=N)
            attn = ex / denom[src]
            out = jax.ops.segment_sum(attn[:, :, None] * v[dst], src, num_segments=N)
            return out.reshape(N, D) @ wo + bo

        def _forward(x, edge_index, noise_levels, f_w1, f_b1, f_w2, f_b2, s1_w, s1_b, b1_w, b1_b, wq, bq, wk, bk, wv, bv, wo, bo, s2_w, s2_b, b2_w, b2_b, m_w1, m_b1, m_w2, m_b2):
            src, dst = (edge_index[0], edge_index[1])
            freqs = jnp.arange(1, NUM_FREQ + 1, dtype=x.dtype) * (2.0 * np.pi / BASE_PERIOD)
            ph = noise_levels * freqs
            emb = jnp.concatenate([jnp.sin(ph), jnp.cos(ph)], axis=-1)
            cond = jax.nn.silu(emb @ f_w1 + f_b1) @ f_w2 + f_b2
            for i in range(NUM_BLOCKS):
                y = _cond_layer_norm(x, cond, s1_w[i], s1_b[i], b1_w[i], b1_b[i])
                y = _sparse_attention(y, src, dst, wq[i], bq[i], wk[i], bk[i], wv[i], bv[i], wo[i], bo[i])
                x = x + y
                y = _cond_layer_norm(x, cond, s2_w[i], s2_b[i], b2_w[i], b2_b[i])
                y = jax.nn.relu(y @ m_w1[i] + m_b1[i]) @ m_w2[i] + m_b2[i]
                x = x + y
            return x
        return _forward(latent_mesh_nodes, edge_index, noise_levels, f_w1, f_b1, f_w2, f_b2, s1_w, s1_b, b1_w, b1_b, wq, bq, wk, bk, wv, bv, wo, bo, s2_w, s2_b, b2_w, b2_b, m_w1, m_b1, m_w2, m_b2)

    def _L2_gnn_ref(x, wc, wn, bias, edge_index):
        import jax, jax.numpy as jnp
        import numpy as np
        N = 50000
        IN_CH = 512
        OUT_CH = 512
        DEG = 32
        E = N * DEG
        alpha = x @ wc
        beta = x @ wn
        src, dst = (edge_index[0], edge_index[1])
        sums = jax.ops.segment_sum(beta[dst], src, num_segments=x.shape[0])
        counts = jax.ops.segment_sum(jnp.ones_like(src, dtype=beta.dtype), src, num_segments=x.shape[0])
        gamma = sums / counts[:, None]
        return alpha + gamma + bias

    def _L3_gnn_ref(x_nodes, x_edges, path_coeffs, src, dst, path_indices):
        import jax, jax.numpy as jnp
        import numpy as np
        N_NODES = 20000
        N_EDGES = 3125
        N_SEG = 16
        EXTENT = 32
        N_PATHS = 64
        OP_SIZE = N_SEG * EXTENT
        n_nodes = x_nodes.shape[0]
        x1 = x_nodes[src].reshape(-1, N_SEG, EXTENT)
        x2 = x_edges.reshape(-1, N_SEG, EXTENT)
        i1, i2, i3 = (path_indices[:, 0], path_indices[:, 1], path_indices[:, 2])
        contrib = path_coeffs[None, :, None] * x1[:, i1, :] * x2[:, i2, :]
        edge_out = jnp.zeros((x2.shape[0], N_SEG, EXTENT), x_nodes.dtype).at[:, i3, :].add(contrib)
        out = jnp.zeros((n_nodes, OP_SIZE), x_nodes.dtype).at[dst].add(edge_out.reshape(-1, OP_SIZE))
        return out
    edge_index = jnp.stack([src, dst])
    batch0 = jnp.zeros((256,), jnp.int32)
    h = jnp.maximum(_layernorm(x, axis=-1), 0.0)
    x = x + _L0_gnn_ref(h, edge_index, batch0, L0_gnn_gcn_W, L0_gnn_gcn_b, L0_gnn_norm_g, L0_gnn_norm_b, L0_gnn_vn_emb, L0_gnn_vn_W1, L0_gnn_vn_b1, L0_gnn_vn_g, L0_gnn_vn_beta, L0_gnn_vn_W2, L0_gnn_vn_b2)
    h = jnp.maximum(_layernorm(x, axis=-1), 0.0)
    x = x + _L1_gnn_ref(h, edge_index, node_vec1, L1_gnn_f_w1, L1_gnn_f_b1, L1_gnn_f_w2, L1_gnn_f_b2, L1_gnn_s1_w, L1_gnn_s1_b, L1_gnn_b1_w, L1_gnn_b1_b, L1_gnn_wq, L1_gnn_bq, L1_gnn_wk, L1_gnn_bk, L1_gnn_wv, L1_gnn_bv, L1_gnn_wo, L1_gnn_bo, L1_gnn_s2_w, L1_gnn_s2_b, L1_gnn_b2_w, L1_gnn_b2_b, L1_gnn_m_w1, L1_gnn_m_b1, L1_gnn_m_w2, L1_gnn_m_b2)
    h = jnp.maximum(_layernorm(x, axis=-1), 0.0)
    x = x + _L2_gnn_ref(h, L2_gnn_wc, L2_gnn_wn, L2_gnn_bias, edge_index)
    h = jnp.maximum(_layernorm(x, axis=-1), 0.0)
    x = x + _L3_gnn_ref(h, edge_attr_512, L3_gnn_path_coeffs, src, dst, L3_gnn_path_indices)
    return x

_drawn_inputs = setup_inputs


def setup_inputs(seed=0):
    import zlib

    import numpy as np

    out = dict(_drawn_inputs(seed))
    spreads = {'L0_gnn_gcn_b': (0.0, 0.1),
     'L0_gnn_norm_g': (1.0, 0.2),
     'L0_gnn_norm_b': (0.0, 0.1),
     'L0_gnn_vn_emb': (0.0, 0.1),
     'L0_gnn_vn_b1': (0.0, 0.8),
     'L0_gnn_vn_g': (1.0, 0.2),
     'L0_gnn_vn_beta': (0.0, 0.1),
     'L0_gnn_vn_b2': (0.0, 0.1),
     'L1_gnn_f_b1': (0.0, 0.8),
     'L1_gnn_f_b2': (0.0, 0.8),
     'L1_gnn_s1_b': (0.0, 0.532),
     'L1_gnn_b1_b': (0.0, 0.421),
     'L1_gnn_bq': (0.0, 0.8),
     'L1_gnn_bk': (0.0, 0.8),
     'L1_gnn_bv': (0.0, 0.1),
     'L1_gnn_bo': (0.0, 0.1),
     'L1_gnn_s2_b': (0.0, 0.583),
     'L1_gnn_b2_b': (0.0, 0.584),
     'L1_gnn_m_b1': (0.0, 0.277),
     'L1_gnn_m_b2': (0.0, 0.1)}
    factors = {'node_vec1': 8.0,
     'L1_gnn_f_w1': 8.0,
     'L1_gnn_f_w2': 8.0,
     'L1_gnn_s1_w': 8.0,
     'L1_gnn_b1_w': 8.0,
     'L1_gnn_wq': 8.0,
     'L1_gnn_wk': 8.0,
     'L1_gnn_s2_w': 8.0,
     'L1_gnn_b2_w': 8.0,
     'L2_gnn_bias': 5.459}
    for name, (base, spread) in spreads.items():
        noise = np.random.default_rng([zlib.crc32(name.encode()), seed]).standard_normal(out[name].shape)
        drawn = base * np.exp(spread * noise) if base else spread * noise
        out[name] = jnp.asarray(drawn.astype(out[name].dtype))
    for name, factor in factors.items():
        out[name] = (out[name] * factor).astype(out[name].dtype)
    return out
```

```python
from contextlib import ExitStack

import concourse.bass as bass
import concourse.mybir as mybir
import numpy as np

F32 = mybir.dt.float32
BF16 = mybir.dt.bfloat16
I32 = mybir.dt.int32
ALU = mybir.AluOpType
ACT = mybir.ActivationFunctionType
AX = mybir.AxisListType

P = 128
N = 256
NT = N // P
D = 512
CT = D // P
E = 8192
ET = E // P
LAYERS = 7
BLOCKS = 4
HEADS = 4
DH = D // HEADS
NF = 32
NC = 16
SEGS, EXT, PATHS = 16, 32, 64
GROUPS = 5
TG = -(-ET // GROUPS)
SIZES = [min(TG, ET - g * TG) for g in range(GROUPS)]
RING = 4
EDGE_AT = [0, 3, 0, 3, 0]
SOURCE_AT = [1, 4, 2, 1, 4]
SUM_AT = [2, 1, 4, 2, 1]
SRC_CUT = 4
HOT = 4

LN_EPS = 1e-5
MSG_EPS = 1e-7
AHEAD = 2
CONSTS = 16
MASKED = -1e30
TINY = 1e-30
DEN_SCALE = float(2.0 ** 40)
DEN_SHIFT = float(40 * np.log(2.0))
DEN_TINY = float(2.0 ** -60)
TWO_PI = 2 * np.pi
PI_A = 6.28125
PI_B = float(np.floor((TWO_PI - PI_A) * 2 ** 24) / 2 ** 24)
PI_C = float(TWO_PI - PI_A - PI_B)
ROUND = 12582912.0
PI_CLIP = 3.1415925

COL_A = [("norm_g", LAYERS), ("norm_b", LAYERS), ("vn_emb", 1), ("vn_g", LAYERS - 1), ("vn_beta", LAYERS - 1)]
COL_B = [("vn_b2", LAYERS - 1), ("bq", BLOCKS), ("bk", BLOCKS), ("m_b1", BLOCKS)]


def column_table():
    at, col = {}, 0
    for name, n in COL_A + COL_B:
        at[name] = col
        col += CT * n
    return at, CT * sum(n for _, n in COL_A), CT * sum(n for _, n in COL_B)


LN_L0_LAST, LN_L1_IN, LN_BLOCK, LN_L2, LN_L3 = 7, 8, 9, 17, 18
TR_BLOCK, TR_L2 = 7, 15


class Steps:

    def __init__(self, eng, sem):
        self.eng, self.sem, self.base, self.n = eng, sem, 0, 0

    def link(self, ins):
        self.n += 1
        ins.then_inc(self.sem, 1)
        self.eng.wait_ge(self.sem, self.base + self.n)

    def enter(self, it, per):
        self.outer, self.start, self.per = self.base, self.base + self.n, per
        self.base, self.n = it * per + self.start, 0

    def leave(self, times):
        assert self.n == self.per, self.n
        self.base, self.n = self.start, self.per * times


def gnn_stack_kernel(nc, A, out):
    COL, NCOL_A, NCOL_B = column_table()
    ctx = ExitStack()
    with ctx:
        def sb(name, shape, dt=F32):
            return ctx.enter_context(nc.sbuf_tensor(name, shape, dt))

        def sem(name):
            return ctx.enter_context(nc.semaphore(name))

        PS = ctx.enter_context(nc.psum_tensor("PS", [P, 8, 512], F32))

        def chunks(bank):
            return PS[:, bank:bank + 2, :].rearrange("p b (c n) -> p (b c) n", n=N)

        GW = TG * D
        big = sb("big", [P, 5 * GW])
        part = [big[:, i * GW:(i + 1) * GW].rearrange("p (j d) -> p j d", j=TG) for i in range(5)]
        assert 6 * CT * D <= 2 * GW and 10 * 1024 <= 2 * GW
        W = big[:, GW:GW + 6 * CT * D]
        wbuf = [W[:, i * CT * D:(i + 1) * CT * D].rearrange("p (c n) -> p c n", c=CT) for i in range(6)]
        R = big[:, 3 * GW:3 * GW + 10 * 1024]

        spare = big[:, 3 * GW + 10 * 1024:5 * GW]

        def region(k, n=1):
            return R[:, 1024 * k:1024 * (k + n)]

        def as_c(ap):
            return ap.rearrange("p (c n) -> p c n", c=CT)

        def as_t(ap):
            return ap.rearrange("p (t n) -> p t n", t=NT)

        x = sb("x", [P, NT, D])
        h = sb("h", [P, NT, D])
        xn = sb("xn", [P, NT, D])
        hT = sb("hT", [P, CT, N])
        hv = as_c(region(0))
        m = as_c(region(1))
        md = as_c(region(2))
        ex = as_t(region(3))
        mex = as_t(region(4))
        rec = as_c(region(5))
        z = as_c(region(6))
        gb = region(8, 2).rearrange("p (k n) -> p k n", k=4)
        qT = as_c(region(0))
        kT = as_c(region(1))
        v = as_t(region(2))
        prob = region(3, 2).rearrange("p (t h n) -> p t h n", t=NT, h=HEADS)
        probT = region(5, 2).rearrange("p (t h n) -> p t h n", t=NT, h=HEADS)
        oT = as_c(region(7))
        mT = as_c(region(0))
        tab = region(8, 2).rearrange("p (k t n) -> p k t n", k=2, t=NT)
        CUT = E // SRC_CUT
        src_all = big[:, 0:3 * CUT].bitcast(I32)
        assert 3 * CUT <= GW
        srcT = sb("srcT", [P, NT, E], BF16)
        tail = sb("tail", [P, 8 * D])
        brow = tail[0:1, 0:4 * D]
        tabw = tail[0:NC + 1, 4 * D:8 * D].rearrange("q (i k d) -> q i k d", i=2, k=2)
        prod = tail[:, 0:RING * TG * EXT].rearrange("p (r j u) -> p r j u", r=RING, u=EXT)
        hs = tail[:, 4 * D:7 * D].bitcast(BF16).rearrange("p (k t d) -> p k t d", k=3, t=NT)
        assert RING * TG * EXT <= 4 * D
        hotd = xn[:, :, :].rearrange("p t (i n) -> p (t i) n", n=N)
        src_i = sb("src_i", [P, ET], I32)
        dst_i = sb("dst_i", [P, ET], I32)
        src_f = sb("src_f", [P, ET])
        dst_f = sb("dst_f", [P, ET])
        dst_n = sb("dst_n", [P, ET])
        iota_f = sb("iota_f", [P, N])
        iota_b = sb("iota_b", [P, N], BF16)
        iota_p = sb("iota_p", [P, NT])
        hot_s, hot_d = hT[:, 0:2, :].bitcast(BF16), hT[:, 2:4, :].bitcast(BF16)
        hot_s = hot_s.rearrange("p c n -> p (c n)").rearrange("p (k n) -> p k n", k=HOT)
        hot_d = hot_d.rearrange("p c n -> p (c n)").rearrange("p (k n) -> p k n", k=HOT)
        cnt = sb("cnt", [P, NT, N])
        cntT = sb("cntT", [P, NT, N])
        mask = sb("mask", [P, NT, N])
        outdeg = sb("outdeg", [P, NT])
        outrec = sb("outrec", [P, NT])
        ident = sb("ident", [P, P])
        ones = sb("ones", [P, P])
        par_a = xn[0:NCOL_A, 0, 0:P]
        par_b = xn[0:NCOL_B, 1, 0:P]
        cols = sb("cols", [P, NCOL_A + NCOL_B])
        consts = sb("consts", [P, 4])
        zero, ln_tiny, den_shift, one = (consts[:, i:i + 1] for i in range(4))
        idle = sb("idle", [1, 40])
        st = sb("st", [P, NT, 6])
        mv = sb("mv", [P, NT, 2])
        var = sb("var", [P, NT])
        lnv = sb("lnv", [P, NT])
        est = sb("est", [P, NT])
        nwt = sb("nwt", [P, NT])
        rstd = sb("rstd", [P, NT])
        hsum = sb("hsum", [P, CT])
        vn = sb("vn", [P, CT])
        vtmp = sb("vtmp", [P, CT])
        vhid = sb("vhid", [P, CT])
        vrow = spare[0:1, N:N + D]
        vst = sb("vst", [1, 6])
        vmv = sb("vmv", [1, 2])
        vvar = sb("vvar", [1, 4])
        mmax = sb("mmax", [P, CT])
        smax = sb("smax", [P, NT * HEADS])
        nmax = sb("nmax", [P, NT * HEADS])
        den = sb("den", [P, NT * HEADS])
        rden = sb("rden", [P, NT * HEADS])
        emb = region(7)[0:2 * NF, 0:N]
        turns = region(7)[0:2 * NF, N:2 * N]
        freq = sb("freq", [2 * NF, 4])
        freq_i = sb("freq_i", [2 * NF, 1], I32)
        fw1 = sb("fw1", [2 * NF, NC])
        fw2 = sb("fw2", [NC, NC])
        fb = sb("fb", [NC, 2])
        cz = region(7)[0:NC, 2 * N:3 * N]
        ce = region(7)[0:NC, 3 * N:4 * N]
        condT = spare[0:NC + 1, 0:N]
        path = sb("path", [1, (PATHS + AHEAD) * 4], I32)
        path_raw = sb("path_raw", [1, PATHS * 3], I32)
        coef = sb("coef", [P, PATHS])

        src_in = [sem(f"src_in{c}") for c in range(SRC_CUT)]
        x_in, edges_in, par_in, gb_in = map(sem, ["x_in", "edges_in", "par_in", "gb_in"])
        noise_in, path_in, path_clear = map(sem, ["noise_in", "path_in", "path_clear"])
        w_in = [sem(f"w_in{i}") for i in range(6)]
        tabw_in = [sem(f"tabw_in{i}") for i in range(2)]
        x2_in = [sem(f"x2_in{g}") for g in range(GROUPS)]
        out_done = sem("out_done")
        zeroed, consts_set, edges_f, hot_ready, hot_used, cnt_done, cnt_set, cntT_done, cntT_set = map(
            sem, ["zeroed", "consts_set", "edges_f", "hot_ready", "hot_used", "cnt_done", "cnt_set", "cntT_done",
                  "cntT_set"])
        par_turned, cols_set, srcT_set = map(sem, ["par_turned", "cols_set", "srcT_set"])
        angle_set, emb_set, cond_a, cond_z, cond_e, cond_s, cond_b, cond_set = map(
            sem, ["angle_set", "emb_set", "cond_a", "cond_z", "cond_e", "cond_s", "cond_b", "cond_set"])
        ln_var, ln_est, ln_out, tr_done = map(sem, ["ln_var", "ln_est", "ln_out", "tr_done"])
        dve_step, act_step = sem("dve_step"), sem("act_step")
        hT_ready, vn_in, vn_hid, vn_var, vn_est, vn_row, vn_col, vn_act, vn_out = map(
            sem, ["hT_ready", "vn_in", "vn_hid", "vn_var", "vn_est", "vn_row", "vn_col", "vn_act", "vn_out"])
        m_ready, md_ready, mT_done, mdT_done, ex_ready, mex_ready, den_done, num_done, rec_est, z_ready, conv_done = map(
            sem, ["m_ready", "md_ready", "mT_done", "mdT_done", "ex_ready", "mex_ready", "den_done", "num_done",
                  "rec_est", "z_ready", "conv_done"])
        tab_done, tab_ready, y_ready, yT_ready, q_done, k_done, v_done, q_ready, k_ready, v_ready = map(
            sem, ["tab_done", "tab_ready", "y_ready", "yT_ready", "q_done", "k_done", "v_done", "q_ready", "k_ready",
                  "v_ready"])
        sc_done, smax_ready, exp_ready, p_ready, pT_done, pT_act, pT_dve, o_done, o_ready, proj_done = map(
            sem, ["sc_done", "smax_ready", "exp_ready", "p_ready", "pT_done", "pT_act", "pT_dve", "o_done", "o_ready",
                  "proj_done"])
        up_done, up_ready, down_done = map(sem, ["up_done", "up_ready", "down_done"])
        beta_done, beta_ready, alpha_done, gamma_done = map(sem, ["beta_done", "beta_ready", "alpha_done", "gamma_done"])
        hs_ready, hot_squared, hotd_ready, acc_zero, x1_done, x1_ready, path_step, tile_summed, final = map(
            sem, ["hs_ready", "hot_squared", "hotd_ready", "acc_zero", "x1_done", "x1_ready", "path_step",
                  "tile_summed", "final"])

        block = ctx.enter_context(nc.Block())

        def bias_of(i):
            k = min(i, 3)
            return brow[0:1, k * D:(k + 1) * D]

        def rows(ap):
            return ap.rearrange("(c p) n -> p c n", p=P)

        def one_row(ap):
            return ap.rearrange("(a n) -> a n", a=1)

        def nodes(ap):
            return ap.rearrange("(t p) d -> p t d", p=P)

        @block.sync
        def _(sp):
            def load_w(i, weight, bias):
                sp.dma_start(wbuf[i], rows(weight)).then_inc(w_in[i], 16)
                if bias is not None:
                    sp.dma_start(bias_of(i), one_row(bias)).then_inc(w_in[i], 16)

            def load_tab(i, k, b):
                ws, bs, wb, bb = [("s1_w", "s1_b", "b1_w", "b1_b"), ("s2_w", "s2_b", "b2_w", "b2_b")][i]
                sp.dma_start(tabw[0:NC, i, 0, :], A["L1_gnn_" + ws][b, :, :]).then_inc(tabw_in[i], 16)
                sp.dma_start(tabw[0:NC, i, 1, :], A["L1_gnn_" + wb][b, :, :]).then_inc(tabw_in[i], 16)
                sp.dma_start(tabw[NC:NC + 1, i, 0, :], A["L1_gnn_" + bs][bass.ds(b, 1), :]).then_inc(tabw_in[i], 16)
                sp.dma_start(tabw[NC:NC + 1, i, 1, :], A["L1_gnn_" + bb][bass.ds(b, 1), :]).then_inc(tabw_in[i], 16)

            sp.dma_start(x[:], nodes(A["x"])).then_inc(x_in, 16)
            sp.dma_start(src_i[:], A["src"].rearrange("(p t) -> p t", t=ET)).then_inc(edges_in, 16)
            sp.dma_start(dst_i[:], A["dst"].rearrange("(p t) -> p t", t=ET)).then_inc(edges_in, 16)
            r = 0
            for tile, names in ((par_a, COL_A), (par_b, COL_B)):
                r = 0
                for name, n in names:
                    full = ("L1_gnn_" if name in ("bq", "bk", "m_b1") else "L0_gnn_") + name
                    a = A[full]
                    a = a.rearrange("(c p) -> c p", p=P) if n == 1 else a.rearrange("l (c p) -> (l c) p", p=P)
                    sp.dma_start(tile[r:r + CT * n, :], a).then_inc(par_in, 16)
                    r += CT * n
            load_w(0, A["L0_gnn_gcn_W"][0], A["L0_gnn_gcn_b"][0])
            load_w(1, A["L0_gnn_vn_W1"][0], A["L0_gnn_vn_b1"][0])
            load_w(2, A["L0_gnn_vn_W2"][0], None)
            sp.dma_start(emb, A["node_vec1"].rearrange("n a -> a n").to_broadcast([2 * NF, N])).then_inc(noise_in, 16)
            sp.dma_start(fw1[:], A["L1_gnn_f_w1"]).then_inc(noise_in, 16)
            sp.dma_start(fw2[:], A["L1_gnn_f_w2"]).then_inc(noise_in, 16)
            sp.dma_start(fb[:, 0:1], A["L1_gnn_f_b1"].rearrange("(n a) -> n a", a=1)).then_inc(noise_in, 16)
            sp.dma_start(fb[:, 1:2], A["L1_gnn_f_b2"].rearrange("(n a) -> n a", a=1)).then_inc(noise_in, 16)
            for c in range(SRC_CUT):
                if c >= 3:
                    sp.wait_ge(srcT_set, (c - 2) * NT)
                sp.dma_start(src_all[:, (c % 3) * CUT:(c % 3 + 1) * CUT],
                             one_row(A["src"])[:, c * CUT:(c + 1) * CUT].to_broadcast([P, CUT])).then_inc(src_in[c], 16)
            for k, name in enumerate(("norm_g", "norm_b")):
                sp.dma_start(gb[:, k, :], A["L0_gnn_" + name][LAYERS - 1:LAYERS, :].to_broadcast([P, D])).then_inc(gb_in, 16)
            load_w(3, A["L1_gnn_wq"][0], None)
            load_w(4, A["L1_gnn_wk"][0], None)
            load_w(5, A["L1_gnn_wv"][0], A["L1_gnn_bv"][0])
            sp.dma_start(path_raw[:], A["L3_gnn_path_indices"].rearrange("(a k) c -> a (k c)", a=1)).then_inc(path_in, 16)
            sp.dma_start(coef[:], one_row(A["L3_gnn_path_coeffs"]).to_broadcast([P, PATHS])).then_inc(path_in, 16)
            load_tab(0, 0, 0)
            load_tab(1, 0, 0)

            def edge_group(g):
                rows_of = A["edge_attr_512"].rearrange("(p t) d -> p t d", t=ET)
                sp.dma_start(part[EDGE_AT[g]][:, 0:SIZES[g], :], rows_of[:, g * TG:g * TG + SIZES[g], :]).then_inc(x2_in[g], 16)

            sp.wait_ge(srcT_set, SRC_CUT * NT)
            edge_group(0)

            def conv_weights(l):
                sp.wait_ge(conv_done, l * 2)
                sp.dma_start(wbuf[0], rows(A["L0_gnn_gcn_W"][bass.ds(l, 1)].rearrange("a k n -> (a k) n"))).then_inc(w_in[0], 16)
                sp.dma_start(bias_of(0), A["L0_gnn_gcn_b"][bass.ds(l, 1), :]).then_inc(w_in[0], 16)

            with sp.Fori(1, LAYERS - 1) as l:
                conv_weights(l)
                sp.wait_ge(vn_hid, l)
                sp.dma_start(wbuf[1], rows(A["L0_gnn_vn_W1"][bass.ds(l, 1)].rearrange("a k n -> (a k) n"))).then_inc(w_in[1], 16)
                sp.dma_start(bias_of(1), A["L0_gnn_vn_b1"][bass.ds(l, 1), :]).then_inc(w_in[1], 16)
                sp.wait_ge(vn_out, l)
                sp.dma_start(wbuf[2], rows(A["L0_gnn_vn_W2"][bass.ds(l, 1)].rearrange("a k n -> (a k) n"))).then_inc(w_in[2], 16)
            conv_weights(LAYERS - 1)
            sp.wait_ge(vn_hid, LAYERS - 1)
            load_w(1, A["L1_gnn_m_w1"][0], None)
            sp.wait_ge(vn_out, LAYERS - 1)
            load_w(2, A["L1_gnn_m_w2"][0], A["L1_gnn_m_b2"][0])
            sp.wait_ge(conv_done, 2 * LAYERS)
            load_w(0, A["L1_gnn_wo"][0], A["L1_gnn_bo"][0])

            def w_at(name, b):
                return rows(A["L1_gnn_" + name][bass.ds(b, 1)].rearrange("a k n -> (a k) n"))

            with sp.Fori(0, BLOCKS - 1) as b:
                sp.wait_ge(tab_done, b * 8 + 4)
                load_tab(0, 0, b + 1)
                sp.wait_ge(q_done, b * 2 + 2)
                sp.dma_start(wbuf[3], w_at("wq", b + 1)).then_inc(w_in[3], 16)
                sp.wait_ge(k_done, b * 2 + 2)
                sp.dma_start(wbuf[4], w_at("wk", b + 1)).then_inc(w_in[4], 16)
                sp.wait_ge(v_done, b * 2 + 2)
                sp.dma_start(wbuf[5], w_at("wv", b + 1)).then_inc(w_in[5], 16)
                sp.dma_start(bias_of(5), A["L1_gnn_bv"][bass.ds(b + 1, 1), :]).then_inc(w_in[5], 16)
                sp.wait_ge(tab_done, b * 8 + 8)
                load_tab(1, 0, b + 1)
                sp.wait_ge(proj_done, b * 2 + 2)
                sp.dma_start(wbuf[0], w_at("wo", b + 1)).then_inc(w_in[0], 16)
                sp.dma_start(bias_of(0), A["L1_gnn_bo"][bass.ds(b + 1, 1), :]).then_inc(w_in[0], 16)
                sp.wait_ge(up_done, b * 2 + 2)
                sp.dma_start(wbuf[1], w_at("m_w1", b + 1)).then_inc(w_in[1], 16)
                sp.wait_ge(down_done, b * 2 + 2)
                sp.dma_start(wbuf[2], w_at("m_w2", b + 1)).then_inc(w_in[2], 16)
                sp.dma_start(bias_of(2), A["L1_gnn_m_b2"][bass.ds(b + 1, 1), :]).then_inc(w_in[2], 16)
            sp.wait_ge(q_done, 2 * BLOCKS)
            load_w(3, A["L2_gnn_wn"], None)
            sp.wait_ge(v_done, 2 * BLOCKS)
            load_w(5, A["L2_gnn_wc"], A["L2_gnn_bias"])

            sp.wait_ge(hs_ready, 1)
            edge_group(1)
            for g in range(2, GROUPS):
                sp.wait_ge(path_step, (g - 1) * 2 * PATHS)
                edge_group(g)
            sp.wait_ge(final, 1)
            sp.dma_start(nodes(out)[:, 0, :], x[:, 0, :]).then_inc(out_done, 16)
            sp.wait_ge(final, 2)
            sp.dma_start(nodes(out)[:, 1, :], x[:, 1, :]).then_inc(out_done, 16)
            sp.wait_ge(out_done, 32)

        @block.gpsimd
        def _(pool):
            pool.memset(ident[:], 0.0).then_inc(zeroed, 1)
            pool.memset(ones[:], 1.0).then_inc(consts_set, 1)
            pool.memset(consts[:, 0:1], 0.0).then_inc(consts_set, 1)
            pool.memset(consts[:, 1:2], DEN_TINY).then_inc(consts_set, 1)
            pool.memset(consts[:, 2:3], DEN_SHIFT).then_inc(consts_set, 1)
            pool.memset(one, 1.0).then_inc(consts_set, 1)
            pool.memset(condT[:], 1.0).then_inc(consts_set, 1)
            pool.iota(iota_f[:], pattern=[[1, N]], base=0, channel_multiplier=0,
                      allow_small_or_imprecise_dtypes=True).then_inc(consts_set, 1)
            pool.iota(iota_b[:], pattern=[[1, N]], base=0, channel_multiplier=0,
                      allow_small_or_imprecise_dtypes=True).then_inc(consts_set, 1)
            pool.iota(iota_p[:], pattern=[[P, NT]], base=0, channel_multiplier=1,
                      allow_small_or_imprecise_dtypes=True).then_inc(consts_set, 1)
            for k in range(2):
                half = slice(NF * k, NF * (k + 1))
                pool.wait_ge(consts_set, 9 + 3 * k)
                pool.iota(freq_i[half, :], pattern=[[0, 1]], base=1, channel_multiplier=1).then_inc(consts_set, 1)
                pool.memset(freq[half, 1:2], 0.25 * k).then_inc(consts_set, 1)
                pool.memset(freq[half, 2:3], float(np.pi / 2) * k).then_inc(consts_set, 1)
            pool.wait_ge(zeroed, 1)
            pool.wait_ge(consts_set, CONSTS - 1)
            pool.affine_select(out=ident[:], in_=ident[:], compare_op=ALU.not_equal, fill=1.0, base=0,
                               pattern=[[-1, P]], channel_multiplier=1).then_inc(consts_set, 1)
            pool.wait_ge(consts_set, CONSTS)
            for c in range(SRC_CUT):
                pool.wait_ge(src_in[c], 16)
                q = P // SRC_CUT
                by_tile = src_all[:, (c % 3) * CUT:(c % 3 + 1) * CUT].rearrange("s (p t) -> s t p", t=ET)
                for s in range(NT):
                    pool.tensor_scalar(srcT[:, s, :].rearrange("s (t p) -> s t p", p=P)[:, :, c * q:(c + 1) * q],
                                       by_tile, iota_p[:, s:s + 1], None, ALU.is_equal).then_inc(srcT_set, 1)

            pool.wait_ge(alpha_done, 2)
            pool.wait_ge(beta_done, 2)
            for g in range(GROUPS):
                if g > 0:
                    pool.wait_ge(path_step, g * 2 * PATHS)
                pool.memset(part[SUM_AT[g]][:, 0:TG // 2, :], 0.0).then_inc(acc_zero, 1)

        @block.scalar
        def _(act):
            steps = Steps(act, act_step)

            def rsqrt_estimate(n):
                act.wait_ge(ln_var, n + 1)
                steps.link(act.activation(lnv[:], var[:], ACT.Ln, bias=zero))
                act.activation(est[:], lnv[:], ACT.Exp, bias=zero, scale=-0.5).then_inc(ln_est, 1)

            def turned(tr):
                for b in range(2):
                    act.wait_ge(tr_done, tr * 2 + (b + 1))
                    yield b

            act.wait_ge(consts_set, CONSTS)
            act.wait_ge(angle_set, 1)
            act.activation(emb, turns, ACT.Sin, bias=zero[0:2 * NF, :]).then_inc(emb_set, 1)
            act.wait_ge(cond_z, 1)
            act.activation(ce, cz, ACT.Exp, bias=zero[0:NC, :], scale=-1.0).then_inc(cond_e, 1)

            act.preload_act_table_set("natural_log_exp_and_others")

            def layer0(l, first):
                rsqrt_estimate(l)
                for b in turned(l):
                    for c in (2 * b, 2 * b + 1):
                        if first:
                            act.activation(hT[:, c, :], chunks(0)[:, c, :], ACT.Relu, bias=zero).then_inc(hT_ready, 1)
                        else:
                            act.activation(hT[:, c, :], chunks(0)[:, c, :], ACT.Relu,
                                           bias=cols[:, bass.ds(l * CT + (COL["norm_b"] - CT + c), 1)],
                                           scale=cols[:, bass.ds(l * CT + (COL["norm_g"] - CT + c), 1)],
                                           accum_out=hsum[:, c:c + 1]).then_inc(hT_ready, 1)
                if not first:
                    act.wait_ge(vn_var, l)
                    steps.link(act.activation(vvar[0:1, 1:2], vvar[0:1, 0:1], ACT.Ln, bias=zero[0:1, :]))
                    act.activation(vvar[0:1, 2:3], vvar[0:1, 1:2], ACT.Exp, bias=zero[0:1, :], scale=-0.5).then_inc(vn_est, 1)
                for t in range(NT):
                    act.wait_ge(mdT_done, l * 2 + (t + 1))
                    act.activation(ex[:, t, :], PS[:, 6 + t, :], ACT.Exp, bias=zero).then_inc(ex_ready, 1)
                for b in range(2):
                    act.wait_ge(den_done, l * 2 + (b + 1))
                    steps.link(act.activation(rec[:, 2 * b:2 * b + 2, :], chunks(0)[:, 2 * b:2 * b + 2, :], ACT.Ln,
                                              bias=ln_tiny, scale=DEN_SCALE))
                    act.activation(rec[:, 2 * b:2 * b + 2, :], rec[:, 2 * b:2 * b + 2, :], ACT.Exp, bias=den_shift,
                                   scale=-1.0).then_inc(rec_est, 1)

            act.wait_ge(cols_set, 2)
            layer0(0, True)
            with act.Fori(1, LAYERS) as l:
                steps.enter(l - 1, 4)
                layer0(l, False)
            steps.leave(LAYERS - 1)
            rsqrt_estimate(LN_L0_LAST)
            rsqrt_estimate(LN_L1_IN)

            def table(k):
                for j in range(4):
                    act.wait_ge(tab_done, k * 4 + (j + 1))
                    act.activation(tab[:, j // 2, j % 2, :], PS[:, 4 + j, :], ACT.Copy).then_inc(tab_ready, 1)

            def y_turned(k):
                for b in turned(k + TR_BLOCK):
                    act.activation(hT[:, 2 * b:2 * b + 2, :], chunks(0)[:, 2 * b:2 * b + 2, :], ACT.Copy).then_inc(yT_ready, 1)

            with act.Fori(0, BLOCKS) as b:
                steps.enter(b, 2)
                table(b * 2)
                rsqrt_estimate(b * 2 + LN_BLOCK)
                y_turned(b * 2)
                for hd in range(HEADS):
                    act.wait_ge(q_done, b * 2 + (hd // 2 + 1))
                    act.activation(qT[:, hd, :], chunks(2)[:, hd, :], ACT.Identity,
                                   bias=cols[:, bass.ds(b * CT + (COL["bq"] + hd), 1)]).then_inc(q_ready, 1)
                for t in range(NT):
                    act.wait_ge(v_done, b * 2 + (t + 1))
                    act.activation(v[:, t, :], PS[:, 6 + t, :], ACT.Copy).then_inc(v_ready, 1)
                for t in range(NT):
                    act.wait_ge(smax_ready, b * 2 + (t + 1))
                    for hd in range(HEADS):
                        k = t * HEADS + hd
                        act.activation(prob[:, t, hd, :], prob[:, t, hd, :], ACT.Exp,
                                       bias=nmax[:, k:k + 1]).then_inc(exp_ready, 1)
                for i in range(2):
                    act.wait_ge(pT_done, b * 4 + (2 * i + 1))
                    act.activation(probT[:, 0, 2 * i:2 * i + 2, :], chunks(4)[:, 2 * i:2 * i + 2, :],
                                   ACT.Copy).then_inc(pT_act, 1)
                for i in range(2):
                    act.wait_ge(o_done, b * 2 + (i + 1))
                    act.activation(oT[:, 2 * i:2 * i + 2, :], chunks(0)[:, 2 * i:2 * i + 2, :], ACT.Copy).then_inc(o_ready, 1)
                table(b * 2 + 1)
                rsqrt_estimate(b * 2 + (LN_BLOCK + 1))
                y_turned(b * 2 + 1)
                for c in range(CT):
                    act.wait_ge(up_done, b * 2 + (c // 2 + 1))
                    act.activation(mT[:, c, :], chunks(2)[:, c, :], ACT.Relu,
                                   bias=cols[:, bass.ds(b * CT + (COL["m_b1"] + c), 1)]).then_inc(up_ready, 1)
            steps.leave(BLOCKS)

            rsqrt_estimate(LN_L2)
            for b in turned(TR_L2):
                act.activation(hT[:, 2 * b:2 * b + 2, :], chunks(0)[:, 2 * b:2 * b + 2, :], ACT.Relu, bias=zero).then_inc(yT_ready, 1)
            for t in range(NT):
                act.wait_ge(beta_done, t + 1)
                act.activation(v[:, t, :], PS[:, 2 + t, :], ACT.Copy).then_inc(beta_ready, 1)
            rsqrt_estimate(LN_L3)

            def x1_tile(g, j, u):
                act.wait_ge(x1_done, j + (g * TG + 1))
                act.activation(part[SOURCE_AT[g]][:, bass.ds(j, 1), :].rearrange("p a d -> p (a d)"),
                               PS[:, 2 + u, :], ACT.Copy).then_inc(x1_ready, 1)

            def x1_group(g):
                with act.Fori(0, SIZES[g] // RING) as q:
                    for u in range(RING):
                        x1_tile(g, q * RING + u, (g * TG + u) % RING)
                for j in range(SIZES[g] // RING * RING, SIZES[g]):
                    x1_tile(g, j, (g * TG + j) % RING)

            def hot(tile, u, count):
                act.activation(hotd[:, u, :], iota_f[:], ACT.Square, bias=dst_n[:, bass.ds(tile, 1)]).then_inc(hot_squared, 1)
                act.wait_ge(hot_squared, count)
                act.activation(hotd[:, u, :], hotd[:, u, :], ACT.Relu, bias=one, scale=-1.0).then_inc(hotd_ready, 1)

            x1_group(0)
            x1_group(1)
            act.wait_ge(hs_ready, 1)
            for u in range(RING):
                hot(u, u, u + 1)
            done = 1
            for g in range(GROUPS):
                upto = ((g + 1) * TG - 1) // RING + 1 if g < GROUPS - 1 else ET // RING
                with act.Fori(done, upto) as q:
                    for u in range(RING):
                        act.wait_ge(tile_summed, q * RING + (u + 1 - RING))
                        hot(q * RING + u, u, q * RING + (u + 1))
                done = upto
                if g + 2 < GROUPS:
                    act.wait_ge(tile_summed, (g + 1) * TG)
                    x1_group(g + 2)

        @block.tensor
        def _(pe):
            def mm(o, lhsT, rhs, start, stop):
                return pe.matmul(o, lhsT, rhs, start=start, stop=stop)

            pe.wait_ge(consts_set, CONSTS)
            pe.wait_ge(par_in, 16 * (len(COL_A) + len(COL_B)))
            pe.transpose(PS[:, 0, 0:NCOL_A], par_a, ident[0:NCOL_A, 0:NCOL_A]).then_inc(par_turned, 1)
            pe.transpose(PS[:, 1, 0:NCOL_B], par_b, ident[0:NCOL_B, 0:NCOL_B]).then_inc(par_turned, 1)

            with pe.Fori(0, ET // HOT) as i:
                for k in range(HOT):
                    pe.wait_ge(hot_ready, i * (2 * HOT) + 2 * (k + 1))
                    for s in range(NT):
                        ins = pe.matmul(PS[:, 2 + s, 0:N], hot_s[:, k, s * P:(s + 1) * P], hot_d[:, k, :],
                                        start=False, stop=True, skip_group_check=True)
                    ins.then_inc(hot_used, 1)
            pe.wait_ge(cnt_set, NT)
            for s in range(NT):
                for t in range(NT):
                    ins = pe.transpose(PS[:, 4 + t, s * P:(s + 1) * P], cnt[:, s, t * P:(t + 1) * P], ident[:])
            ins.then_inc(cntT_done, 1)

            pe.wait_ge(noise_in, 16 * 5)
            pe.wait_ge(emb_set, 1)
            mm(PS[0:NC, 6, 0:N], fw1[:], emb, True, True).then_inc(cond_a, 1)
            pe.wait_ge(cond_s, 1)
            mm(PS[0:NC, 7, 0:N], fw2[:], cz, True, True).then_inc(cond_b, 1)

            def turn(tr, ready, value, per):
                pe.wait_ge(ready, value)
                for b in range(2):
                    for c in (2 * b, 2 * b + 1):
                        for t in range(NT):
                            ins = pe.transpose(chunks(0)[:, c, t * P:(t + 1) * P], xn[:, t, c * P:(c + 1) * P], ident[:])
                    ins.then_inc(tr_done, 1)

            def bias_row(bank, i):
                for t in range(NT):
                    mm(PS[:, bank + t, :], ones[0:1, :], bias_of(i), True, False)

            def dense(bank, inT, i, done, bias):
                for t in range(NT):
                    if bias:
                        mm(PS[:, bank + t, :], ones[0:1, :], bias_of(i), True, False)
                    for c in range(CT):
                        ins = mm(PS[:, bank + t, :], inT[:, c, t * P:(t + 1) * P], wbuf[i][:, c, :],
                                 c == 0 and not bias, c == CT - 1)
                    ins.then_inc(done, 1)

            def dense_T(bank, i, inT, done):
                for o in range(CT):
                    for c in range(CT):
                        ins = mm(chunks(bank)[:, o, :], wbuf[i][:, c, o * P:(o + 1) * P], inT[:, c, :], c == 0, c == CT - 1)
                    if o % 2:
                        ins.then_inc(done, 1)

            def layer0(l, first):
                if not first:
                    pe.wait_ge(w_in[1], l * 32)
                turn(l, ln_out, l * 2 + 2, None)
                if not first:
                    mm(PS[0:1, 2, :], ones[0:1, 0:1], bias_of(1), True, False)
                    pe.wait_ge(vn_in, l)
                    for c in range(CT):
                        ins = mm(PS[0:1, 2, :], vtmp[:, c:c + 1], wbuf[1][:, c, :], False, c == CT - 1)
                    ins.then_inc(vn_hid, 1)
                    pe.wait_ge(vn_row, l)
                    for c in range(CT):
                        ins = mm(PS[:, 3, c:c + 1], vrow[0:1, c * P:(c + 1) * P], ones[0:1, 0:1], True, True)
                    ins.then_inc(vn_col, 1)
                    pe.wait_ge(w_in[2], l * 16)
                    pe.wait_ge(vn_act, l)
                    for o in range(CT):
                        for c in range(CT):
                            ins = mm(PS[:, 3, CT + o:CT + o + 1], wbuf[2][:, c, o * P:(o + 1) * P], vhid[:, c:c + 1],
                                     c == 0, c == CT - 1)
                    ins.then_inc(vn_out, 1)
                for val, bank, ready, done in ((m, 4, m_ready, mT_done), (md, 6, md_ready, mdT_done)):
                    pe.wait_ge(ready, l + 1)
                    for t in range(NT):
                        for c in range(CT):
                            ins = pe.transpose(PS[:, bank + t, c * P:(c + 1) * P], val[:, c, t * P:(t + 1) * P], ident[:])
                        ins.then_inc(done, 1)
                for val, bank, ready, done in ((ex, 0, ex_ready, den_done), (mex, 2, mex_ready, num_done)):
                    pe.wait_ge(ready, l * 2 + 2)
                    for c in range(CT):
                        for t in range(NT):
                            ins = mm(chunks(bank)[:, c, :], val[:, t, c * P:(c + 1) * P], cnt[:, t, :], t == 0, t == NT - 1)
                        if c % 2:
                            ins.then_inc(done, 1)
                pe.wait_ge(w_in[0], l * 32 + 32)
                bias_row(4, 0)
                for c in range(CT):
                    pe.wait_ge(z_ready, l * 2 + (c // 2 + 1))
                    for t in range(NT):
                        ins = mm(PS[:, 4 + t, :], z[:, c, t * P:(t + 1) * P], wbuf[0][:, c, :], False, c == CT - 1)
                        if c == CT - 1:
                            ins.then_inc(conv_done, 1)

            pe.wait_ge(cols_set, 4)
            layer0(0, True)
            with pe.Fori(1, LAYERS) as l:
                layer0(l, False)

            def table(k, i, b):
                pe.wait_ge(tabw_in[i], b * 64 + 64)
                for j in range(4):
                    t = j % 2
                    mm(PS[:, 4 + j, :], condT[:, t * P:(t + 1) * P], tabw[:, i, j // 2, :], True, True).then_inc(tab_done, 1)

            pe.wait_ge(cond_set, 1)
            pe.wait_ge(ln_out, LN_L1_IN * 2 + 2)
            with pe.Fori(0, BLOCKS) as b:
                table(b * 2, 0, b)
                turn(b * 2 + TR_BLOCK, y_ready, b * 4 + 2, None)
                pe.wait_ge(yT_ready, b * 4 + 2)
                pe.wait_ge(w_in[3], b * 16 + 16)
                dense_T(2, 3, hT, q_done)
                pe.wait_ge(tab_ready, b * 8 + 4)
                pe.wait_ge(w_in[4], b * 16 + 16)
                dense_T(4, 4, hT, k_done)
                pe.wait_ge(w_in[5], b * 32 + 32)
                dense(6, hT, 5, v_done, True)
                pe.wait_ge(q_ready, b * 4 + 4)
                pe.wait_ge(k_ready, b * 4 + 4)
                for t in range(NT):
                    for hd in range(HEADS):
                        ins = mm(chunks(2 * t)[:, hd, :], qT[:, hd, t * P:(t + 1) * P], kT[:, hd, :], True, True)
                        if hd % 2:
                            ins.then_inc(sc_done, 1)
                pe.wait_ge(v_ready, b * 2 + 2)
                for t in range(NT):
                    for hd in range(HEADS):
                        pe.wait_ge(p_ready, b * 8 + (t * HEADS + hd + 1))
                        for dt in range(NT):
                            ins = pe.transpose(chunks(4 + 2 * dt)[:, hd, t * P:(t + 1) * P],
                                               prob[:, t, hd, dt * P:(dt + 1) * P], ident[:])
                            if t == 1 and hd % 2:
                                ins.then_inc(pT_done, 1)
                pe.wait_ge(pT_act, b * 2 + 2)
                pe.wait_ge(pT_dve, b * 2 + 2)
                for hd in range(HEADS):
                    for dt in range(NT):
                        ins = mm(chunks(0)[:, hd, :], v[:, dt, hd * P:(hd + 1) * P], probT[:, dt, hd, :],
                                 dt == 0, dt == NT - 1)
                    if hd % 2:
                        ins.then_inc(o_done, 1)
                table(b * 2 + 1, 1, b)
                pe.wait_ge(w_in[0], b * 32 + (LAYERS + 1) * 32)
                pe.wait_ge(o_ready, b * 2 + 2)
                dense(2, oT, 0, proj_done, True)
                turn(b * 2 + (TR_BLOCK + 1), y_ready, b * 4 + 4, None)
                pe.wait_ge(yT_ready, b * 4 + 4)
                pe.wait_ge(w_in[1], b * 16 + ((LAYERS - 1) * 32 + 16))
                dense_T(2, 1, hT, up_done)
                pe.wait_ge(w_in[2], b * 32 + ((LAYERS - 1) * 16 + 32))
                pe.wait_ge(up_ready, b * 4 + 4)
                dense(0, mT, 2, down_done, True)

            turn(TR_L2, ln_out, LN_L2 * 2 + 2, None)
            pe.wait_ge(yT_ready, 4 * BLOCKS + 2)
            pe.wait_ge(w_in[3], 16 * (BLOCKS + 1))
            dense(2, hT, 3, beta_done, False)
            pe.wait_ge(w_in[5], 32 * (BLOCKS + 1))
            dense(4, hT, 5, alpha_done, True)
            pe.wait_ge(beta_ready, 2)
            for s in range(NT):
                for t in range(NT):
                    ins = mm(PS[:, 6 + s, :], cntT[:, t, s * P:(s + 1) * P], v[:, t, :], t == 0, t == NT - 1)
                ins.then_inc(gamma_done, 1)

            def gather(g, j, u, first):
                tile = j + g * TG
                if not first:
                    pe.wait_ge(x1_ready, j + (g * TG + 1 - RING))
                for s in range(NT):
                    for k in range(3):
                        ins = mm(PS[:, 2 + u, :], srcT[:, s, bass.ds(tile * P, P)], hs[:, k, s, :],
                                 s == 0 and k == 0, s == NT - 1 and k == 2)
                ins.then_inc(x1_done, 1)

            def gather_group(g):
                start = 0
                if g == 0:
                    for j in range(RING):
                        gather(g, j, j, True)
                    start = 1
                with pe.Fori(start, SIZES[g] // RING) as q:
                    for u in range(RING):
                        gather(g, q * RING + u, (g * TG + u) % RING, False)
                for j in range(SIZES[g] // RING * RING, SIZES[g]):
                    gather(g, j, (g * TG + j) % RING, False)

            def add_tile(g, j, u):
                pe.wait_ge(hotd_ready, j + (g * TG + 1))
                for t in range(NT):
                    ins = pe.matmul(PS[:, t, :], hotd[:, u, t * P:(t + 1) * P],
                                    part[SUM_AT[g]][:, bass.ds(j, 1), :].rearrange("p a d -> p (a d)"),
                                    start=False, stop=True, skip_group_check=True)
                ins.then_inc(tile_summed, 1)

            def sum_group(g):
                pe.wait_ge(path_step, (g + 1) * 2 * PATHS)
                with pe.Fori(0, SIZES[g] // RING) as q:
                    for u in range(RING):
                        add_tile(g, q * RING + u, (g * TG + u) % RING)
                for j in range(SIZES[g] // RING * RING, SIZES[g]):
                    add_tile(g, j, (g * TG + j) % RING)

            pe.wait_ge(srcT_set, SRC_CUT * NT)
            pe.wait_ge(hs_ready, 1)
            gather_group(0)
            gather_group(1)
            for g in range(GROUPS):
                sum_group(g)
                if g + 2 < GROUPS:
                    gather_group(g + 2)

        @block.vector
        def _(dve):
            steps = Steps(dve, dve_step)
            link = steps.link
            carried = []

            def carry():
                carried.append(0)
                dve.memset(idle[0:1, len(carried):len(carried) + 1], 0.0)

            def newton(y, a, w, o):
                link(dve.tensor_tensor(a, y, y, ALU.mult))
                link(dve.tensor_tensor(a, a, w, ALU.mult))
                link(dve.tensor_scalar(a, a, -0.5, 1.5, ALU.mult, ALU.add))
                link(dve.tensor_tensor(o, y, a, ALU.mult))

            def layer_norm(n, inp):
                for t in range(NT):
                    ins = dve.bn_stats(st[:, t, :], inp[:, t, :])
                link(ins)
                carry()
                for t in range(NT):
                    ins = dve.bn_aggr(mv[:, t, :], st[:, t, :])
                link(ins)
                dve.tensor_scalar(var[:], mv[:, :, 1], LN_EPS, None, ALU.add).then_inc(ln_var, 1)
                dve.wait_ge(ln_est, n + 1)
                dve.wait_ge(ln_var, n + 1)
                newton(est[:], nwt[:], var[:], rstd[:])
                for t in range(NT):
                    dve.tensor_scalar(xn[:, t, :], inp[:, t, :], mv[:, t, 0:1], rstd[:, t:t + 1],
                                      ALU.subtract, ALU.mult).then_inc(ln_out, 1)

            dve.memset(path[:], 0).then_inc(path_clear, 1)
            dve.wait_ge(edges_in, 32)
            dve.tensor_copy(src_f[:], src_i[:]).then_inc(edges_f, 1)
            dve.tensor_copy(dst_f[:], dst_i[:]).then_inc(edges_f, 1)
            dve.tensor_scalar(dst_n[:], dst_i[:], -1.0, None, ALU.mult).then_inc(edges_f, 1)
            dve.memset(PS[:, 2:4, :], 0.0).then_inc(edges_f, 1)
            dve.wait_ge(edges_f, 4)
            dve.wait_ge(consts_set, CONSTS)
            def hot(tile, k):
                dve.tensor_scalar(hot_s[:, k, :], iota_b[:], src_f[:, bass.ds(tile, 1)], None, ALU.is_equal).then_inc(hot_ready, 1)
                dve.tensor_scalar(hot_d[:, k, :], iota_b[:], dst_f[:, bass.ds(tile, 1)], None, ALU.is_equal).then_inc(hot_ready, 1)

            for k in range(HOT):
                hot(k, k)
            with dve.Fori(1, ET // HOT) as i:
                for k in range(HOT):
                    dve.wait_ge(hot_used, i * HOT + (k + 1 - HOT))
                    hot(i * HOT + k, k)
            dve.wait_ge(hot_used, ET)
            for s in range(NT):
                dve.tensor_copy(cnt[:, s, :], PS[:, 2 + s, 0:N]).then_inc(cnt_set, 1)
            dve.wait_ge(cnt_set, NT)
            link(dve.tensor_scalar(mask[:], cnt[:], 0.0, MASKED, ALU.is_equal, ALU.mult))
            link(dve.tensor_reduce(outdeg[:], cnt[:], AX.X, ALU.add))
            link(dve.reciprocal(outrec[:], outdeg[:]))
            dve.wait_ge(cntT_done, 1)
            for t in range(NT):
                dve.tensor_copy(cntT[:, t, :], PS[:, 4 + t, 0:N]).then_inc(cols_set, 1)
            dve.wait_ge(par_turned, 2)
            dve.tensor_copy(cols[:, 0:NCOL_A], PS[:, 0, 0:NCOL_A]).then_inc(cols_set, 1)
            dve.tensor_copy(cols[:, NCOL_A:], PS[:, 1, 0:NCOL_B]).then_inc(cols_set, 1)
            dve.wait_ge(cols_set, 4)

            dve.wait_ge(path_in, 32)
            dve.wait_ge(path_clear, 1)
            table = path[0:1, :].rearrange("a (r k) -> a r k", k=4)
            raw = path_raw[0:1, :].rearrange("a (r k) -> a r k", k=3)
            dve.tensor_scalar(table[:, 0:PATHS, 0:2], raw[:, :, 0:2], EXT, None, ALU.mult)
            link(dve.tensor_scalar(table[:, AHEAD:, 2:3], raw[:, :, 2:3], EXT, None, ALU.mult))
            dve.wait_ge(noise_in, 16 * 5)
            link(dve.tensor_scalar(freq[:, 0:1], freq_i[:], float(np.float32(TWO_PI / 16)), None, ALU.mult))
            link(dve.tensor_scalar(emb, emb, freq[:, 0:1], None, ALU.mult))
            link(dve.tensor_scalar(turns, emb, float(1 / TWO_PI), freq[:, 1:2], ALU.mult, ALU.add))
            link(dve.tensor_scalar(turns, turns, ROUND, None, ALU.add))
            link(dve.tensor_scalar(turns, turns, -ROUND, None, ALU.add))
            for third in (PI_A, PI_B, PI_C):
                link(dve.scalar_tensor_tensor(out=emb, in0=turns, scalar=-third, in1=emb, op0=ALU.mult, op1=ALU.add))
            link(dve.tensor_scalar(turns, emb, freq[:, 2:3], PI_CLIP, ALU.add, ALU.min))
            dve.tensor_scalar(turns, turns, -PI_CLIP, None, ALU.max).then_inc(angle_set, 1)
            dve.wait_ge(cond_a, 1)
            dve.tensor_scalar(cz, PS[0:NC, 6, 0:N], fb[:, 0:1], None, ALU.add).then_inc(cond_z, 1)
            dve.wait_ge(cond_e, 1)
            dve.wait_ge(cond_z, 1)
            link(dve.tensor_scalar(ce, ce, 1.0, None, ALU.add))
            link(dve.reciprocal(ce, ce))
            dve.tensor_tensor(cz, cz, ce, ALU.mult).then_inc(cond_s, 1)
            dve.wait_ge(cond_b, 1)
            dve.tensor_scalar(condT[0:NC, :], PS[0:NC, 7, 0:N], fb[:, 1:2], None, ALU.add).then_inc(cond_set, 1)

            def layer0(l, first):
                layer_norm(l, x if first else h)
                if first:
                    link(dve.tensor_copy(vn[:], cols[:, COL["vn_emb"]:COL["vn_emb"] + CT]))
                    dve.wait_ge(hT_ready, CT)
                else:
                    def par(name):
                        return cols[:, bass.ds(l * CT + (COL[name] - CT), CT)]

                    dve.wait_ge(hT_ready, l * CT + CT)
                    dve.tensor_tensor(vtmp[:], hsum[:], vn[:], ALU.add).then_inc(vn_in, 1)
                    dve.wait_ge(vn_hid, l)
                    link(dve.bn_stats(vst[:], PS[0:1, 2, :]))
                    carry()
                    link(dve.bn_aggr(vmv[:], vst[:]))
                    dve.tensor_scalar(vvar[0:1, 0:1], vmv[0:1, 1:2], LN_EPS, None, ALU.add).then_inc(vn_var, 1)
                    dve.wait_ge(vn_est, l)
                    dve.wait_ge(vn_var, l)
                    newton(vvar[0:1, 2:3], vvar[0:1, 3:4], vvar[0:1, 0:1], vvar[0:1, 1:2])
                    dve.tensor_scalar(vrow[:], PS[0:1, 2, :], vmv[0:1, 0:1], vvar[0:1, 1:2],
                                      ALU.subtract, ALU.mult).then_inc(vn_row, 1)
                    dve.wait_ge(vn_col, l)
                    link(dve.tensor_tensor(vhid[:], PS[:, 3, 0:CT], par("vn_g"), ALU.mult))
                    link(dve.tensor_tensor(vhid[:], vhid[:], par("vn_beta"), ALU.add))
                    dve.tensor_scalar(vhid[:], vhid[:], 0.0, None, ALU.max).then_inc(vn_act, 1)
                    dve.wait_ge(vn_out, l)
                    link(dve.tensor_tensor(vn[:], PS[:, 3, CT:2 * CT], par("vn_b2"), ALU.add))
                for c in range(CT):
                    ins = dve.tensor_scalar(hv[:, c, :], hT[:, c, :], vn[:, c:c + 1], None, ALU.add)
                link(ins)
                dve.tensor_scalar(m, hv, 0.0, MSG_EPS, ALU.max, ALU.add).then_inc(m_ready, 1)
                dve.wait_ge(m_ready, l + 1)
                link(dve.tensor_reduce(mmax[:], m, AX.X, ALU.max))
                for c in range(CT):
                    ins = dve.tensor_scalar(md[:, c, :], m[:, c, :], mmax[:, c:c + 1], None, ALU.subtract)
                ins.then_inc(md_ready, 1)
                for t in range(NT):
                    dve.wait_ge(mT_done, l * 2 + (t + 1))
                    dve.wait_ge(ex_ready, l * 2 + (t + 1))
                    dve.tensor_tensor(mex[:, t, :], PS[:, 4 + t, :], ex[:, t, :], ALU.mult).then_inc(mex_ready, 1)
                for b in range(2):
                    two = slice(2 * b, 2 * b + 2)
                    dve.wait_ge(rec_est, l * 2 + (b + 1))
                    link(dve.tensor_tensor(z[:, two, :], chunks(0)[:, two, :], rec[:, two, :], ALU.mult))
                    link(dve.scalar_tensor_tensor(out=z[:, two, :], in0=z[:, two, :], scalar=-2.0,
                                                  in1=rec[:, two, :], op0=ALU.add, op1=ALU.mult))
                    dve.wait_ge(num_done, l * 2 + (b + 1))
                    link(dve.tensor_tensor(z[:, two, :], chunks(2)[:, two, :], z[:, two, :], ALU.mult))
                    dve.tensor_tensor(z[:, two, :], hv[:, two, :], z[:, two, :], ALU.subtract).then_inc(z_ready, 1)
                for t in range(NT):
                    dve.wait_ge(conv_done, l * 2 + (t + 1))
                    if first:
                        ins = dve.tensor_copy(h[:, t, :], PS[:, 4 + t, :])
                    else:
                        ins = dve.tensor_tensor(h[:, t, :], PS[:, 4 + t, :], h[:, t, :], ALU.add)
                link(ins)

            dve.wait_ge(x_in, 16)
            layer0(0, True)
            with dve.Fori(1, LAYERS) as l:
                steps.enter(l - 1, 24)
                layer0(l, False)
            steps.leave(LAYERS - 1)

            layer_norm(LN_L0_LAST, h)
            dve.wait_ge(ln_out, LN_L0_LAST * 2 + 2)
            dve.wait_ge(gb_in, 32)
            for k, op, o in ((0, ALU.mult, xn), (1, ALU.add, xn)):
                for t in range(NT):
                    ins = dve.tensor_tensor(o[:, t, :], xn[:, t, :], gb[:, k, :], op)
                link(ins)
            link(dve.tensor_tensor(x[:], x[:], xn[:], ALU.add))
            layer_norm(LN_L1_IN, x)
            dve.wait_ge(ln_out, LN_L1_IN * 2 + 2)
            link(dve.tensor_scalar(h[:], xn[:], 0.0, None, ALU.max))

            def cond_norm(k):
                layer_norm(k + LN_BLOCK, h)
                dve.wait_ge(ln_out, k * 2 + (LN_BLOCK * 2 + 2))
                dve.wait_ge(tab_ready, k * 4 + 4)
                for t in range(NT):
                    ins = dve.scalar_tensor_tensor(out=xn[:, t, :], in0=tab[:, 0, t, :], scalar=1.0, in1=xn[:, t, :],
                                                   op0=ALU.add, op1=ALU.mult)
                link(ins)
                for t in range(NT):
                    dve.tensor_tensor(xn[:, t, :], xn[:, t, :], tab[:, 1, t, :], ALU.add).then_inc(y_ready, 1)

            def residual(bank, done, value):
                for t in range(NT):
                    dve.wait_ge(done, value + (t + 1))
                    ins = dve.tensor_tensor(h[:, t, :], PS[:, bank + t, :], h[:, t, :], ALU.add)
                link(ins)

            with dve.Fori(0, BLOCKS) as b:
                steps.enter(b, 24)
                cond_norm(b * 2)
                for hd in range(HEADS):
                    dve.wait_ge(k_done, b * 2 + (hd // 2 + 1))
                    dve.tensor_scalar(kT[:, hd, :], chunks(4)[:, hd, :], cols[:, bass.ds(b * CT + (COL["bk"] + hd), 1)],
                                      None, ALU.add).then_inc(k_ready, 1)
                for t in range(NT):
                    for hd in range(HEADS):
                        k = t * HEADS + hd
                        if hd % 2 == 0:
                            dve.wait_ge(sc_done, b * 4 + (2 * t + hd // 2 + 1))
                            carry()
                        ins = dve.tensor_tensor_reduce(out=prob[:, t, hd, :], in0=chunks(2 * t)[:, hd, :],
                                                       in1=mask[:, t, :], scale=float(DH) ** -0.5, scalar=-3e38,
                                                       op0=ALU.add, op1=ALU.max, accum_out=smax[:, k:k + 1])
                    link(ins)
                    four = slice(t * HEADS, (t + 1) * HEADS)
                    dve.tensor_scalar(nmax[:, four], smax[:, four], -1.0, None, ALU.mult).then_inc(smax_ready, 1)
                for t in range(NT):
                    four = slice(t * HEADS, (t + 1) * HEADS)
                    for hd in range(HEADS):
                        k = t * HEADS + hd
                        dve.wait_ge(exp_ready, b * 8 + (k + 1))
                        ins = dve.tensor_tensor_reduce(out=prob[:, t, hd, :], in0=prob[:, t, hd, :],
                                                       in1=cnt[:, t, :], scale=1.0, scalar=0.0,
                                                       op0=ALU.mult, op1=ALU.add, accum_out=den[:, k:k + 1])
                    link(ins)
                    link(dve.tensor_scalar(den[:, four], den[:, four], TINY, None, ALU.max))
                    link(dve.reciprocal(rden[:, four], den[:, four]))
                    for hd in range(HEADS):
                        k = t * HEADS + hd
                        dve.tensor_scalar(prob[:, t, hd, :], prob[:, t, hd, :], rden[:, k:k + 1], None,
                                          ALU.mult).then_inc(p_ready, 1)
                for i in range(2):
                    dve.wait_ge(pT_done, b * 4 + (2 * i + 2))
                    dve.tensor_copy(probT[:, 1, 2 * i:2 * i + 2, :], chunks(6)[:, 2 * i:2 * i + 2, :]).then_inc(pT_dve, 1)
                residual(2, proj_done, b * 2)
                cond_norm(b * 2 + 1)
                residual(0, down_done, b * 2)
            steps.leave(BLOCKS)

            link(dve.tensor_tensor(x[:], x[:], h[:], ALU.add))
            layer_norm(LN_L2, x)
            for t in range(NT):
                dve.wait_ge(alpha_done, t + 1)
                ins = dve.tensor_tensor(x[:, t, :], PS[:, 4 + t, :], x[:, t, :], ALU.add)
            link(ins)
            for t in range(NT):
                dve.wait_ge(gamma_done, t + 1)
                ins = dve.scalar_tensor_tensor(out=x[:, t, :], in0=PS[:, 6 + t, :], scalar=outrec[:, t:t + 1],
                                               in1=x[:, t, :], op0=ALU.mult, op1=ALU.add)
            link(ins)
            layer_norm(LN_L3, x)
            dve.wait_ge(ln_out, LN_L3 * 2 + 2)
            link(dve.tensor_scalar(h[:], xn[:], 0.0, None, ALU.max))
            dve.memset(PS[:, 0:NT, :], 0.0)
            link(dve.tensor_copy(hs[:, 0, :, :], h[:]))
            link(dve.tensor_tensor(h[:], h[:], hs[:, 0, :, :], ALU.subtract))
            link(dve.tensor_copy(hs[:, 1, :, :], h[:]))
            dve.tensor_tensor(hs[:, 2, :, :], h[:], hs[:, 1, :, :], ALU.subtract).then_inc(hs_ready, 1)

            regs = [[dve.alloc_register(f"path{u}_{k}") for k in range(4)] for u in range(RING)]
            for g in range(GROUPS):
                if g > 0:
                    dve.wait_ge(path_step, g * 2 * PATHS)
                dve.memset(part[SUM_AT[g]][:, TG // 2:TG, :], 0.0).then_inc(acc_zero, 1)
                dve.wait_ge(x2_in[g], 16)
                dve.wait_ge(x1_ready, min((g + 1) * TG, ET))
                dve.wait_ge(acc_zero, (g + 1) * 2)
                n = SIZES[g]
                xs, xe, sums = (part[at[g]][:, 0:n, :] for at in (SOURCE_AT, EDGE_AT, SUM_AT))

                def path_rows(row, lo, n_rows, slot):
                    at = [four for four in regs[0:n_rows]]
                    dve.load([r for four in at for r in four], path[0:1, bass.ds(row * 4, 4 * n_rows)])
                    for j in range(n_rows):
                        i1, i2, i3 = (dve.snap(r, min_val=0, max_val=(SEGS - 1) * EXT) for r in at[j][0:3])
                        if lo + j >= AHEAD:
                            dve.wait_ge(path_step, row * 2 + (g * 2 * PATHS + 2 * j + 1 - 2 * AHEAD))
                            o = sums[:, :, bass.ds(i3, EXT)]
                            dve.tensor_tensor(o, o, prod[:, (slot + j - AHEAD) % RING, 0:n, :], ALU.add).then_inc(path_step, 1)
                        if lo + j < PATHS:
                            dve.scalar_tensor_tensor(
                                out=prod[:, (slot + j) % RING, 0:n, :], in0=xs[:, :, bass.ds(i1, EXT)],
                                scalar=coef[:, bass.ds(row + j, 1)], in1=xe[:, :, bass.ds(i2, EXT)],
                                op0=ALU.mult, op1=ALU.mult).then_inc(path_step, 1)

                path_rows(0, 0, AHEAD, 0)
                with dve.Fori(0, PATHS // RING - 1) as q:
                    path_rows(q * RING + AHEAD, AHEAD, RING, AHEAD)
                last = PATHS - RING + AHEAD
                path_rows(last, last, RING, last % RING)
            for t in range(NT):
                dve.wait_ge(tile_summed, ET)
                dve.tensor_tensor(x[:, t, :], PS[:, t, :], x[:, t, :], ALU.add).then_inc(final, 1)


_OUTS = [((N, D), "float32")]


def kernel(**inputs):
    import numpy as _np
    import concourse.bacc as _bacc
    from concourse import mybir as _mybir
    from concourse.bass_utils import run_bass_kernel_spmd as _run

    nc = _bacc.Bacc("TRN2", target_bir_lowering=False, num_devices=1)
    arrays, args = {}, {}
    for name in inputs:
        a = _np.ascontiguousarray(inputs[name])
        arrays[f"in_{name}_dram"] = a
        args[name] = nc.dram_tensor(f"in_{name}_dram", a.shape, _mybir.dt.from_np(a.dtype), kind="ExternalInput").ap()
    shape, dtype = _OUTS[0]
    out = nc.dram_tensor("out_0_dram", shape, _mybir.dt.from_np(_np.dtype(dtype)), kind="ExternalOutput").ap()
    gnn_stack_kernel(nc, args, out)
    r = _run(nc, [arrays], core_ids=[0])
    return r.results[0]["out_0_dram"]
```

```python
from contextlib import ExitStack

import concourse.bass as bass
import concourse.mybir as mybir
import numpy as np

F32 = mybir.dt.float32
BF16 = mybir.dt.bfloat16
I32 = mybir.dt.int32
ALU = mybir.AluOpType
ACT = mybir.ActivationFunctionType
AX = mybir.AxisListType

P = 128
N = 256
NT = N // P
D = 512
CT = D // P
E = 8192
ET = E // P
LAYERS = 7
BLOCKS = 4
HEADS = 4
DH = D // HEADS
NF = 32
NC = 16
SEGS, EXT, PATHS = 16, 32, 64
GROUPS = 5
TG = -(-ET // GROUPS)
SIZES = [min(TG, ET - g * TG) for g in range(GROUPS)]
RING = 4
EDGE_AT = [0, 3, 0, 3, 0]
SOURCE_AT = [1, 4, 2, 1, 4]
SUM_AT = [2, 1, 4, 2, 1]
SRC_CUT = 4
HOT = 4

LN_EPS = 1e-5
MSG_EPS = 1e-7
AHEAD = 2
CONSTS = 17
MASKED = -1e30
TINY = 1e-30
DEN_SCALE = float(2.0 ** 40)
DEN_SHIFT = float(40 * np.log(2.0))
DEN_TINY = float(2.0 ** -60)
TWO_PI = 2 * np.pi
PI_A = 6.28125
PI_B = float(np.floor((TWO_PI - PI_A) * 2 ** 24) / 2 ** 24)
PI_C = float(TWO_PI - PI_A - PI_B)
ROUND = 12582912.0
PI_CLIP = 3.1415925

COL_A = [("norm_g", LAYERS), ("norm_b", LAYERS), ("vn_emb", 1), ("vn_g", LAYERS - 1), ("vn_beta", LAYERS - 1)]
COL_B = [("vn_b2", LAYERS - 1), ("bq", BLOCKS), ("bk", BLOCKS), ("m_b1", BLOCKS)]


def column_table():
    at, col = {}, 0
    for name, n in COL_A + COL_B:
        at[name] = col
        col += CT * n
    return at, CT * sum(n for _, n in COL_A), CT * sum(n for _, n in COL_B)


LN_L0_LAST, LN_L1_IN, LN_BLOCK, LN_L2, LN_L3 = 7, 8, 9, 17, 18
OUT_L2, OUT_L3 = LN_L1_IN + 1, LN_L1_IN + 2
TR_BLOCK, TR_L2 = 7, 15


class Steps:

    def __init__(self, eng, sem):
        self.eng, self.sem, self.base, self.n = eng, sem, 0, 0

    def link(self, ins):
        self.n += 1
        ins.then_inc(self.sem, 1)
        self.eng.wait_ge(self.sem, self.base + self.n)

    def enter(self, it, per):
        self.outer, self.start, self.per = self.base, self.base + self.n, per
        self.base, self.n = it * per + self.start, 0

    def leave(self, times):
        assert self.n == self.per, self.n
        self.base, self.n = self.start, self.per * times


def gnn_stack_kernel(nc, A, out):
    COL, NCOL_A, NCOL_B = column_table()
    ctx = ExitStack()
    with ctx:
        def sb(name, shape, dt=F32):
            return ctx.enter_context(nc.sbuf_tensor(name, shape, dt))

        def sem(name):
            return ctx.enter_context(nc.semaphore(name))

        PS = ctx.enter_context(nc.psum_tensor("PS", [P, 8, 512], F32))

        def chunks(bank):
            return PS[:, bank:bank + 2, :].rearrange("p b (c n) -> p (b c) n", n=N)

        GW = TG * D
        big = sb("big", [P, 5 * GW])
        part = [big[:, i * GW:(i + 1) * GW].rearrange("p (j d) -> p j d", j=TG) for i in range(5)]
        assert 6 * CT * D <= 2 * GW and 10 * 1024 <= 2 * GW
        W = big[:, GW:GW + 6 * CT * D]
        wbuf = [W[:, i * CT * D:(i + 1) * CT * D].rearrange("p (c n) -> p c n", c=CT) for i in range(6)]
        R = big[:, 3 * GW:3 * GW + 10 * 1024]

        spare = big[:, 3 * GW + 10 * 1024:5 * GW]

        def region(k, n=1):
            return R[:, 1024 * k:1024 * (k + n)]

        def as_c(ap):
            return ap.rearrange("p (c n) -> p c n", c=CT)

        def as_t(ap):
            return ap.rearrange("p (t n) -> p t n", t=NT)

        x = sb("x", [P, NT, D])
        h = sb("h", [P, NT, D])
        xn = sb("xn", [P, NT, D])
        hT = sb("hT", [P, CT, N])
        hv = as_c(region(0))
        m = as_c(region(1))
        md = as_c(region(2))
        ex = as_t(region(3))
        mex = as_t(region(4))
        rec = as_c(region(5))
        z = as_c(region(6))
        gb = region(8, 2).rearrange("p (k n) -> p k n", k=4)
        qT = as_c(region(0))
        kT = as_c(region(1))
        v = as_t(region(2))
        prob = region(3, 2).rearrange("p (t h n) -> p t h n", t=NT, h=HEADS)
        probT = region(5, 2).rearrange("p (t h n) -> p t h n", t=NT, h=HEADS)
        oT = as_c(region(7))
        mT = as_c(region(0))
        tab = region(8, 2).rearrange("p (k t n) -> p k t n", k=2, t=NT)
        CUT = E // SRC_CUT
        src_all = big[:, 0:3 * CUT].bitcast(I32)
        assert 3 * CUT <= GW
        srcT = sb("srcT", [P, NT, E], BF16)
        tail = sb("tail", [P, 8 * D])
        brow = tail[:, 0:4 * D]
        tabw = tail[0:NC + 1, 4 * D:8 * D].rearrange("q (i k d) -> q i k d", i=2, k=2)
        prod = tail[:, 0:RING * TG * EXT].rearrange("p (r j u) -> p r j u", r=RING, u=EXT)
        hs = tail[:, 4 * D:7 * D].bitcast(BF16).rearrange("p (k t d) -> p k t d", k=3, t=NT)
        assert RING * TG * EXT <= 4 * D
        hotd = xn[:, :, :].rearrange("p t (i n) -> p (t i) n", n=N)
        src_i = sb("src_i", [P, ET], I32)
        dst_i = sb("dst_i", [P, ET], I32)
        src_f = sb("src_f", [P, ET])
        dst_f = sb("dst_f", [P, ET])
        dst_n = sb("dst_n", [P, ET])
        iota_f = sb("iota_f", [P, N])
        iota_b = sb("iota_b", [P, N], BF16)
        iota_p = sb("iota_p", [P, NT])
        hot_s, hot_d = hT[:, 0:2, :].bitcast(BF16), hT[:, 2:4, :].bitcast(BF16)
        hot_s = hot_s.rearrange("p c n -> p (c n)").rearrange("p (k n) -> p k n", k=HOT)
        hot_d = hot_d.rearrange("p c n -> p (c n)").rearrange("p (k n) -> p k n", k=HOT)
        cnt = sb("cnt", [P, NT, N])
        cntT = sb("cntT", [P, NT, N])
        mask = sb("mask", [P, NT, N])
        outdeg = sb("outdeg", [P, NT])
        outrec = sb("outrec", [P, NT])
        ident = sb("ident", [P, P])
        ones = sb("ones", [P, P])
        par_a = xn[0:NCOL_A, 0, 0:P]
        par_b = xn[0:NCOL_B, 1, 0:P]
        cols = sb("cols", [P, NCOL_A + NCOL_B])
        consts = sb("consts", [P, 5])
        zero, ln_tiny, den_shift, one, ln_eps = (consts[:, i:i + 1] for i in range(5))
        idle = sb("idle", [1, 40])
        st = sb("st", [P, NT, 6])
        mv = sb("mv", [P, NT, 2])
        var = sb("var", [P, NT])
        lnv = sb("lnv", [P, NT])
        est = sb("est", [P, NT])
        nwt = sb("nwt", [P, NT])
        rstd = sb("rstd", [P, NT])
        hsum = sb("hsum", [P, CT])
        vn = sb("vn", [P, CT])
        vtmp = sb("vtmp", [P, CT])
        vhid = sb("vhid", [P, CT])
        vrow = spare[0:1, N:N + D]
        vst = sb("vst", [1, 6])
        vmv = sb("vmv", [1, 2])
        vvar = sb("vvar", [1, 4])
        hmax = sb("hmax", [P, CT])
        vne = sb("vne", [P, CT])
        mmax = sb("mmax", [P, CT])
        smax = sb("smax", [P, NT * HEADS])
        nmax = sb("nmax", [P, NT * HEADS])
        den = sb("den", [P, NT * HEADS])
        rden = sb("rden", [P, NT * HEADS])
        emb = region(7)[0:2 * NF, 0:N]
        turns = region(7)[0:2 * NF, N:2 * N]
        freq = sb("freq", [2 * NF, 4])
        freq_i = sb("freq_i", [2 * NF, 1], I32)
        fw1 = sb("fw1", [2 * NF, NC])
        fw2 = sb("fw2", [NC, NC])
        fb = sb("fb", [NC, 2])
        cz = region(7)[0:NC, 2 * N:3 * N]
        ce = region(7)[0:NC, 3 * N:4 * N]
        condT = spare[0:NC + 1, 0:N]
        path = sb("path", [1, (PATHS + AHEAD) * 4], I32)
        path_raw = sb("path_raw", [1, PATHS * 3], I32)
        coef = sb("coef", [P, PATHS])

        src_in = [sem(f"src_in{c}") for c in range(SRC_CUT)]
        x_in, edges_in, par_in, gb_in = map(sem, ["x_in", "edges_in", "par_in", "gb_in"])
        noise_in, path_in, path_clear = map(sem, ["noise_in", "path_in", "path_clear"])
        w_in = [sem(f"w_in{i}") for i in range(6)]
        tabw_in = [sem(f"tabw_in{i}") for i in range(2)]
        x2_in = [sem(f"x2_in{g}") for g in range(GROUPS)]
        out_done = sem("out_done")
        zeroed, consts_set, edges_f, hot_ready, hot_used, cnt_done, cnt_set, cntT_done, cntT_set = map(
            sem, ["zeroed", "consts_set", "edges_f", "hot_ready", "hot_used", "cnt_done", "cnt_set", "cntT_done",
                  "cntT_set"])
        par_turned, cols_set, srcT_set = map(sem, ["par_turned", "cols_set", "srcT_set"])
        angle_set, emb_set, cond_a, cond_z, cond_e, cond_s, cond_b, cond_set = map(
            sem, ["angle_set", "emb_set", "cond_a", "cond_z", "cond_e", "cond_s", "cond_b", "cond_set"])
        ln_var, ln_est, ln_out, tr_done = map(sem, ["ln_var", "ln_est", "ln_out", "tr_done"])
        bias_added = sem("bias_added")
        dve_step, act_step = sem("dve_step"), sem("act_step")
        hT_ready, vn_in, vn_hid, vn_var, vn_est, vn_row, vn_col, vn_act, vn_out = map(
            sem, ["hT_ready", "vn_in", "vn_hid", "vn_var", "vn_est", "vn_row", "vn_col", "vn_act", "vn_out"])
        m_ready, md_ready, mT_done, mdT_done, ex_ready, mex_ready, den_done, num_done, rec_est, z_ready, conv_done = map(
            sem, ["m_ready", "md_ready", "mT_done", "mdT_done", "ex_ready", "mex_ready", "den_done", "num_done",
                  "rec_est", "z_ready", "conv_done"])
        tab_done, tab_ready, y_ready, yT_ready, q_done, k_done, v_done, q_ready, k_ready, v_ready = map(
            sem, ["tab_done", "tab_ready", "y_ready", "yT_ready", "q_done", "k_done", "v_done", "q_ready", "k_ready",
                  "v_ready"])
        sc_done, smax_ready, exp_ready, p_ready, pT_done, pT_act, pT_dve, o_done, o_ready, proj_done = map(
            sem, ["sc_done", "smax_ready", "exp_ready", "p_ready", "pT_done", "pT_act", "pT_dve", "o_done", "o_ready",
                  "proj_done"])
        up_done, up_ready, down_done = map(sem, ["up_done", "up_ready", "down_done"])
        beta_done, beta_ready, alpha_done, gamma_done = map(sem, ["beta_done", "beta_ready", "alpha_done", "gamma_done"])
        hs_ready, hot_squared, hotd_ready, acc_zero, x1_done, x1_ready, path_step, tile_summed, final = map(
            sem, ["hs_ready", "hot_squared", "hotd_ready", "acc_zero", "x1_done", "x1_ready", "path_step",
                  "tile_summed", "final"])

        block = ctx.enter_context(nc.Block())

        def halves(bank):
            return PS[:, bank, :].rearrange("p (t d) -> p t d", t=NT)

        def bias_of(i):
            k = min(i, 3)
            return brow[0:1 if i == 1 else P, k * D:(k + 1) * D]

        def rows(ap):
            return ap.rearrange("(c p) n -> p c n", p=P)

        def one_row(ap):
            return ap.rearrange("(a n) -> a n", a=1)

        def nodes(ap):
            return ap.rearrange("(t p) d -> p t d", p=P)

        @block.sync
        def _(sp):
            def load_w(i, weight, bias):
                sp.dma_start(wbuf[i], rows(weight)).then_inc(w_in[i], 16)
                if bias is not None:
                    sp.dma_start(bias_of(i), one_row(bias) if i == 1 else spread(one_row(bias))).then_inc(w_in[i], 16)

            def spread(row):
                return row.to_broadcast([P, D])

            def load_tab(i, k, b):
                ws, bs, wb, bb = [("s1_w", "s1_b", "b1_w", "b1_b"), ("s2_w", "s2_b", "b2_w", "b2_b")][i]
                sp.dma_start(tabw[0:NC, i, 0, :], A["L1_gnn_" + ws][b, :, :]).then_inc(tabw_in[i], 16)
                sp.dma_start(tabw[0:NC, i, 1, :], A["L1_gnn_" + wb][b, :, :]).then_inc(tabw_in[i], 16)
                sp.dma_start(tabw[NC:NC + 1, i, 0, :], A["L1_gnn_" + bs][bass.ds(b, 1), :]).then_inc(tabw_in[i], 16)
                sp.dma_start(tabw[NC:NC + 1, i, 1, :], A["L1_gnn_" + bb][bass.ds(b, 1), :]).then_inc(tabw_in[i], 16)

            sp.dma_start(x[:], nodes(A["x"])).then_inc(x_in, 16)
            sp.dma_start(src_i[:], A["src"].rearrange("(p t) -> p t", t=ET)).then_inc(edges_in, 16)
            sp.dma_start(dst_i[:], A["dst"].rearrange("(p t) -> p t", t=ET)).then_inc(edges_in, 16)
            r = 0
            for tile, names in ((par_a, COL_A), (par_b, COL_B)):
                r = 0
                for name, n in names:
                    full = ("L1_gnn_" if name in ("bq", "bk", "m_b1") else "L0_gnn_") + name
                    a = A[full]
                    a = a.rearrange("(c p) -> c p", p=P) if n == 1 else a.rearrange("l (c p) -> (l c) p", p=P)
                    sp.dma_start(tile[r:r + CT * n, :], a).then_inc(par_in, 16)
                    r += CT * n
            load_w(0, A["L0_gnn_gcn_W"][0], A["L0_gnn_gcn_b"][0])
            load_w(1, A["L0_gnn_vn_W1"][0], A["L0_gnn_vn_b1"][0])
            load_w(2, A["L0_gnn_vn_W2"][0], None)
            sp.dma_start(emb, A["node_vec1"].rearrange("n a -> a n").to_broadcast([2 * NF, N])).then_inc(noise_in, 16)
            sp.dma_start(fw1[:], A["L1_gnn_f_w1"]).then_inc(noise_in, 16)
            sp.dma_start(fw2[:], A["L1_gnn_f_w2"]).then_inc(noise_in, 16)
            sp.dma_start(fb[:, 0:1], A["L1_gnn_f_b1"].rearrange("(n a) -> n a", a=1)).then_inc(noise_in, 16)
            sp.dma_start(fb[:, 1:2], A["L1_gnn_f_b2"].rearrange("(n a) -> n a", a=1)).then_inc(noise_in, 16)
            for c in range(SRC_CUT):
                if c >= 3:
                    sp.wait_ge(srcT_set, (c - 2) * NT)
                sp.dma_start(src_all[:, (c % 3) * CUT:(c % 3 + 1) * CUT],
                             one_row(A["src"])[:, c * CUT:(c + 1) * CUT].to_broadcast([P, CUT])).then_inc(src_in[c], 16)
            for k, name in enumerate(("norm_g", "norm_b")):
                sp.dma_start(gb[:, k, :], A["L0_gnn_" + name][LAYERS - 1:LAYERS, :].to_broadcast([P, D])).then_inc(gb_in, 16)
            load_w(3, A["L1_gnn_wq"][0], None)
            load_w(4, A["L1_gnn_wk"][0], None)
            load_w(5, A["L1_gnn_wv"][0], A["L1_gnn_bv"][0])
            sp.dma_start(path_raw[:], A["L3_gnn_path_indices"].rearrange("(a k) c -> a (k c)", a=1)).then_inc(path_in, 16)
            sp.dma_start(coef[:], one_row(A["L3_gnn_path_coeffs"]).to_broadcast([P, PATHS])).then_inc(path_in, 16)
            load_tab(0, 0, 0)
            load_tab(1, 0, 0)

            def edge_group(g):
                rows_of = A["edge_attr_512"].rearrange("(p t) d -> p t d", t=ET)
                sp.dma_start(part[EDGE_AT[g]][:, 0:SIZES[g], :], rows_of[:, g * TG:g * TG + SIZES[g], :]).then_inc(x2_in[g], 16)

            sp.wait_ge(srcT_set, SRC_CUT * NT)
            edge_group(0)

            def conv_weights(l):
                sp.wait_ge(conv_done, l * 2)
                sp.wait_ge(bias_added, l)
                sp.dma_start(wbuf[0], rows(A["L0_gnn_gcn_W"][bass.ds(l, 1)].rearrange("a k n -> (a k) n"))).then_inc(w_in[0], 16)
                sp.dma_start(bias_of(0), spread(A["L0_gnn_gcn_b"][bass.ds(l, 1), :])).then_inc(w_in[0], 16)

            with sp.Fori(1, LAYERS - 1) as l:
                conv_weights(l)
                sp.wait_ge(vn_hid, l)
                sp.dma_start(wbuf[1], rows(A["L0_gnn_vn_W1"][bass.ds(l, 1)].rearrange("a k n -> (a k) n"))).then_inc(w_in[1], 16)
                sp.dma_start(bias_of(1), A["L0_gnn_vn_b1"][bass.ds(l, 1), :]).then_inc(w_in[1], 16)
                sp.wait_ge(vn_out, l)
                sp.dma_start(wbuf[2], rows(A["L0_gnn_vn_W2"][bass.ds(l, 1)].rearrange("a k n -> (a k) n"))).then_inc(w_in[2], 16)
            conv_weights(LAYERS - 1)
            sp.wait_ge(vn_hid, LAYERS - 1)
            load_w(1, A["L1_gnn_m_w1"][0], None)
            sp.wait_ge(vn_out, LAYERS - 1)
            load_w(2, A["L1_gnn_m_w2"][0], A["L1_gnn_m_b2"][0])
            sp.wait_ge(conv_done, 2 * LAYERS)
            sp.wait_ge(bias_added, LAYERS)
            load_w(0, A["L1_gnn_wo"][0], A["L1_gnn_bo"][0])

            def w_at(name, b):
                return rows(A["L1_gnn_" + name][bass.ds(b, 1)].rearrange("a k n -> (a k) n"))

            with sp.Fori(0, BLOCKS - 1) as b:
                sp.wait_ge(tab_done, b * 8 + 4)
                load_tab(0, 0, b + 1)
                sp.wait_ge(q_done, b * 2 + 2)
                sp.dma_start(wbuf[3], w_at("wq", b + 1)).then_inc(w_in[3], 16)
                sp.wait_ge(k_done, b * 2 + 2)
                sp.dma_start(wbuf[4], w_at("wk", b + 1)).then_inc(w_in[4], 16)
                sp.wait_ge(v_done, b * 2 + 2)
                sp.dma_start(wbuf[5], w_at("wv", b + 1)).then_inc(w_in[5], 16)
                sp.wait_ge(v_ready, b * 2 + 2)
                sp.dma_start(bias_of(5), spread(A["L1_gnn_bv"][bass.ds(b + 1, 1), :])).then_inc(w_in[5], 16)
                sp.wait_ge(tab_done, b * 8 + 8)
                load_tab(1, 0, b + 1)
                sp.wait_ge(proj_done, b * 2 + 2)
                sp.dma_start(wbuf[0], w_at("wo", b + 1)).then_inc(w_in[0], 16)
                sp.wait_ge(bias_added, b * 2 + (LAYERS + 1))
                sp.dma_start(bias_of(0), spread(A["L1_gnn_bo"][bass.ds(b + 1, 1), :])).then_inc(w_in[0], 16)
                sp.wait_ge(up_done, b * 2 + 2)
                sp.dma_start(wbuf[1], w_at("m_w1", b + 1)).then_inc(w_in[1], 16)
                sp.wait_ge(down_done, b * 2 + 2)
                sp.dma_start(wbuf[2], w_at("m_w2", b + 1)).then_inc(w_in[2], 16)
                sp.wait_ge(bias_added, b * 2 + (LAYERS + 2))
                sp.dma_start(bias_of(2), spread(A["L1_gnn_m_b2"][bass.ds(b + 1, 1), :])).then_inc(w_in[2], 16)
            sp.wait_ge(q_done, 2 * BLOCKS)
            load_w(3, A["L2_gnn_wn"], None)
            sp.wait_ge(v_done, 2 * BLOCKS)
            sp.wait_ge(v_ready, 2 * BLOCKS)
            load_w(5, A["L2_gnn_wc"], A["L2_gnn_bias"])

            sp.wait_ge(hs_ready, 1)
            edge_group(1)
            for g in range(2, GROUPS):
                sp.wait_ge(path_step, (g - 1) * 2 * PATHS)
                edge_group(g)
            sp.wait_ge(final, 1)
            sp.dma_start(nodes(out)[:, 0, :], x[:, 0, :]).then_inc(out_done, 16)
            sp.wait_ge(final, 2)
            sp.dma_start(nodes(out)[:, 1, :], x[:, 1, :]).then_inc(out_done, 16)
            sp.wait_ge(out_done, 32)

        @block.gpsimd
        def _(pool):
            pool.memset(ident[:], 0.0).then_inc(zeroed, 1)
            pool.memset(ones[:], 1.0).then_inc(consts_set, 1)
            pool.memset(consts[:, 0:1], 0.0).then_inc(consts_set, 1)
            pool.memset(consts[:, 1:2], DEN_TINY).then_inc(consts_set, 1)
            pool.memset(consts[:, 2:3], DEN_SHIFT).then_inc(consts_set, 1)
            pool.memset(one, 1.0).then_inc(consts_set, 1)
            pool.memset(ln_eps, LN_EPS).then_inc(consts_set, 1)
            pool.memset(condT[:], 1.0).then_inc(consts_set, 1)
            pool.iota(iota_f[:], pattern=[[1, N]], base=0, channel_multiplier=0,
                      allow_small_or_imprecise_dtypes=True).then_inc(consts_set, 1)
            pool.iota(iota_b[:], pattern=[[1, N]], base=0, channel_multiplier=0,
                      allow_small_or_imprecise_dtypes=True).then_inc(consts_set, 1)
            pool.iota(iota_p[:], pattern=[[P, NT]], base=0, channel_multiplier=1,
                      allow_small_or_imprecise_dtypes=True).then_inc(consts_set, 1)
            for k in range(2):
                half = slice(NF * k, NF * (k + 1))
                pool.wait_ge(consts_set, 10 + 3 * k)
                pool.iota(freq_i[half, :], pattern=[[0, 1]], base=1, channel_multiplier=1).then_inc(consts_set, 1)
                pool.memset(freq[half, 1:2], 0.25 * k).then_inc(consts_set, 1)
                pool.memset(freq[half, 2:3], float(np.pi / 2) * k).then_inc(consts_set, 1)
            pool.wait_ge(zeroed, 1)
            pool.wait_ge(consts_set, CONSTS - 1)
            pool.affine_select(out=ident[:], in_=ident[:], compare_op=ALU.not_equal, fill=1.0, base=0,
                               pattern=[[-1, P]], channel_multiplier=1).then_inc(consts_set, 1)
            pool.wait_ge(consts_set, CONSTS)
            for c in range(SRC_CUT):
                pool.wait_ge(src_in[c], 16)
                q = P // SRC_CUT
                by_tile = src_all[:, (c % 3) * CUT:(c % 3 + 1) * CUT].rearrange("s (p t) -> s t p", t=ET)
                for s in range(NT):
                    pool.tensor_scalar(srcT[:, s, :].rearrange("s (t p) -> s t p", p=P)[:, :, c * q:(c + 1) * q],
                                       by_tile, iota_p[:, s:s + 1], None, ALU.is_equal).then_inc(srcT_set, 1)

            pool.wait_ge(alpha_done, 2)
            pool.wait_ge(beta_done, 2)
            for g in range(GROUPS):
                if g > 0:
                    pool.wait_ge(path_step, g * 2 * PATHS)
                pool.memset(part[SUM_AT[g]][:, 0:TG // 2, :], 0.0).then_inc(acc_zero, 1)

        @block.scalar
        def _(act):
            steps = Steps(act, act_step)

            def rsqrt_estimate(n):
                act.wait_ge(ln_var, n + 1)
                steps.link(act.activation(lnv[:], mv[:, :, 1], ACT.Ln, bias=ln_eps))
                act.activation(est[:], lnv[:], ACT.Exp, bias=zero, scale=-0.5).then_inc(ln_est, 1)

            def turned(tr):
                for b in range(2):
                    act.wait_ge(tr_done, tr * 2 + (b + 1))
                    yield b

            act.wait_ge(consts_set, CONSTS)
            act.wait_ge(angle_set, 1)
            act.activation(emb, turns, ACT.Sin, bias=zero[0:2 * NF, :]).then_inc(emb_set, 1)
            act.wait_ge(cond_z, 1)
            act.activation(ce, cz, ACT.Exp, bias=zero[0:NC, :], scale=-1.0).then_inc(cond_e, 1)

            act.preload_act_table_set("natural_log_exp_and_others")

            def layer0(l, first):
                rsqrt_estimate(l)
                for b in turned(l):
                    for c in (2 * b, 2 * b + 1):
                        if first:
                            act.activation(hT[:, c, :], chunks(0)[:, c, :], ACT.Relu, bias=zero).then_inc(hT_ready, 1)
                        else:
                            act.activation(hT[:, c, :], chunks(0)[:, c, :], ACT.Relu,
                                           bias=cols[:, bass.ds(l * CT + (COL["norm_b"] - CT + c), 1)],
                                           scale=cols[:, bass.ds(l * CT + (COL["norm_g"] - CT + c), 1)],
                                           accum_out=hsum[:, c:c + 1]).then_inc(hT_ready, 1)
                if not first:
                    act.wait_ge(vn_var, l)
                    steps.link(act.activation(vvar[0:1, 1:2], vmv[0:1, 1:2], ACT.Ln, bias=ln_eps[0:1, :]))
                    act.activation(vvar[0:1, 2:3], vvar[0:1, 1:2], ACT.Exp, bias=zero[0:1, :], scale=-0.5).then_inc(vn_est, 1)
                for b in range(2):
                    act.wait_ge(mdT_done, l * 2 + (b + 1))
                    act.activation(ex[:, :, b * N:(b + 1) * N], halves(6 + b), ACT.Exp, bias=zero).then_inc(ex_ready, 1)
                for b in range(2):
                    act.wait_ge(den_done, l * 2 + (b + 1))
                    steps.link(act.activation(rec[:, 2 * b:2 * b + 2, :], chunks(0)[:, 2 * b:2 * b + 2, :], ACT.Ln,
                                              bias=ln_tiny, scale=DEN_SCALE))
                    act.activation(rec[:, 2 * b:2 * b + 2, :], rec[:, 2 * b:2 * b + 2, :], ACT.Exp, bias=den_shift,
                                   scale=-1.0).then_inc(rec_est, 1)

            act.wait_ge(cols_set, 2)
            layer0(0, True)
            with act.Fori(1, LAYERS) as l:
                steps.enter(l - 1, 4)
                layer0(l, False)
            steps.leave(LAYERS - 1)
            rsqrt_estimate(LN_L0_LAST)
            rsqrt_estimate(LN_L1_IN)

            def table(k, part):
                for t in range(NT):
                    act.wait_ge(tab_done, k * 4 + (2 * part + t + 1))
                    act.activation(tab[:, part, t, :], PS[:, 4 + 2 * part + t, :], ACT.Identity,
                                   bias=zero if part else one).then_inc(tab_ready, 1)

            def y_turned(k):
                for b in turned(k + TR_BLOCK):
                    act.activation(hT[:, 2 * b:2 * b + 2, :], chunks(0)[:, 2 * b:2 * b + 2, :], ACT.Copy).then_inc(yT_ready, 1)

            with act.Fori(0, BLOCKS) as b:
                steps.enter(b, 2)
                table(b * 2, 0)
                rsqrt_estimate(b * 2 + LN_BLOCK)
                table(b * 2, 1)
                y_turned(b * 2)
                for hd in range(HEADS):
                    act.wait_ge(q_done, b * 2 + (hd // 2 + 1))
                    act.activation(qT[:, hd, :], chunks(2)[:, hd, :], ACT.Identity,
                                   bias=cols[:, bass.ds(b * CT + (COL["bq"] + hd), 1)]).then_inc(q_ready, 1)
                for t in range(NT):
                    act.wait_ge(smax_ready, b * 2 + (t + 1))
                    for hd in range(HEADS):
                        k = t * HEADS + hd
                        act.activation(prob[:, t, hd, :], prob[:, t, hd, :], ACT.Exp,
                                       bias=nmax[:, k:k + 1]).then_inc(exp_ready, 1)
                for i in range(2):
                    act.wait_ge(pT_done, b * 4 + (2 * i + 1))
                    act.activation(probT[:, 0, 2 * i:2 * i + 2, :], chunks(4)[:, 2 * i:2 * i + 2, :],
                                   ACT.Copy).then_inc(pT_act, 1)
                for i in range(2):
                    act.wait_ge(o_done, b * 2 + (i + 1))
                    act.activation(oT[:, 2 * i:2 * i + 2, :], chunks(0)[:, 2 * i:2 * i + 2, :], ACT.Copy).then_inc(o_ready, 1)
                table(b * 2 + 1, 0)
                rsqrt_estimate(b * 2 + (LN_BLOCK + 1))
                table(b * 2 + 1, 1)
                y_turned(b * 2 + 1)
                for c in range(CT):
                    act.wait_ge(up_done, b * 2 + (c // 2 + 1))
                    act.activation(mT[:, c, :], chunks(2)[:, c, :], ACT.Relu,
                                   bias=cols[:, bass.ds(b * CT + (COL["m_b1"] + c), 1)]).then_inc(up_ready, 1)
            steps.leave(BLOCKS)

            rsqrt_estimate(LN_L2)
            for b in turned(TR_L2):
                act.activation(hT[:, 2 * b:2 * b + 2, :], chunks(0)[:, 2 * b:2 * b + 2, :], ACT.Relu, bias=zero).then_inc(yT_ready, 1)
            for t in range(NT):
                act.wait_ge(beta_done, t + 1)
                act.activation(v[:, t, :], PS[:, 2 + t, :], ACT.Copy).then_inc(beta_ready, 1)
            rsqrt_estimate(LN_L3)

            def x1_tile(g, j, u):
                act.wait_ge(x1_done, j + (g * TG + 1))
                act.activation(part[SOURCE_AT[g]][:, bass.ds(j, 1), :].rearrange("p a d -> p (a d)"),
                               PS[:, 2 + u, :], ACT.Copy).then_inc(x1_ready, 1)

            def x1_group(g):
                with act.Fori(0, SIZES[g] // RING) as q:
                    for u in range(RING):
                        x1_tile(g, q * RING + u, (g * TG + u) % RING)
                for j in range(SIZES[g] // RING * RING, SIZES[g]):
                    x1_tile(g, j, (g * TG + j) % RING)

            def hot(tile, u, count):
                act.activation(hotd[:, u, :], iota_f[:], ACT.Square, bias=dst_n[:, bass.ds(tile, 1)]).then_inc(hot_squared, 1)
                act.wait_ge(hot_squared, count)
                act.activation(hotd[:, u, :], hotd[:, u, :], ACT.Relu, bias=one, scale=-1.0).then_inc(hotd_ready, 1)

            x1_group(0)
            x1_group(1)
            act.wait_ge(hs_ready, 1)
            for u in range(RING):
                hot(u, u, u + 1)
            done = 1
            for g in range(GROUPS):
                upto = ((g + 1) * TG - 1) // RING + 1 if g < GROUPS - 1 else ET // RING
                with act.Fori(done, upto) as q:
                    for u in range(RING):
                        act.wait_ge(tile_summed, q * RING + (u + 1 - RING))
                        hot(q * RING + u, u, q * RING + (u + 1))
                done = upto
                if g + 2 < GROUPS:
                    act.wait_ge(tile_summed, (g + 1) * TG)
                    x1_group(g + 2)

        @block.tensor
        def _(pe):
            def mm(o, lhsT, rhs, start, stop):
                return pe.matmul(o, lhsT, rhs, start=start, stop=stop)

            pe.wait_ge(consts_set, CONSTS)
            pe.wait_ge(par_in, 16 * (len(COL_A) + len(COL_B)))
            pe.transpose(PS[:, 0, 0:NCOL_A], par_a, ident[0:NCOL_A, 0:NCOL_A]).then_inc(par_turned, 1)
            pe.transpose(PS[:, 1, 0:NCOL_B], par_b, ident[0:NCOL_B, 0:NCOL_B]).then_inc(par_turned, 1)

            with pe.Fori(0, ET // HOT) as i:
                for k in range(HOT):
                    pe.wait_ge(hot_ready, i * (2 * HOT) + 2 * (k + 1))
                    for s in range(NT):
                        ins = pe.matmul(PS[:, 2 + s, 0:N], hot_s[:, k, s * P:(s + 1) * P], hot_d[:, k, :],
                                        start=False, stop=True, skip_group_check=True)
                    ins.then_inc(hot_used, 1)
            pe.wait_ge(cnt_set, NT)
            for s in range(NT):
                for t in range(NT):
                    ins = pe.transpose(PS[:, 4 + t, s * P:(s + 1) * P], cnt[:, s, t * P:(t + 1) * P], ident[:])
            ins.then_inc(cntT_done, 1)

            pe.wait_ge(noise_in, 16 * 5)
            pe.wait_ge(emb_set, 1)
            mm(PS[0:NC, 6, 0:N], fw1[:], emb, True, True).then_inc(cond_a, 1)
            pe.wait_ge(cond_s, 1)
            mm(PS[0:NC, 7, 0:N], fw2[:], cz, True, True).then_inc(cond_b, 1)

            def turn(tr, ready, value):
                for t in range(NT):
                    pe.wait_ge(ready, value + (t + 1))
                    for c in range(CT):
                        ins = pe.transpose(chunks(0)[:, c, t * P:(t + 1) * P], xn[:, t, c * P:(c + 1) * P], ident[:])
                        if t == NT - 1 and c % 2:
                            ins.then_inc(tr_done, 1)

            def dense(bank, inT, i, done, ready, value):
                for t in range(NT):
                    for c in range(CT):
                        if t == 0 and c % 2 == 0 and ready is not None:
                            pe.wait_ge(ready, value + (c // 2 + 1))
                        ins = mm(PS[:, bank + t, :], inT[:, c, t * P:(t + 1) * P], wbuf[i][:, c, :], c == 0, c == CT - 1)
                    ins.then_inc(done, 1)

            def dense_T(bank, i, inT, done, ready, value):
                for o in range(CT):
                    for c in range(CT):
                        if o == 0 and c % 2 == 0 and ready is not None:
                            pe.wait_ge(ready, value + (c // 2 + 1))
                        ins = mm(chunks(bank)[:, o, :], wbuf[i][:, c, o * P:(o + 1) * P], inT[:, c, :], c == 0, c == CT - 1)
                    if o % 2:
                        ins.then_inc(done, 1)

            def layer0(l, first):
                if not first:
                    pe.wait_ge(w_in[1], l * 32)
                turn(l, ln_out, l * 2)
                if not first:
                    mm(PS[0:1, 2, :], ones[0:1, 0:1], bias_of(1), True, False)
                    pe.wait_ge(vn_in, l)
                    for c in range(CT):
                        ins = mm(PS[0:1, 2, :], vtmp[:, c:c + 1], wbuf[1][:, c, :], False, c == CT - 1)
                    ins.then_inc(vn_hid, 1)
                    pe.wait_ge(vn_row, l)
                    for c in range(CT):
                        ins = mm(PS[:, 3, c:c + 1], vrow[0:1, c * P:(c + 1) * P], ones[0:1, 0:1], True, True)
                    ins.then_inc(vn_col, 1)
                    pe.wait_ge(w_in[2], l * 16)
                    pe.wait_ge(vn_act, l)
                    for o in range(CT):
                        for c in range(CT):
                            ins = mm(PS[:, 3, CT + o:CT + o + 1], wbuf[2][:, c, o * P:(o + 1) * P], vhid[:, c:c + 1],
                                     c == 0, c == CT - 1)
                    ins.then_inc(vn_out, 1)
                for b in range(2):
                    for val, bank, ready, done in ((m, 4, m_ready, mT_done), (md, 6, md_ready, mdT_done)):
                        pe.wait_ge(ready, l * 2 + (b + 1))
                        for c in range(2):
                            for t in range(NT):
                                ins = pe.transpose(halves(bank + b)[:, t, c * P:(c + 1) * P],
                                                   val[:, 2 * b + c, t * P:(t + 1) * P], ident[:])
                        ins.then_inc(done, 1)
                for val, bank, ready, done in ((ex, 0, ex_ready, den_done), (mex, 2, mex_ready, num_done)):
                    for c in range(CT):
                        if c % 2 == 0:
                            pe.wait_ge(ready, l * 2 + (c // 2 + 1))
                        for t in range(NT):
                            ins = mm(chunks(bank)[:, c, :], val[:, t, c * P:(c + 1) * P], cnt[:, t, :], t == 0, t == NT - 1)
                        if c % 2:
                            ins.then_inc(done, 1)
                pe.wait_ge(w_in[0], l * 32 + 32)
                for b in range(2):
                    pe.wait_ge(z_ready, l * 2 + (b + 1))
                    for t in range(NT):
                        for c in (2 * b, 2 * b + 1):
                            ins = mm(PS[:, 4 + t, :], z[:, c, t * P:(t + 1) * P], wbuf[0][:, c, :], c == 0, c == CT - 1)
                        if b:
                            ins.then_inc(conv_done, 1)

            pe.wait_ge(cols_set, 4)
            layer0(0, True)
            with pe.Fori(1, LAYERS) as l:
                layer0(l, False)

            def table(k, i, b):
                pe.wait_ge(tabw_in[i], b * 64 + 64)
                for j in range(4):
                    t = j % 2
                    mm(PS[:, 4 + j, :], condT[:, t * P:(t + 1) * P], tabw[:, i, j // 2, :], True, True).then_inc(tab_done, 1)

            pe.wait_ge(cond_set, 1)
            pe.wait_ge(ln_out, LN_L1_IN * 2 + 2)
            with pe.Fori(0, BLOCKS) as b:
                table(b * 2, 0, b)
                turn(b * 2 + TR_BLOCK, y_ready, b * 4)
                pe.wait_ge(w_in[3], b * 16 + 16)
                dense_T(2, 3, hT, q_done, yT_ready, b * 4)
                pe.wait_ge(tab_ready, b * 8 + 4)
                pe.wait_ge(w_in[4], b * 16 + 16)
                dense_T(4, 4, hT, k_done, None, 0)
                pe.wait_ge(q_ready, b * 4 + 4)
                for t in range(NT):
                    for hd in range(HEADS):
                        if t == 0:
                            pe.wait_ge(k_ready, b * 4 + (hd + 1))
                        ins = mm(chunks(2 * t)[:, hd, :], qT[:, hd, t * P:(t + 1) * P], kT[:, hd, :], True, True)
                        if hd % 2:
                            ins.then_inc(sc_done, 1)
                pe.wait_ge(smax_ready, b * 2 + 1)
                pe.wait_ge(w_in[5], b * 32 + 32)
                dense(0, hT, 5, v_done, None, 0)
                for t in range(NT):
                    for hd in range(HEADS):
                        pe.wait_ge(p_ready, b * 8 + (t * HEADS + hd + 1))
                        for dt in range(NT):
                            ins = pe.transpose(chunks(4 + 2 * dt)[:, hd, t * P:(t + 1) * P],
                                               prob[:, t, hd, dt * P:(dt + 1) * P], ident[:])
                            if t == 1 and hd % 2:
                                ins.then_inc(pT_done, 1)
                pe.wait_ge(v_ready, b * 2 + 2)
                for hd in range(HEADS):
                    if hd % 2 == 0:
                        pe.wait_ge(pT_act, b * 2 + (hd // 2 + 1))
                        pe.wait_ge(pT_dve, b * 2 + (hd // 2 + 1))
                    for dt in range(NT):
                        ins = mm(chunks(0)[:, hd, :], v[:, dt, hd * P:(hd + 1) * P], probT[:, dt, hd, :],
                                 dt == 0, dt == NT - 1)
                    if hd % 2:
                        ins.then_inc(o_done, 1)
                pe.wait_ge(w_in[0], b * 32 + (LAYERS + 1) * 32)
                dense(2, oT, 0, proj_done, o_ready, b * 2)
                table(b * 2 + 1, 1, b)
                turn(b * 2 + (TR_BLOCK + 1), y_ready, b * 4 + 2)
                pe.wait_ge(w_in[1], b * 16 + ((LAYERS - 1) * 32 + 16))
                dense_T(2, 1, hT, up_done, yT_ready, b * 4 + 2)
                pe.wait_ge(w_in[2], b * 32 + ((LAYERS - 1) * 16 + 32))
                pe.wait_ge(up_ready, b * 4 + 4)
                dense(0, mT, 2, down_done, None, 0)

            turn(TR_L2, ln_out, OUT_L2 * 2)
            pe.wait_ge(w_in[3], 16 * (BLOCKS + 1))
            dense(2, hT, 3, beta_done, yT_ready, 4 * BLOCKS)
            pe.wait_ge(w_in[5], 32 * (BLOCKS + 1))
            dense(4, hT, 5, alpha_done, None, 0)
            pe.wait_ge(beta_ready, 2)
            for s in range(NT):
                for t in range(NT):
                    ins = mm(PS[:, 6 + s, :], cntT[:, t, s * P:(s + 1) * P], v[:, t, :], t == 0, t == NT - 1)
                ins.then_inc(gamma_done, 1)

            def gather(g, j, u, first):
                tile = j + g * TG
                if not first:
                    pe.wait_ge(x1_ready, j + (g * TG + 1 - RING))
                for s in range(NT):
                    for k in range(3):
                        ins = mm(PS[:, 2 + u, :], srcT[:, s, bass.ds(tile * P, P)], hs[:, k, s, :],
                                 s == 0 and k == 0, s == NT - 1 and k == 2)
                ins.then_inc(x1_done, 1)

            def gather_group(g):
                start = 0
                if g == 0:
                    for j in range(RING):
                        gather(g, j, j, True)
                    start = 1
                with pe.Fori(start, SIZES[g] // RING) as q:
                    for u in range(RING):
                        gather(g, q * RING + u, (g * TG + u) % RING, False)
                for j in range(SIZES[g] // RING * RING, SIZES[g]):
                    gather(g, j, (g * TG + j) % RING, False)

            def add_tile(g, j, u):
                pe.wait_ge(hotd_ready, j + (g * TG + 1))
                for t in range(NT):
                    ins = pe.matmul(PS[:, t, :], hotd[:, u, t * P:(t + 1) * P],
                                    part[SUM_AT[g]][:, bass.ds(j, 1), :].rearrange("p a d -> p (a d)"),
                                    start=False, stop=True, skip_group_check=True)
                ins.then_inc(tile_summed, 1)

            def sum_group(g):
                pe.wait_ge(path_step, (g + 1) * 2 * PATHS)
                with pe.Fori(0, SIZES[g] // RING) as q:
                    for u in range(RING):
                        add_tile(g, q * RING + u, (g * TG + u) % RING)
                for j in range(SIZES[g] // RING * RING, SIZES[g]):
                    add_tile(g, j, (g * TG + j) % RING)

            pe.wait_ge(srcT_set, SRC_CUT * NT)
            pe.wait_ge(hs_ready, 1)
            gather_group(0)
            gather_group(1)
            for g in range(GROUPS):
                sum_group(g)
                if g + 2 < GROUPS:
                    gather_group(g + 2)

        @block.vector
        def _(dve):
            steps = Steps(dve, dve_step)
            link = steps.link
            carried = []

            def carry():
                carried.append(0)
                dve.memset(idle[0:1, len(carried):len(carried) + 1], 0.0)

            def newton(y, a, w, o):
                link(dve.tensor_tensor(a, y, y, ALU.mult))
                link(dve.tensor_tensor(a, a, w, ALU.mult))
                link(dve.tensor_scalar(a, a, -0.5, 1.5, ALU.mult, ALU.add))
                link(dve.tensor_tensor(o, y, a, ALU.mult))

            def stats(t, inp):
                return dve.bn_stats(st[:, t, :], inp[:, t, :])

            def variance(n):
                carry()
                for t in range(NT):
                    ins = dve.bn_aggr(mv[:, t, :], st[:, t, :])
                ins.then_inc(ln_var, 1)
                dve.wait_ge(ln_var, n + 1)
                dve.tensor_scalar(var[:], mv[:, :, 1], LN_EPS, None, ALU.add)

            def refine(n):
                dve.wait_ge(ln_est, n + 1)
                newton(est[:], nwt[:], var[:], rstd[:])

            def take_stats(inp):
                for t in range(NT):
                    ins = stats(t, inp)
                link(ins)

            def layer_norm(n, inp):
                variance(n)
                refine(n)
                for t in range(NT):
                    dve.tensor_scalar(xn[:, t, :], inp[:, t, :], mv[:, t, 0:1], rstd[:, t:t + 1],
                                      ALU.subtract, ALU.mult).then_inc(ln_out, 1)

            def residual(bank, done, value):
                for t in range(NT):
                    dve.wait_ge(done, value + (t + 1))
                    link(dve.tensor_tensor(h[:, t, :], PS[:, bank + t, :], h[:, t, :], ALU.add))
                    ins = stats(t, h)
                link(ins)

            def add_bias(i, to):
                for t in range(NT):
                    ins = dve.tensor_tensor(to[:, t, :], to[:, t, :], bias_of(i), ALU.add)
                ins.then_inc(bias_added, 1)

            dve.memset(path[:], 0).then_inc(path_clear, 1)
            dve.wait_ge(edges_in, 32)
            dve.tensor_copy(src_f[:], src_i[:]).then_inc(edges_f, 1)
            dve.tensor_copy(dst_f[:], dst_i[:]).then_inc(edges_f, 1)
            dve.tensor_scalar(dst_n[:], dst_i[:], -1.0, None, ALU.mult).then_inc(edges_f, 1)
            dve.memset(PS[:, 2:4, :], 0.0).then_inc(edges_f, 1)
            dve.wait_ge(edges_f, 4)
            dve.wait_ge(consts_set, CONSTS)
            def hot(tile, k):
                dve.tensor_scalar(hot_s[:, k, :], iota_b[:], src_f[:, bass.ds(tile, 1)], None, ALU.is_equal).then_inc(hot_ready, 1)
                dve.tensor_scalar(hot_d[:, k, :], iota_b[:], dst_f[:, bass.ds(tile, 1)], None, ALU.is_equal).then_inc(hot_ready, 1)

            for k in range(HOT):
                hot(k, k)
            with dve.Fori(1, ET // HOT) as i:
                for k in range(HOT):
                    dve.wait_ge(hot_used, i * HOT + (k + 1 - HOT))
                    hot(i * HOT + k, k)
            dve.wait_ge(hot_used, ET)
            for s in range(NT):
                dve.tensor_copy(cnt[:, s, :], PS[:, 2 + s, 0:N]).then_inc(cnt_set, 1)
            dve.wait_ge(cnt_set, NT)
            link(dve.tensor_scalar(mask[:], cnt[:], 0.0, MASKED, ALU.is_equal, ALU.mult))
            link(dve.tensor_reduce(outdeg[:], cnt[:], AX.X, ALU.add))
            link(dve.reciprocal(outrec[:], outdeg[:]))
            dve.wait_ge(cntT_done, 1)
            for t in range(NT):
                dve.tensor_copy(cntT[:, t, :], PS[:, 4 + t, 0:N]).then_inc(cols_set, 1)
            dve.wait_ge(par_turned, 2)
            dve.tensor_copy(cols[:, 0:NCOL_A], PS[:, 0, 0:NCOL_A]).then_inc(cols_set, 1)
            dve.tensor_copy(cols[:, NCOL_A:], PS[:, 1, 0:NCOL_B]).then_inc(cols_set, 1)
            dve.wait_ge(cols_set, 4)

            dve.wait_ge(path_in, 32)
            dve.wait_ge(path_clear, 1)
            table = path[0:1, :].rearrange("a (r k) -> a r k", k=4)
            raw = path_raw[0:1, :].rearrange("a (r k) -> a r k", k=3)
            dve.tensor_scalar(table[:, 0:PATHS, 0:2], raw[:, :, 0:2], EXT, None, ALU.mult)
            link(dve.tensor_scalar(table[:, AHEAD:, 2:3], raw[:, :, 2:3], EXT, None, ALU.mult))
            dve.wait_ge(noise_in, 16 * 5)
            link(dve.tensor_scalar(freq[:, 0:1], freq_i[:], float(np.float32(TWO_PI / 16)), None, ALU.mult))
            link(dve.tensor_scalar(emb, emb, freq[:, 0:1], None, ALU.mult))
            link(dve.tensor_scalar(turns, emb, float(1 / TWO_PI), freq[:, 1:2], ALU.mult, ALU.add))
            link(dve.tensor_scalar(turns, turns, ROUND, None, ALU.add))
            link(dve.tensor_scalar(turns, turns, -ROUND, None, ALU.add))
            for third in (PI_A, PI_B, PI_C):
                link(dve.scalar_tensor_tensor(out=emb, in0=turns, scalar=-third, in1=emb, op0=ALU.mult, op1=ALU.add))
            link(dve.tensor_scalar(turns, emb, freq[:, 2:3], PI_CLIP, ALU.add, ALU.min))
            dve.tensor_scalar(turns, turns, -PI_CLIP, None, ALU.max).then_inc(angle_set, 1)
            dve.wait_ge(cond_a, 1)
            dve.tensor_scalar(cz, PS[0:NC, 6, 0:N], fb[:, 0:1], None, ALU.add).then_inc(cond_z, 1)
            dve.wait_ge(cond_e, 1)
            dve.wait_ge(cond_z, 1)
            link(dve.tensor_scalar(ce, ce, 1.0, None, ALU.add))
            link(dve.reciprocal(ce, ce))
            dve.tensor_tensor(cz, cz, ce, ALU.mult).then_inc(cond_s, 1)
            dve.wait_ge(cond_b, 1)
            dve.tensor_scalar(condT[0:NC, :], PS[0:NC, 7, 0:N], fb[:, 1:2], None, ALU.add).then_inc(cond_set, 1)

            def layer0(l, first):
                layer_norm(l, x if first else h)
                dve.wait_ge(hT_ready, l * CT + CT)
                if first:
                    link(dve.tensor_copy(vn[:], cols[:, COL["vn_emb"]:COL["vn_emb"] + CT]))
                    dve.tensor_reduce(hmax[:], hT[:], AX.X, ALU.max)
                else:
                    def par(name):
                        return cols[:, bass.ds(l * CT + (COL[name] - CT), CT)]

                    dve.tensor_tensor(vtmp[:], hsum[:], vn[:], ALU.add).then_inc(vn_in, 1)
                    link(dve.tensor_reduce(hmax[:], hT[:], AX.X, ALU.max))
                    dve.wait_ge(w_in[0], l * 32 + 32)
                    carry()
                    add_bias(0, h)
                    dve.wait_ge(vn_hid, l)
                    link(dve.bn_stats(vst[:], PS[0:1, 2, :]))
                    carry()
                    dve.bn_aggr(vmv[:], vst[:]).then_inc(vn_var, 1)
                    dve.wait_ge(vn_var, l)
                    dve.tensor_scalar(vvar[0:1, 0:1], vmv[0:1, 1:2], LN_EPS, None, ALU.add)
                    dve.wait_ge(vn_est, l)
                    newton(vvar[0:1, 2:3], vvar[0:1, 3:4], vvar[0:1, 0:1], vvar[0:1, 1:2])
                    dve.tensor_scalar(vrow[:], PS[0:1, 2, :], vmv[0:1, 0:1], vvar[0:1, 1:2],
                                      ALU.subtract, ALU.mult).then_inc(vn_row, 1)
                    dve.wait_ge(vn_col, l)
                    link(dve.tensor_tensor(vhid[:], PS[:, 3, 0:CT], par("vn_g"), ALU.mult))
                    link(dve.tensor_tensor(vhid[:], vhid[:], par("vn_beta"), ALU.add))
                    dve.tensor_scalar(vhid[:], vhid[:], 0.0, None, ALU.max).then_inc(vn_act, 1)
                    dve.wait_ge(vn_out, l)
                    link(dve.tensor_tensor(vn[:], PS[:, 3, CT:2 * CT], par("vn_b2"), ALU.add))
                link(dve.tensor_scalar(vne[:], vn[:], MSG_EPS, None, ALU.add))
                dve.tensor_tensor(mmax[:], hmax[:], vne[:], ALU.add)
                for b in range(2):
                    for c in (2 * b, 2 * b + 1):
                        ins = dve.tensor_scalar(m[:, c, :], hT[:, c, :], vne[:, c:c + 1], MSG_EPS, ALU.add, ALU.max)
                    ins.then_inc(m_ready, 1)
                    dve.wait_ge(m_ready, l * 2 + (b + 1))
                    if b == 0:
                        link(dve.tensor_scalar(mmax[:], mmax[:], MSG_EPS, None, ALU.max))
                    for c in (2 * b, 2 * b + 1):
                        ins = dve.tensor_scalar(md[:, c, :], m[:, c, :], mmax[:, c:c + 1], None, ALU.subtract)
                    ins.then_inc(md_ready, 1)
                for c in range(CT):
                    ins = dve.tensor_scalar(hv[:, c, :], hT[:, c, :], vn[:, c:c + 1], None, ALU.add)
                for b in range(2):
                    half = slice(b * N, (b + 1) * N)
                    dve.wait_ge(mT_done, l * 2 + (b + 1))
                    dve.wait_ge(ex_ready, l * 2 + (b + 1))
                    dve.tensor_tensor(mex[:, :, half], halves(4 + b), ex[:, :, half], ALU.mult).then_inc(mex_ready, 1)
                for b in range(2):
                    two = slice(2 * b, 2 * b + 2)
                    dve.wait_ge(rec_est, l * 2 + (b + 1))
                    link(dve.tensor_tensor(z[:, two, :], chunks(0)[:, two, :], rec[:, two, :], ALU.mult))
                    link(dve.scalar_tensor_tensor(out=z[:, two, :], in0=z[:, two, :], scalar=-2.0,
                                                  in1=rec[:, two, :], op0=ALU.add, op1=ALU.mult))
                    dve.wait_ge(num_done, l * 2 + (b + 1))
                    link(dve.tensor_tensor(z[:, two, :], chunks(2)[:, two, :], z[:, two, :], ALU.mult))
                    dve.tensor_tensor(z[:, two, :], hv[:, two, :], z[:, two, :], ALU.subtract).then_inc(z_ready, 1)
                if first:
                    dve.wait_ge(w_in[0], 32)
                    for t in range(NT):
                        dve.wait_ge(conv_done, t + 1)
                        ins = dve.tensor_tensor(h[:, t, :], PS[:, 4 + t, :], bias_of(0), ALU.add)
                    ins.then_inc(bias_added, 1)
                    dve.wait_ge(bias_added, 1)
                    take_stats(h)
                else:
                    residual(4, conv_done, l * 2)

            dve.wait_ge(x_in, 16)
            take_stats(x)
            layer0(0, True)
            with dve.Fori(1, LAYERS) as l:
                steps.enter(l - 1, 24)
                layer0(l, False)
            steps.leave(LAYERS - 1)

            layer_norm(LN_L0_LAST, h)
            dve.wait_ge(ln_out, LN_L0_LAST * 2 + 2)
            dve.wait_ge(gb_in, 32)
            for k, op in ((0, ALU.mult), (1, ALU.add)):
                for t in range(NT):
                    ins = dve.tensor_tensor(xn[:, t, :], xn[:, t, :], gb[:, k, :], op)
                link(ins)
            link(dve.tensor_tensor(x[:], x[:], xn[:], ALU.add))
            take_stats(x)
            layer_norm(LN_L1_IN, x)
            dve.wait_ge(ln_out, LN_L1_IN * 2 + 2)
            link(dve.tensor_scalar(h[:], xn[:], 0.0, None, ALU.max))
            take_stats(h)

            def cond_norm(k):
                variance(k + LN_BLOCK)
                for t in range(NT):
                    dve.wait_ge(tab_ready, k * 4 + (t + 1))
                    ins = dve.scalar_tensor_tensor(out=xn[:, t, :], in0=h[:, t, :], scalar=mv[:, t, 0:1],
                                                   in1=tab[:, 0, t, :], op0=ALU.subtract, op1=ALU.mult)
                link(ins)
                refine(k + LN_BLOCK)
                for t in range(NT):
                    dve.wait_ge(tab_ready, k * 4 + (t + 3))
                    dve.scalar_tensor_tensor(out=xn[:, t, :], in0=xn[:, t, :], scalar=rstd[:, t:t + 1],
                                             in1=tab[:, 1, t, :], op0=ALU.mult, op1=ALU.add).then_inc(y_ready, 1)

            with dve.Fori(0, BLOCKS) as b:
                steps.enter(b, 24)
                cond_norm(b * 2)
                dve.wait_ge(w_in[0], b * 32 + (LAYERS + 1) * 32)
                carry()
                add_bias(0, h)
                for hd in range(HEADS):
                    dve.wait_ge(k_done, b * 2 + (hd // 2 + 1))
                    dve.tensor_scalar(kT[:, hd, :], chunks(4)[:, hd, :], cols[:, bass.ds(b * CT + (COL["bk"] + hd), 1)],
                                      None, ALU.add).then_inc(k_ready, 1)
                for t in range(NT):
                    for hd in range(HEADS):
                        k = t * HEADS + hd
                        if hd % 2 == 0:
                            dve.wait_ge(sc_done, b * 4 + (2 * t + hd // 2 + 1))
                            carry()
                        ins = dve.tensor_tensor_reduce(out=prob[:, t, hd, :], in0=chunks(2 * t)[:, hd, :],
                                                       in1=mask[:, t, :], scale=float(DH) ** -0.5, scalar=-3e38,
                                                       op0=ALU.add, op1=ALU.max, accum_out=smax[:, k:k + 1])
                    link(ins)
                    four = slice(t * HEADS, (t + 1) * HEADS)
                    dve.tensor_scalar(nmax[:, four], smax[:, four], -1.0, None, ALU.mult).then_inc(smax_ready, 1)
                for t in range(NT):
                    four = slice(t * HEADS, (t + 1) * HEADS)
                    for hd in range(HEADS):
                        k = t * HEADS + hd
                        dve.wait_ge(exp_ready, b * 8 + (k + 1))
                        ins = dve.tensor_tensor_reduce(out=prob[:, t, hd, :], in0=prob[:, t, hd, :],
                                                       in1=cnt[:, t, :], scale=1.0, scalar=0.0,
                                                       op0=ALU.mult, op1=ALU.add, accum_out=den[:, k:k + 1])
                    link(ins)
                    link(dve.tensor_scalar(den[:, four], den[:, four], TINY, None, ALU.max))
                    link(dve.reciprocal(rden[:, four], den[:, four]))
                    for hd in range(HEADS):
                        k = t * HEADS + hd
                        dve.tensor_scalar(prob[:, t, hd, :], prob[:, t, hd, :], rden[:, k:k + 1], None,
                                          ALU.mult).then_inc(p_ready, 1)
                    if t == 0:
                        dve.wait_ge(w_in[5], b * 32 + 32)
                    dve.wait_ge(v_done, b * 2 + (t + 1))
                    dve.tensor_tensor(v[:, t, :], PS[:, t, :], bias_of(5), ALU.add).then_inc(v_ready, 1)
                for i in range(2):
                    dve.wait_ge(pT_done, b * 4 + (2 * i + 2))
                    dve.tensor_copy(probT[:, 1, 2 * i:2 * i + 2, :], chunks(6)[:, 2 * i:2 * i + 2, :]).then_inc(pT_dve, 1)
                dve.wait_ge(bias_added, b * 2 + (LAYERS + 1))
                residual(2, proj_done, b * 2)
                cond_norm(b * 2 + 1)
                dve.wait_ge(w_in[2], b * 32 + ((LAYERS - 1) * 16 + 32))
                carry()
                add_bias(2, h)
                dve.wait_ge(bias_added, b * 2 + (LAYERS + 2))
                residual(0, down_done, b * 2)
            steps.leave(BLOCKS)

            link(dve.tensor_tensor(x[:], x[:], h[:], ALU.add))
            take_stats(x)
            layer_norm(LN_L2, x)
            dve.wait_ge(ln_out, OUT_L2 * 2 + 2)
            dve.wait_ge(w_in[5], 32 * (BLOCKS + 1))
            add_bias(5, x)
            dve.wait_ge(bias_added, LAYERS + 2 * BLOCKS + 1)
            for t in range(NT):
                dve.wait_ge(alpha_done, t + 1)
                ins = dve.tensor_tensor(x[:, t, :], PS[:, 4 + t, :], x[:, t, :], ALU.add)
            link(ins)
            for t in range(NT):
                dve.wait_ge(gamma_done, t + 1)
                ins = dve.scalar_tensor_tensor(out=x[:, t, :], in0=PS[:, 6 + t, :], scalar=outrec[:, t:t + 1],
                                               in1=x[:, t, :], op0=ALU.mult, op1=ALU.add)
            link(ins)
            take_stats(x)
            layer_norm(LN_L3, x)
            dve.wait_ge(ln_out, OUT_L3 * 2 + 2)
            link(dve.tensor_scalar(h[:], xn[:], 0.0, None, ALU.max))
            dve.memset(PS[:, 0:NT, :], 0.0)
            link(dve.tensor_copy(hs[:, 0, :, :], h[:]))
            link(dve.tensor_tensor(h[:], h[:], hs[:, 0, :, :], ALU.subtract))
            link(dve.tensor_copy(hs[:, 1, :, :], h[:]))
            dve.tensor_tensor(hs[:, 2, :, :], h[:], hs[:, 1, :, :], ALU.subtract).then_inc(hs_ready, 1)

            regs = [[dve.alloc_register(f"path{u}_{k}") for k in range(4)] for u in range(RING)]
            for g in range(GROUPS):
                if g > 0:
                    dve.wait_ge(path_step, g * 2 * PATHS)
                dve.memset(part[SUM_AT[g]][:, TG // 2:TG, :], 0.0).then_inc(acc_zero, 1)
                dve.wait_ge(x2_in[g], 16)
                dve.wait_ge(x1_ready, min((g + 1) * TG, ET))
                dve.wait_ge(acc_zero, (g + 1) * 2)
                n = SIZES[g]
                xs, xe, sums = (part[at[g]][:, 0:n, :] for at in (SOURCE_AT, EDGE_AT, SUM_AT))

                def path_rows(row, lo, n_rows, slot):
                    at = [four for four in regs[0:n_rows]]
                    dve.load([r for four in at for r in four], path[0:1, bass.ds(row * 4, 4 * n_rows)])
                    for j in range(n_rows):
                        i1, i2, i3 = (dve.snap(r, min_val=0, max_val=(SEGS - 1) * EXT) for r in at[j][0:3])
                        if lo + j >= AHEAD:
                            dve.wait_ge(path_step, row * 2 + (g * 2 * PATHS + 2 * j + 1 - 2 * AHEAD))
                            o = sums[:, :, bass.ds(i3, EXT)]
                            dve.tensor_tensor(o, o, prod[:, (slot + j - AHEAD) % RING, 0:n, :], ALU.add).then_inc(path_step, 1)
                        if lo + j < PATHS:
                            dve.scalar_tensor_tensor(
                                out=prod[:, (slot + j) % RING, 0:n, :], in0=xs[:, :, bass.ds(i1, EXT)],
                                scalar=coef[:, bass.ds(row + j, 1)], in1=xe[:, :, bass.ds(i2, EXT)],
                                op0=ALU.mult, op1=ALU.mult).then_inc(path_step, 1)

                path_rows(0, 0, AHEAD, 0)
                with dve.Fori(0, PATHS // RING - 1) as q:
                    path_rows(q * RING + AHEAD, AHEAD, RING, AHEAD)
                last = PATHS - RING + AHEAD
                path_rows(last, last, RING, last % RING)
            for t in range(NT):
                dve.wait_ge(tile_summed, ET)
                dve.tensor_tensor(x[:, t, :], PS[:, t, :], x[:, t, :], ALU.add).then_inc(final, 1)


_OUTS = [((N, D), "float32")]


def kernel(**inputs):
    import numpy as _np
    import concourse.bacc as _bacc
    from concourse import mybir as _mybir
    from concourse.bass_utils import run_bass_kernel_spmd as _run

    nc = _bacc.Bacc("TRN2", target_bir_lowering=False, num_devices=1)
    arrays, args = {}, {}
    for name in inputs:
        a = _np.ascontiguousarray(inputs[name])
        arrays[f"in_{name}_dram"] = a
        args[name] = nc.dram_tensor(f"in_{name}_dram", a.shape, _mybir.dt.from_np(a.dtype), kind="ExternalInput").ap()
    shape, dtype = _OUTS[0]
    out = nc.dram_tensor("out_0_dram", shape, _mybir.dt.from_np(_np.dtype(dtype)), kind="ExternalOutput").ap()
    gnn_stack_kernel(nc, args, out)
    r = _run(nc, [arrays], core_ids=[0])
    return r.results[0]["out_0_dram"]
```

```python
from contextlib import ExitStack

import concourse.bass as bass
import concourse.mybir as mybir
import numpy as np

F32 = mybir.dt.float32
BF16 = mybir.dt.bfloat16
I32 = mybir.dt.int32
ALU = mybir.AluOpType
ACT = mybir.ActivationFunctionType
AX = mybir.AxisListType

P = 128
N = 256
NT = N // P
D = 512
CT = D // P
E = 8192
ET = E // P
LAYERS = 7
BLOCKS = 4
HEADS = 4
DH = D // HEADS
NF = 32
NC = 16
SEGS, EXT, PATHS = 16, 32, 64
GROUPS = 5
TG = -(-ET // GROUPS)
SIZES = [min(TG, ET - g * TG) for g in range(GROUPS)]
RING = 4
EDGE_AT = [0, 3, 0, 3, 0]
SOURCE_AT = [1, 4, 2, 1, 4]
SUM_AT = [2, 1, 4, 2, 1]
ZERO_CUT = (2, 7)
SRC_CUT = 4
HOT = 8
BY_ACT = 3

LN_EPS = 1e-5
MSG_EPS = 1e-7
AHEAD = 2
CONSTS = 17
MASKED = -1e30
TINY = 1e-30
DEN_SCALE = float(2.0 ** 40)
DEN_SHIFT = float(40 * np.log(2.0))
DEN_TINY = float(2.0 ** -60)
TWO_PI = 2 * np.pi
PI_A = 6.28125
PI_B = float(np.floor((TWO_PI - PI_A) * 2 ** 24) / 2 ** 24)
PI_C = float(TWO_PI - PI_A - PI_B)
ROUND = 12582912.0
PI_CLIP = 3.1415925

COL_A = [("norm_g", LAYERS), ("norm_b", LAYERS), ("vn_emb", 1), ("vn_g", LAYERS - 1), ("vn_beta", LAYERS - 1)]
COL_B = [("vn_b1", LAYERS - 1), ("vn_b2", LAYERS - 1), ("bq", BLOCKS), ("bk", BLOCKS), ("m_b1", BLOCKS)]


def column_table():
    at, col = {}, 0
    for name, n in COL_A + COL_B:
        at[name] = col
        col += CT * n
    return at, CT * sum(n for _, n in COL_A), CT * sum(n for _, n in COL_B)


LN_L0_LAST, LN_L1_IN, LN_BLOCK, LN_L2, LN_L3 = 7, 8, 9, 17, 18
OUT_L2, OUT_L3 = LN_L1_IN + 1, LN_L1_IN + 2
TR_BLOCK, TR_L2 = 7, 15
W1_BANKS, W2_BANKS = (2, 3, 6, 7), (4, 5, 6, 7)


class Steps:

    def __init__(self, eng, sem):
        self.eng, self.sem, self.base, self.n = eng, sem, 0, 0

    def link(self, ins):
        self.mark(ins)
        self.await_marked()

    def mark(self, ins):
        self.n += 1
        ins.then_inc(self.sem, 1)

    def await_marked(self):
        self.eng.wait_ge(self.sem, self.base + self.n)

    def enter(self, it, per):
        self.outer, self.start, self.per = self.base, self.base + self.n, per
        self.base, self.n = it * per + self.start, 0

    def leave(self, times):
        assert self.n == self.per, self.n
        self.base, self.n = self.start, self.per * times


def gnn_stack_kernel(nc, A, out):
    COL, NCOL_A, NCOL_B = column_table()
    ctx = ExitStack()
    with ctx:
        def sb(name, shape, dt=F32):
            return ctx.enter_context(nc.sbuf_tensor(name, shape, dt))

        def sem(name):
            return ctx.enter_context(nc.semaphore(name))

        PS = ctx.enter_context(nc.psum_tensor("PS", [P, 8, 512], F32))

        def chunks(bank):
            return PS[:, bank:bank + 2, :].rearrange("p b (c n) -> p (b c) n", n=N)

        GW = TG * D
        big = sb("big", [P, 5 * GW])
        part = [big[:, i * GW:(i + 1) * GW].rearrange("p (j d) -> p j d", j=TG) for i in range(5)]
        assert 6 * CT * D <= 2 * GW and 10 * 1024 <= 2 * GW
        W = big[:, GW:GW + 6 * CT * D]
        wbuf = [W[:, i * CT * D:(i + 1) * CT * D].rearrange("p (c n) -> p c n", c=CT) for i in range(6)]
        R = big[:, 3 * GW:3 * GW + 10 * 1024]

        spare = big[:, 3 * GW + 10 * 1024:5 * GW]

        def region(k, n=1):
            return R[:, 1024 * k:1024 * (k + n)]

        def as_c(ap):
            return ap.rearrange("p (c n) -> p c n", c=CT)

        def as_t(ap):
            return ap.rearrange("p (t n) -> p t n", t=NT)

        x = sb("x", [P, NT, D])
        h = sb("h", [P, NT, D])
        xn = sb("xn", [P, NT, D])
        hT = sb("hT", [P, CT, N])
        hv = as_c(region(0))
        m = as_c(region(1))
        md = as_c(region(2))
        ex = as_t(region(3))
        mex = as_t(region(4))
        rec = as_c(region(5))
        z = as_c(region(6))
        gb = region(8, 2).rearrange("p (k n) -> p k n", k=4)
        qT = as_c(region(0))
        kT = as_c(region(1))
        v = as_t(region(2))
        prob = region(3, 2).rearrange("p (t h n) -> p t h n", t=NT, h=HEADS)
        probT = region(5, 2).rearrange("p (t h n) -> p t h n", t=NT, h=HEADS)
        oT = as_c(region(7))
        mT = as_c(region(0))
        tab = region(8, 2).rearrange("p (k t n) -> p k t n", k=2, t=NT)
        CUT = E // SRC_CUT
        src_all = big[:, 0:3 * CUT].bitcast(I32)
        assert 3 * CUT <= GW
        srcT = sb("srcT", [P, NT, E], BF16)
        tail = sb("tail", [P, 8 * D])
        brow = tail[:, 0:4 * D]
        tabw = tail[0:NC + 1, 4 * D:8 * D].rearrange("q (i k d) -> q i k d", i=2, k=2)
        prod = tail[:, 0:RING * TG * EXT].rearrange("p (r j u) -> p r j u", r=RING, u=EXT)
        hs = tail[:, 4 * D:7 * D].bitcast(BF16).rearrange("p (k t d) -> p k t d", k=3, t=NT)
        assert RING * TG * EXT <= 4 * D
        hotd = xn[:, :, :].rearrange("p t (i n) -> p (t i) n", n=N)
        src_i, dst_i = (region(2)[:, i * ET:(i + 1) * ET].bitcast(I32) for i in range(2))
        src_f, src_n = (region(2)[:, i * ET:(i + 1) * ET] for i in (2, 3))
        dst_f = sb("dst_f", [P, ET])
        dst_n = sb("dst_n", [P, ET])
        iota_f = sb("iota_f", [P, N])
        iota_b = sb("iota_b", [P, N], BF16)
        iota_p = sb("iota_p", [P, NT])
        hot_s = region(0).bitcast(BF16).rearrange("p (k n) -> p k n", k=HOT)
        hot_d = region(1).bitcast(BF16).rearrange("p (k n) -> p k n", k=HOT)
        cnt = sb("cnt", [P, NT, N])
        cntT = sb("cntT", [P, NT, N])
        mask = sb("mask", [P, NT, N])
        outdeg = sb("outdeg", [P, NT])
        outrec = sb("outrec", [P, NT])
        ident = sb("ident", [P, P])
        ones = sb("ones", [P, P])
        par_a = xn[0:NCOL_A, 0, 0:P]
        par_b = xn[0:NCOL_B, 1, 0:P]
        cols = sb("cols", [P, NCOL_A + NCOL_B])
        consts = sb("consts", [P, 5])
        zero, ln_tiny, den_shift, one, ln_eps = (consts[:, i:i + 1] for i in range(5))
        idle = sb("idle", [1, 40])
        st = sb("st", [P, NT, 6])
        mv = sb("mv", [P, NT, 2])
        var = sb("var", [P, NT])
        lnv = sb("lnv", [P, NT])
        est = sb("est", [P, NT])
        nwt = sb("nwt", [P, NT])
        rstd = sb("rstd", [P, NT])
        hsum = sb("hsum", [P, CT])
        vn = sb("vn", [P, CT])
        vtmp = sb("vtmp", [P, CT])
        vhid = sb("vhid", [P, CT])
        vcen = sb("vcen", [P, CT])
        vsq = sb("vsq", [P, CT])
        vsum = sb("vsum", [P, 2])
        vvar = sb("vvar", [P, 4])
        scrap = region(1, 2).rearrange("p (o d) -> p o d", o=CT)
        w1T, w2T = wbuf[3], wbuf[4]
        hmax = sb("hmax", [P, CT])
        vne = sb("vne", [P, CT])
        mmax = sb("mmax", [P, CT])
        smax = sb("smax", [P, NT * HEADS])
        nmax = sb("nmax", [P, NT * HEADS])
        den = sb("den", [P, NT * HEADS])
        rden = sb("rden", [P, NT * HEADS])
        emb = region(7)[0:2 * NF, 0:N]
        turns = region(7)[0:2 * NF, N:2 * N]
        turn_part = region(7)[0:2 * NF, 2 * N:3 * N]
        freq = sb("freq", [2 * NF, 4])
        freq_i = sb("freq_i", [2 * NF, 1], I32)
        fw1 = sb("fw1", [2 * NF, NC])
        fw2 = sb("fw2", [NC, NC])
        fb = sb("fb", [NC, 2])
        cz = region(7)[0:NC, 2 * N:3 * N]
        ce = region(7)[0:NC, 3 * N:4 * N]
        condT = spare[0:NC + 1, 0:N]
        path = sb("path", [1, (PATHS + AHEAD) * 4], I32)
        path_raw = sb("path_raw", [1, PATHS * 3], I32)
        coef = sb("coef", [P, PATHS])

        src_in = [sem(f"src_in{c}") for c in range(SRC_CUT)]
        x_in, edges_in, par_in, gb_in = map(sem, ["x_in", "edges_in", "par_in", "gb_in"])
        noise_in, path_in, path_clear = map(sem, ["noise_in", "path_in", "path_clear"])
        w_in = [sem(f"w_in{i}") for i in range(6)]
        tabw_in = [sem(f"tabw_in{i}") for i in range(2)]
        x2_in = [sem(f"x2_in{g}") for g in range(GROUPS)]
        out_done = sem("out_done")
        zeroed, consts_set, edges_f, hot_ready, src_squared, src_hot, hot_used, cnt_set, cntT_done = map(
            sem, ["zeroed", "consts_set", "edges_f", "hot_ready", "src_squared", "src_hot", "hot_used", "cnt_set",
                  "cntT_done"])
        par_turned, cols_set, srcT_set = map(sem, ["par_turned", "cols_set", "srcT_set"])
        angle_set, emb_set, cond_a, cond_z, cond_e, cond_s, cond_b, cond_set = map(
            sem, ["angle_set", "emb_set", "cond_a", "cond_z", "cond_e", "cond_s", "cond_b", "cond_set"])
        ln_var, ln_est, ln_out, tr_done = map(sem, ["ln_var", "ln_est", "ln_out", "tr_done"])
        bias_added = sem("bias_added")
        dve_step, act_step, pool_step = sem("dve_step"), sem("act_step"), sem("pool_step")
        w1_turned, w1T_set, w2_turned, w2T_set = map(sem, ["w1_turned", "w1T_set", "w2_turned", "w2T_set"])
        hT_ready, vn_in, vn_spread, vn_sum, vn_mean, vn_squares, vn_total, vn_var, vn_est, vn_act, vn_act_spread = map(
            sem, ["hT_ready", "vn_in", "vn_spread", "vn_sum", "vn_mean", "vn_squares", "vn_total", "vn_var", "vn_est", "vn_act",
                  "vn_act_spread"])
        m_ready, md_ready, mT_done, mdT_done, ex_ready, mex_ready, den_done, num_done, rec_est, z_ready, conv_done = map(
            sem, ["m_ready", "md_ready", "mT_done", "mdT_done", "ex_ready", "mex_ready", "den_done", "num_done",
                  "rec_est", "z_ready", "conv_done"])
        tab_done, tab_ready, y_ready, yT_ready, q_done, k_done, v_done, q_ready, k_ready, v_ready = map(
            sem, ["tab_done", "tab_ready", "y_ready", "yT_ready", "q_done", "k_done", "v_done", "q_ready", "k_ready",
                  "v_ready"])
        sc_done, smax_ready, exp_ready, p_ready, pT_done, pT_act, pT_dve, o_done, o_ready, proj_done = map(
            sem, ["sc_done", "smax_ready", "exp_ready", "p_ready", "pT_done", "pT_act", "pT_dve", "o_done", "o_ready",
                  "proj_done"])
        up_done, up_ready, down_done = map(sem, ["up_done", "up_ready", "down_done"])
        beta_done, beta_ready, alpha_done, gamma_done = map(sem, ["beta_done", "beta_ready", "alpha_done", "gamma_done"])
        hs_ready, hot_squared, hotd_ready, acc_zero, x1_done, x1_ready, path_step, tile_summed, final = map(
            sem, ["hs_ready", "hot_squared", "hotd_ready", "acc_zero", "x1_done", "x1_ready", "path_step",
                  "tile_summed", "final"])

        block = ctx.enter_context(nc.Block())

        def halves(bank):
            return PS[:, bank, :].rearrange("p (t d) -> p t d", t=NT)

        def bias_of(i):
            k = min(i, 3)
            return brow[:, k * D:(k + 1) * D]

        def rows(ap):
            return ap.rearrange("(c p) n -> p c n", p=P)

        def one_row(ap):
            return ap.rearrange("(a n) -> a n", a=1)

        def nodes(ap):
            return ap.rearrange("(t p) d -> p t d", p=P)

        @block.sync
        def _(sp):
            def load_w(i, weight, bias):
                sp.dma_start(wbuf[i], rows(weight)).then_inc(w_in[i], 16)
                if bias is not None:
                    sp.dma_start(bias_of(i), spread(one_row(bias))).then_inc(w_in[i], 16)

            def spread(row):
                return row.to_broadcast([P, D])

            def load_tab(i, b):
                ws, bs, wb, bb = [("s1_w", "s1_b", "b1_w", "b1_b"), ("s2_w", "s2_b", "b2_w", "b2_b")][i]
                sp.dma_start(tabw[0:NC, i, 0, :], A["L1_gnn_" + ws][b, :, :]).then_inc(tabw_in[i], 16)
                sp.dma_start(tabw[0:NC, i, 1, :], A["L1_gnn_" + wb][b, :, :]).then_inc(tabw_in[i], 16)
                sp.dma_start(tabw[NC:NC + 1, i, 0, :], A["L1_gnn_" + bs][bass.ds(b, 1), :]).then_inc(tabw_in[i], 16)
                sp.dma_start(tabw[NC:NC + 1, i, 1, :], A["L1_gnn_" + bb][bass.ds(b, 1), :]).then_inc(tabw_in[i], 16)

            sp.dma_start(src_i[:], A["src"].rearrange("(p t) -> p t", t=ET)).then_inc(edges_in, 16)
            sp.dma_start(dst_i[:], A["dst"].rearrange("(p t) -> p t", t=ET)).then_inc(edges_in, 16)
            sp.dma_start(emb, A["node_vec1"].rearrange("n a -> a n").to_broadcast([2 * NF, N])).then_inc(noise_in, 16)
            sp.dma_start(fw1[:], A["L1_gnn_f_w1"]).then_inc(noise_in, 16)
            sp.dma_start(fw2[:], A["L1_gnn_f_w2"]).then_inc(noise_in, 16)
            sp.dma_start(fb[:, 0:1], A["L1_gnn_f_b1"].rearrange("(n a) -> n a", a=1)).then_inc(noise_in, 16)
            sp.dma_start(fb[:, 1:2], A["L1_gnn_f_b2"].rearrange("(n a) -> n a", a=1)).then_inc(noise_in, 16)
            sp.dma_start(x[:], nodes(A["x"])).then_inc(x_in, 16)
            for tile, names in ((par_a, COL_A), (par_b, COL_B)):
                r = 0
                for name, n in names:
                    full = ("L1_gnn_" if name in ("bq", "bk", "m_b1") else "L0_gnn_") + name
                    a = A[full]
                    a = a.rearrange("(c p) -> c p", p=P) if n == 1 else a.rearrange("l (c p) -> (l c) p", p=P)
                    sp.dma_start(tile[r:r + CT * n, :], a).then_inc(par_in, 16)
                    r += CT * n
            sp.dma_start(path_raw[:], A["L3_gnn_path_indices"].rearrange("(a k) c -> a (k c)", a=1)).then_inc(path_in, 16)
            sp.dma_start(coef[:], one_row(A["L3_gnn_path_coeffs"]).to_broadcast([P, PATHS])).then_inc(path_in, 16)
            load_w(0, A["L0_gnn_gcn_W"][0], A["L0_gnn_gcn_b"][0])
            load_w(1, A["L0_gnn_vn_W1"][0], None)
            load_w(2, A["L0_gnn_vn_W2"][0], None)
            def load_src(c):
                sp.dma_start(src_all[:, (c % 3) * CUT:(c % 3 + 1) * CUT],
                             one_row(A["src"])[:, c * CUT:(c + 1) * CUT].to_broadcast([P, CUT])).then_inc(src_in[c], 16)

            for c in range(3):
                load_src(c)
            for k, name in enumerate(("norm_g", "norm_b")):
                sp.dma_start(gb[:, k, :], A["L0_gnn_" + name][LAYERS - 1:LAYERS, :].to_broadcast([P, D])).then_inc(gb_in, 16)
            load_w(5, A["L1_gnn_wv"][0], A["L1_gnn_bv"][0])

            load_tab(0, 0)
            load_tab(1, 0)
            sp.wait_ge(srcT_set, NT)
            load_src(3)

            def edge_group(g):
                rows_of = A["edge_attr_512"].rearrange("(p t) d -> p t d", t=ET)
                sp.dma_start(part[EDGE_AT[g]][:, 0:SIZES[g], :], rows_of[:, g * TG:g * TG + SIZES[g], :]).then_inc(x2_in[g], 16)

            def conv_weights(l):
                sp.wait_ge(conv_done, l * 2)
                sp.wait_ge(bias_added, l)
                sp.dma_start(wbuf[0], rows(A["L0_gnn_gcn_W"][bass.ds(l, 1)].rearrange("a k n -> (a k) n"))).then_inc(w_in[0], 16)
                sp.dma_start(bias_of(0), spread(A["L0_gnn_gcn_b"][bass.ds(l, 1), :])).then_inc(w_in[0], 16)

            with sp.Fori(1, LAYERS - 1) as l:
                conv_weights(l)
                sp.wait_ge(w1_turned, l * CT)
                sp.dma_start(wbuf[1], rows(A["L0_gnn_vn_W1"][bass.ds(l, 1)].rearrange("a k n -> (a k) n"))).then_inc(w_in[1], 16)
                sp.wait_ge(w2_turned, l * CT)
                sp.dma_start(wbuf[2], rows(A["L0_gnn_vn_W2"][bass.ds(l, 1)].rearrange("a k n -> (a k) n"))).then_inc(w_in[2], 16)
            conv_weights(LAYERS - 1)
            sp.wait_ge(srcT_set, SRC_CUT * NT)
            edge_group(0)

            sp.wait_ge(w1_turned, (LAYERS - 1) * CT)
            load_w(1, A["L1_gnn_m_w1"][0], None)
            sp.wait_ge(w2_turned, (LAYERS - 1) * CT)
            load_w(2, A["L1_gnn_m_w2"][0], A["L1_gnn_m_b2"][0])
            sp.wait_ge(vn_sum, LAYERS - 1)
            load_w(3, A["L1_gnn_wq"][0], None)
            sp.wait_ge(m_ready, 2 * LAYERS)
            load_w(4, A["L1_gnn_wk"][0], None)
            sp.wait_ge(conv_done, 2 * LAYERS)
            sp.wait_ge(bias_added, LAYERS)
            load_w(0, A["L1_gnn_wo"][0], A["L1_gnn_bo"][0])

            def w_at(name, b):
                return rows(A["L1_gnn_" + name][bass.ds(b, 1)].rearrange("a k n -> (a k) n"))

            with sp.Fori(0, BLOCKS - 1) as b:
                sp.wait_ge(tab_done, b * 8 + 4)
                load_tab(0, b + 1)
                sp.wait_ge(q_done, b * 2 + 2)
                sp.dma_start(wbuf[3], w_at("wq", b + 1)).then_inc(w_in[3], 16)
                sp.wait_ge(k_done, b * 2 + 2)
                sp.dma_start(wbuf[4], w_at("wk", b + 1)).then_inc(w_in[4], 16)
                sp.wait_ge(v_done, b * 2 + 2)
                sp.dma_start(wbuf[5], w_at("wv", b + 1)).then_inc(w_in[5], 16)
                sp.wait_ge(v_ready, b * 2 + 2)
                sp.dma_start(bias_of(5), spread(A["L1_gnn_bv"][bass.ds(b + 1, 1), :])).then_inc(w_in[5], 16)
                sp.wait_ge(tab_done, b * 8 + 8)
                load_tab(1, b + 1)
                sp.wait_ge(proj_done, b * 2 + 2)
                sp.dma_start(wbuf[0], w_at("wo", b + 1)).then_inc(w_in[0], 16)
                sp.wait_ge(bias_added, b * 2 + (LAYERS + 1))
                sp.dma_start(bias_of(0), spread(A["L1_gnn_bo"][bass.ds(b + 1, 1), :])).then_inc(w_in[0], 16)
                sp.wait_ge(up_done, b * 2 + 2)
                sp.dma_start(wbuf[1], w_at("m_w1", b + 1)).then_inc(w_in[1], 16)
                sp.wait_ge(down_done, b * 2 + 2)
                sp.dma_start(wbuf[2], w_at("m_w2", b + 1)).then_inc(w_in[2], 16)
                sp.wait_ge(bias_added, b * 2 + (LAYERS + 2))
                sp.dma_start(bias_of(2), spread(A["L1_gnn_m_b2"][bass.ds(b + 1, 1), :])).then_inc(w_in[2], 16)
            sp.wait_ge(q_done, 2 * BLOCKS)
            load_w(3, A["L2_gnn_wn"], None)
            sp.wait_ge(v_done, 2 * BLOCKS)
            sp.wait_ge(v_ready, 2 * BLOCKS)
            load_w(5, A["L2_gnn_wc"], A["L2_gnn_bias"])

            sp.wait_ge(hs_ready, 3)
            edge_group(1)
            for g in range(2, GROUPS):
                sp.wait_ge(path_step, (g - 1) * 2 * PATHS)
                edge_group(g)
            sp.wait_ge(final, 1)
            sp.dma_start(nodes(out)[:, 0, :], x[:, 0, :]).then_inc(out_done, 16)
            sp.wait_ge(final, 2)
            sp.dma_start(nodes(out)[:, 1, :], x[:, 1, :]).then_inc(out_done, 16)
            sp.wait_ge(out_done, 32)

        @block.gpsimd
        def _(pool):
            pool.memset(ident[:], 0.0).then_inc(zeroed, 1)
            pool.memset(ones[:], 1.0).then_inc(consts_set, 1)
            pool.memset(consts[:, 0:1], 0.0).then_inc(consts_set, 1)
            pool.memset(consts[:, 1:2], DEN_TINY).then_inc(consts_set, 1)
            pool.memset(consts[:, 2:3], DEN_SHIFT).then_inc(consts_set, 1)
            pool.memset(one, 1.0).then_inc(consts_set, 1)
            pool.memset(ln_eps, LN_EPS).then_inc(consts_set, 1)
            pool.memset(condT[:], 1.0).then_inc(consts_set, 1)
            pool.iota(iota_f[:], pattern=[[1, N]], base=0, channel_multiplier=0,
                      allow_small_or_imprecise_dtypes=True).then_inc(consts_set, 1)
            pool.iota(iota_b[:], pattern=[[1, N]], base=0, channel_multiplier=0,
                      allow_small_or_imprecise_dtypes=True).then_inc(consts_set, 1)
            pool.iota(iota_p[:], pattern=[[P, NT]], base=0, channel_multiplier=1,
                      allow_small_or_imprecise_dtypes=True).then_inc(consts_set, 1)
            for k in range(2):
                half = slice(NF * k, NF * (k + 1))
                pool.wait_ge(consts_set, 10 + 3 * k)
                pool.iota(freq_i[half, :], pattern=[[0, 1]], base=1, channel_multiplier=1).then_inc(consts_set, 1)
                pool.memset(freq[half, 1:2], 0.25 * k).then_inc(consts_set, 1)
                pool.memset(freq[half, 2:3], float(np.pi / 2) * k).then_inc(consts_set, 1)
            pool.wait_ge(zeroed, 1)
            pool.wait_ge(consts_set, CONSTS - 1)
            pool.affine_select(out=ident[:], in_=ident[:], compare_op=ALU.not_equal, fill=1.0, base=0,
                               pattern=[[-1, P]], channel_multiplier=1).then_inc(consts_set, 1)
            steps = Steps(pool, pool_step)
            link = steps.link
            pool.wait_ge(consts_set, CONSTS)
            pool.wait_ge(noise_in, 16 * 5)
            link(pool.tensor_scalar(freq[:, 0:1], freq_i[:], float(np.float32(TWO_PI / 16)), None, ALU.mult))
            link(pool.tensor_scalar(emb, emb, freq[:, 0:1], None, ALU.mult))
            link(pool.tensor_scalar(turns, emb, float(1 / TWO_PI), freq[:, 1:2], ALU.mult, ALU.add))
            link(pool.tensor_scalar(turns, turns, ROUND, None, ALU.add))
            link(pool.tensor_scalar(turns, turns, -ROUND, None, ALU.add))
            for third in (PI_A, PI_B, PI_C):
                link(pool.tensor_scalar(turn_part, turns, third, None, ALU.mult))
                link(pool.tensor_tensor(emb, emb, turn_part, ALU.subtract))
            link(pool.tensor_scalar(turns, emb, freq[:, 2:3], PI_CLIP, ALU.add, ALU.min))
            pool.tensor_scalar(turns, turns, -PI_CLIP, None, ALU.max).then_inc(angle_set, 1)
            pool.wait_ge(consts_set, CONSTS)
            for c in range(SRC_CUT):
                pool.wait_ge(src_in[c], 16)
                q = P // SRC_CUT
                by_tile = src_all[:, (c % 3) * CUT:(c % 3 + 1) * CUT].rearrange("s (p t) -> s t p", t=ET)
                for s in range(NT):
                    pool.tensor_scalar(srcT[:, s, :].rearrange("s (t p) -> s t p", p=P)[:, :, c * q:(c + 1) * q],
                                       by_tile, iota_p[:, s:s + 1], None, ALU.is_equal).then_inc(srcT_set, 1)

            pool.wait_ge(alpha_done, 2)
            pool.wait_ge(beta_done, 2)
            for g in range(GROUPS):
                if g > 0:
                    pool.wait_ge(path_step, g * 2 * PATHS)
                pool.memset(part[SUM_AT[g]][:, ZERO_CUT[1]:TG, :], 0.0).then_inc(acc_zero, 1)

        @block.scalar
        def _(act):
            steps = Steps(act, act_step)

            def rsqrt_estimate(n):
                act.wait_ge(ln_var, n + 1)
                steps.link(act.activation(lnv[:], mv[:, :, 1], ACT.Ln, bias=ln_eps))
                act.activation(est[:], lnv[:], ACT.Exp, bias=zero, scale=-0.5).then_inc(ln_est, 1)

            def turned(tr):
                for b in range(2):
                    act.wait_ge(tr_done, tr * 2 + (b + 1))
                    yield b

            def hot_turn(i, first):
                for k in range(HOT - BY_ACT, HOT):
                    if not first:
                        act.wait_ge(hot_used, i * HOT + (k + 1 - HOT))
                    act.activation(hot_s[:, k, :], iota_f[:], ACT.Square,
                                   bias=src_n[:, bass.ds(i * HOT + k, 1)]).then_inc(src_squared, 1)
                for k in range(HOT - BY_ACT, HOT):
                    n = k + 1 - (HOT - BY_ACT)
                    act.wait_ge(src_squared, i * BY_ACT + n)
                    act.activation(hot_s[:, k, :], hot_s[:, k, :], ACT.Relu, bias=one, scale=-1.0).then_inc(src_hot, 1)

            act.preload_act_table_set("natural_log_exp_and_others")
            act.wait_ge(consts_set, CONSTS)
            act.wait_ge(edges_f, 5)
            hot_turn(0, True)
            with act.Fori(1, ET // HOT) as i:
                hot_turn(i, False)
            act.wait_ge(angle_set, 1)
            act.activation(emb, turns, ACT.Sin, bias=zero[0:2 * NF, :]).then_inc(emb_set, 1)
            act.preload_act_table_set("natural_log_exp_and_others")
            act.wait_ge(cond_z, 1)
            act.activation(ce, cz, ACT.Exp, bias=zero[0:NC, :], scale=-1.0).then_inc(cond_e, 1)

            def turned_weights(l, wT, banks, turned_w, wT_set, outs):
                for o in outs:
                    act.wait_ge(turned_w, l * CT + (o + 1 - CT))
                    act.activation(wT[:, o, :], PS[:, banks[o], :], ACT.Copy).then_inc(wT_set, 1)

            def layer0(l, first):
                if not first:
                    turned_weights(l, w1T, W1_BANKS, w1_turned, w1T_set, (0, 1))
                rsqrt_estimate(l)
                if not first:
                    turned_weights(l, w1T, W1_BANKS, w1_turned, w1T_set, (2, 3))
                for b in turned(l):
                    for c in (2 * b, 2 * b + 1):
                        if first:
                            act.activation(hT[:, c, :], chunks(0)[:, c, :], ACT.Relu, bias=zero).then_inc(hT_ready, 1)
                        else:
                            act.activation(hT[:, c, :], chunks(0)[:, c, :], ACT.Relu,
                                           bias=cols[:, bass.ds(l * CT + (COL["norm_b"] - CT + c), 1)],
                                           scale=cols[:, bass.ds(l * CT + (COL["norm_g"] - CT + c), 1)],
                                           accum_out=hsum[:, c:c + 1]).then_inc(hT_ready, 1)
                if not first:
                    turned_weights(l, w2T, W2_BANKS, w2_turned, w2T_set, range(CT))
                    act.wait_ge(vn_var, l)
                    steps.link(act.activation(vvar[:, 1:2], vvar[:, 0:1], ACT.Ln, bias=zero))
                    act.activation(vvar[:, 2:3], vvar[:, 1:2], ACT.Exp, bias=zero, scale=-0.5).then_inc(vn_est, 1)
                for b in range(2):
                    act.wait_ge(mdT_done, l * 2 + (b + 1))
                    act.activation(ex[:, :, b * N:(b + 1) * N], halves(6 + b), ACT.Exp, bias=zero).then_inc(ex_ready, 1)
                for b in range(2):
                    act.wait_ge(den_done, l * 2 + (b + 1))
                    steps.link(act.activation(rec[:, 2 * b:2 * b + 2, :], chunks(0)[:, 2 * b:2 * b + 2, :], ACT.Ln,
                                              bias=ln_tiny, scale=DEN_SCALE))
                    act.activation(rec[:, 2 * b:2 * b + 2, :], rec[:, 2 * b:2 * b + 2, :], ACT.Exp, bias=den_shift,
                                   scale=-1.0).then_inc(rec_est, 1)

            act.wait_ge(cols_set, 2)
            layer0(0, True)
            act.wait_ge(cond_b, 1)
            act.activation(condT[0:NC, :], PS[0:NC, 7, 0:N], ACT.Identity, bias=fb[:, 1:2]).then_inc(cond_set, 1)
            with act.Fori(1, LAYERS) as l:
                steps.enter(l - 1, 4)
                layer0(l, False)
            steps.leave(LAYERS - 1)
            rsqrt_estimate(LN_L0_LAST)
            rsqrt_estimate(LN_L1_IN)

            def table(k, part):
                for t in range(NT):
                    act.wait_ge(tab_done, k * 4 + (2 * part + t + 1))
                    act.activation(tab[:, part, t, :], PS[:, 4 + 2 * part + t, :], ACT.Identity,
                                   bias=zero if part else one).then_inc(tab_ready, 1)

            def y_turned(k):
                for b in turned(k + TR_BLOCK):
                    act.activation(hT[:, 2 * b:2 * b + 2, :], chunks(0)[:, 2 * b:2 * b + 2, :], ACT.Copy).then_inc(yT_ready, 1)

            with act.Fori(0, BLOCKS) as b:
                steps.enter(b, 2)
                table(b * 2, 0)
                rsqrt_estimate(b * 2 + LN_BLOCK)
                table(b * 2, 1)
                y_turned(b * 2)
                for hd in range(HEADS):
                    act.wait_ge(q_done, b * 2 + (hd // 2 + 1))
                    act.activation(qT[:, hd, :], chunks(2)[:, hd, :], ACT.Identity,
                                   bias=cols[:, bass.ds(b * CT + (COL["bq"] + hd), 1)]).then_inc(q_ready, 1)
                for t in range(NT):
                    act.wait_ge(smax_ready, b * 2 + (t + 1))
                    for hd in range(HEADS):
                        k = t * HEADS + hd
                        act.activation(prob[:, t, hd, :], prob[:, t, hd, :], ACT.Exp,
                                       bias=nmax[:, k:k + 1]).then_inc(exp_ready, 1)
                for i in range(2):
                    act.wait_ge(pT_done, b * 4 + (2 * i + 1))
                    act.activation(probT[:, 0, 2 * i:2 * i + 2, :], chunks(4)[:, 2 * i:2 * i + 2, :],
                                   ACT.Copy).then_inc(pT_act, 1)
                for i in range(2):
                    act.wait_ge(o_done, b * 2 + (i + 1))
                    act.activation(oT[:, 2 * i:2 * i + 2, :], chunks(0)[:, 2 * i:2 * i + 2, :], ACT.Copy).then_inc(o_ready, 1)
                table(b * 2 + 1, 0)
                rsqrt_estimate(b * 2 + (LN_BLOCK + 1))
                table(b * 2 + 1, 1)
                y_turned(b * 2 + 1)
                for c in range(CT):
                    act.wait_ge(up_done, b * 2 + (c // 2 + 1))
                    act.activation(mT[:, c, :], chunks(2)[:, c, :], ACT.Relu,
                                   bias=cols[:, bass.ds(b * CT + (COL["m_b1"] + c), 1)]).then_inc(up_ready, 1)
            steps.leave(BLOCKS)

            rsqrt_estimate(LN_L2)
            for b in turned(TR_L2):
                act.activation(hT[:, 2 * b:2 * b + 2, :], chunks(0)[:, 2 * b:2 * b + 2, :], ACT.Relu, bias=zero).then_inc(yT_ready, 1)
            for t in range(NT):
                act.wait_ge(beta_done, t + 1)
                act.activation(v[:, t, :], PS[:, 2 + t, :], ACT.Copy).then_inc(beta_ready, 1)
            rsqrt_estimate(LN_L3)

            def x1_tile(g, j, u):
                act.wait_ge(x1_done, j + (g * TG + 1))
                act.activation(part[SOURCE_AT[g]][:, bass.ds(j, 1), :].rearrange("p a d -> p (a d)"),
                               PS[:, 2 + u, :], ACT.Copy).then_inc(x1_ready, 1)

            def x1_group(g):
                with act.Fori(0, SIZES[g] // RING) as q:
                    for u in range(RING):
                        x1_tile(g, q * RING + u, (g * TG + u) % RING)
                for j in range(SIZES[g] // RING * RING, SIZES[g]):
                    x1_tile(g, j, (g * TG + j) % RING)

            def hot(tile, u, count):
                act.activation(hotd[:, u, :], iota_f[:], ACT.Square, bias=dst_n[:, bass.ds(tile, 1)]).then_inc(hot_squared, 1)
                act.wait_ge(hot_squared, count)
                act.activation(hotd[:, u, :], hotd[:, u, :], ACT.Relu, bias=one, scale=-1.0).then_inc(hotd_ready, 1)

            def zero_sums(g):
                cut = part[SUM_AT[g]][:, ZERO_CUT[0]:ZERO_CUT[1], :].rearrange("p j d -> p (j d)")
                act.activation(cut, zero.to_broadcast([P, (ZERO_CUT[1] - ZERO_CUT[0]) * D]), ACT.Copy).then_inc(acc_zero, 1)

            act.wait_ge(hs_ready, 3)
            zero_sums(0)
            x1_group(0)
            x1_group(1)
            for u in range(RING):
                hot(u, u, u + 1)
            done = 1
            for g in range(GROUPS):
                if g + 1 < GROUPS:
                    act.wait_ge(path_step, (g + 1) * 2 * PATHS)
                    zero_sums(g + 1)
                upto = ((g + 1) * TG - 1) // RING + 1 if g < GROUPS - 1 else ET // RING
                with act.Fori(done, upto) as q:
                    for u in range(RING):
                        act.wait_ge(tile_summed, q * RING + (u + 1 - RING))
                        hot(q * RING + u, u, q * RING + (u + 1))
                done = upto
                if g + 2 < GROUPS:
                    act.wait_ge(tile_summed, (g + 1) * TG)
                    x1_group(g + 2)

        @block.tensor
        def _(pe):
            def mm(o, lhsT, rhs, start, stop):
                return pe.matmul(o, lhsT, rhs, start=start, stop=stop)

            with pe.Fori(0, ET // HOT) as i:
                for k in range(HOT):
                    pe.wait_ge(hot_ready, i * (2 * HOT - BY_ACT) + (k + 1 + min(k + 1, HOT - BY_ACT)))
                    if k >= HOT - BY_ACT:
                        pe.wait_ge(src_hot, i * BY_ACT + (k + 1 - (HOT - BY_ACT)))
                    for s in range(NT):
                        ins = pe.matmul(PS[:, 2 + s, 0:N], hot_s[:, k, s * P:(s + 1) * P], hot_d[:, k, :],
                                        start=False, stop=True, skip_group_check=True)
                    ins.then_inc(hot_used, 1)
            pe.wait_ge(consts_set, CONSTS)
            pe.wait_ge(par_in, 16 * (len(COL_A) + len(COL_B)))
            pe.transpose(PS[:, 0, 0:NCOL_A], par_a, ident[0:NCOL_A, 0:NCOL_A]).then_inc(par_turned, 1)
            pe.transpose(PS[:, 1, 0:NCOL_B], par_b, ident[0:NCOL_B, 0:NCOL_B]).then_inc(par_turned, 1)
            pe.wait_ge(cnt_set, NT)
            for s in range(NT):
                for t in range(NT):
                    ins = pe.transpose(PS[:, 4 + t, s * P:(s + 1) * P], cnt[:, s, t * P:(t + 1) * P], ident[:])
            ins.then_inc(cntT_done, 1)

            pe.wait_ge(noise_in, 16 * 5)
            pe.wait_ge(emb_set, 1)
            mm(PS[0:NC, 6, 0:N], fw1[:], emb, True, True).then_inc(cond_a, 1)

            def turn(tr, ready, value):
                for t in range(NT):
                    pe.wait_ge(ready, value + (t + 1))
                    for c in range(CT):
                        ins = pe.transpose(chunks(0)[:, c, t * P:(t + 1) * P], xn[:, t, c * P:(c + 1) * P], ident[:])
                        if t == NT - 1 and c % 2:
                            ins.then_inc(tr_done, 1)

            def dense(bank, inT, i, done, ready, value):
                for t in range(NT):
                    for c in range(CT):
                        if t == 0 and c % 2 == 0 and ready is not None:
                            pe.wait_ge(ready, value + (c // 2 + 1))
                        ins = mm(PS[:, bank + t, :], inT[:, c, t * P:(t + 1) * P], wbuf[i][:, c, :], c == 0, c == CT - 1)
                    ins.then_inc(done, 1)

            def dense_T(bank, i, inT, done, ready, value):
                for o in range(CT):
                    for c in range(CT):
                        if o == 0 and c % 2 == 0 and ready is not None:
                            pe.wait_ge(ready, value + (c // 2 + 1))
                        ins = mm(chunks(bank)[:, o, :], wbuf[i][:, c, o * P:(o + 1) * P], inT[:, c, :], c == 0, c == CT - 1)
                    if o % 2:
                        ins.then_inc(done, 1)

            def layer0(l, first):
                def turn_weights(i, banks, done):
                    for o in range(CT):
                        for c in range(CT):
                            ins = pe.transpose(PS[:, banks[o], c * P:(c + 1) * P], wbuf[i][:, c, o * P:(o + 1) * P], ident[:])
                        ins.then_inc(done, 1)

                def spread_column(bank, col, done):
                    for c in range(CT):
                        ins = mm(PS[:, bank, c * P:(c + 1) * P], col[:, c:c + 1].to_broadcast([P, P]), ident[:], True, True)
                    ins.then_inc(done, 1)

                if not first:
                    pe.wait_ge(w_in[1], l * 16)
                    turn_weights(1, W1_BANKS, w1_turned)
                turn(l, ln_out, l * 2)
                if not first:
                    pe.wait_ge(w1T_set, l * CT)
                    pe.wait_ge(vn_in, l)
                    spread_column(2, vtmp, vn_spread)
                    pe.wait_ge(w_in[2], l * 16)
                    turn_weights(2, W2_BANKS, w2_turned)
                    pe.wait_ge(vn_sum, l)
                    mm(PS[:, 0, 0:1], ones[:], vsum[:, 0:1], True, True).then_inc(vn_mean, 1)
                    pe.wait_ge(vn_squares, l)
                    mm(PS[:, 1, 0:1], ones[:], vsum[:, 1:2], True, True).then_inc(vn_total, 1)
                    pe.wait_ge(vn_act, l)
                    spread_column(3, vhid, vn_act_spread)
                for b in range(2):
                    for val, bank, ready, done in ((m, 4, m_ready, mT_done), (md, 6, md_ready, mdT_done)):
                        pe.wait_ge(ready, l * 2 + (b + 1))
                        for c in range(2):
                            for t in range(NT):
                                ins = pe.transpose(halves(bank + b)[:, t, c * P:(c + 1) * P],
                                                   val[:, 2 * b + c, t * P:(t + 1) * P], ident[:])
                        ins.then_inc(done, 1)
                for val, bank, ready, done in ((ex, 0, ex_ready, den_done), (mex, 2, mex_ready, num_done)):
                    for c in range(CT):
                        if c % 2 == 0:
                            pe.wait_ge(ready, l * 2 + (c // 2 + 1))
                        for t in range(NT):
                            ins = mm(chunks(bank)[:, c, :], val[:, t, c * P:(c + 1) * P], cnt[:, t, :], t == 0, t == NT - 1)
                        if c % 2:
                            ins.then_inc(done, 1)
                pe.wait_ge(w_in[0], l * 32 + 32)
                for b in range(2):
                    pe.wait_ge(z_ready, l * 2 + (b + 1))
                    for t in range(NT):
                        for c in (2 * b, 2 * b + 1):
                            ins = mm(PS[:, 4 + t, :], z[:, c, t * P:(t + 1) * P], wbuf[0][:, c, :], c == 0, c == CT - 1)
                        if b:
                            ins.then_inc(conv_done, 1)

            pe.wait_ge(cols_set, 4)
            layer0(0, True)
            pe.wait_ge(cond_s, 1)
            mm(PS[0:NC, 7, 0:N], fw2[:], cz, True, True).then_inc(cond_b, 1)
            pe.wait_ge(cond_set, 1)
            with pe.Fori(1, LAYERS) as l:
                layer0(l, False)

            def table(k, i, b):
                pe.wait_ge(tabw_in[i], b * 64 + 64)
                for j in range(4):
                    t = j % 2
                    mm(PS[:, 4 + j, :], condT[:, t * P:(t + 1) * P], tabw[:, i, j // 2, :], True, True).then_inc(tab_done, 1)

            pe.wait_ge(ln_out, LN_L1_IN * 2 + 2)
            with pe.Fori(0, BLOCKS) as b:
                table(b * 2, 0, b)
                turn(b * 2 + TR_BLOCK, y_ready, b * 4)
                pe.wait_ge(w_in[3], b * 16 + 16)
                dense_T(2, 3, hT, q_done, yT_ready, b * 4)
                pe.wait_ge(tab_ready, b * 8 + 4)
                pe.wait_ge(w_in[4], b * 16 + 16)
                dense_T(4, 4, hT, k_done, None, 0)
                pe.wait_ge(q_ready, b * 4 + 4)
                for t in range(NT):
                    for hd in range(HEADS):
                        if t == 0:
                            pe.wait_ge(k_ready, b * 4 + (hd + 1))
                        ins = mm(chunks(2 * t)[:, hd, :], qT[:, hd, t * P:(t + 1) * P], kT[:, hd, :], True, True)
                        if hd % 2:
                            ins.then_inc(sc_done, 1)
                pe.wait_ge(smax_ready, b * 2 + 1)
                pe.wait_ge(w_in[5], b * 32 + 32)
                dense(0, hT, 5, v_done, None, 0)
                for t in range(NT):
                    for hd in range(HEADS):
                        pe.wait_ge(p_ready, b * 8 + (t * HEADS + hd + 1))
                        for dt in range(NT):
                            ins = pe.transpose(chunks(4 + 2 * dt)[:, hd, t * P:(t + 1) * P],
                                               prob[:, t, hd, dt * P:(dt + 1) * P], ident[:])
                            if t == 1 and hd % 2:
                                ins.then_inc(pT_done, 1)
                pe.wait_ge(v_ready, b * 2 + 2)
                for hd in range(HEADS):
                    if hd % 2 == 0:
                        pe.wait_ge(pT_act, b * 2 + (hd // 2 + 1))
                        pe.wait_ge(pT_dve, b * 2 + (hd // 2 + 1))
                    for dt in range(NT):
                        ins = mm(chunks(0)[:, hd, :], v[:, dt, hd * P:(hd + 1) * P], probT[:, dt, hd, :],
                                 dt == 0, dt == NT - 1)
                    if hd % 2:
                        ins.then_inc(o_done, 1)
                pe.wait_ge(w_in[0], b * 32 + (LAYERS + 1) * 32)
                dense(2, oT, 0, proj_done, o_ready, b * 2)
                table(b * 2 + 1, 1, b)
                turn(b * 2 + (TR_BLOCK + 1), y_ready, b * 4 + 2)
                pe.wait_ge(w_in[1], b * 16 + LAYERS * 16)
                dense_T(2, 1, hT, up_done, yT_ready, b * 4 + 2)
                pe.wait_ge(w_in[2], b * 32 + ((LAYERS - 1) * 16 + 32))
                pe.wait_ge(up_ready, b * 4 + 4)
                dense(0, mT, 2, down_done, None, 0)

            turn(TR_L2, ln_out, OUT_L2 * 2)
            pe.wait_ge(w_in[3], 16 * (BLOCKS + 1))
            dense(2, hT, 3, beta_done, yT_ready, 4 * BLOCKS)
            pe.wait_ge(w_in[5], 32 * (BLOCKS + 1))
            dense(4, hT, 5, alpha_done, None, 0)
            pe.wait_ge(beta_ready, 2)
            for s in range(NT):
                for t in range(NT):
                    ins = mm(PS[:, 6 + s, :], cntT[:, t, s * P:(s + 1) * P], v[:, t, :], t == 0, t == NT - 1)
                ins.then_inc(gamma_done, 1)

            def gather_part(tile, u, k):
                for s in range(NT):
                    ins = mm(PS[:, 2 + u, :], srcT[:, s, bass.ds(tile * P, P)], hs[:, k, s, :],
                             s == 0 and k == 0, s == NT - 1 and k == 2)
                return ins

            def gather(g, j, u):
                tile = j + g * TG
                pe.wait_ge(x1_ready, j + (g * TG + 1 - RING))
                for k in range(3):
                    ins = gather_part(tile, u, k)
                ins.then_inc(x1_done, 1)

            def gather_group(g):
                start = 0
                if g == 0:
                    for k in range(3):
                        pe.wait_ge(hs_ready, k + 1)
                        for j in range(RING):
                            ins = gather_part(j, j, k)
                            if k == 2:
                                ins.then_inc(x1_done, 1)
                    start = 1
                with pe.Fori(start, SIZES[g] // RING) as q:
                    for u in range(RING):
                        gather(g, q * RING + u, (g * TG + u) % RING)
                for j in range(SIZES[g] // RING * RING, SIZES[g]):
                    gather(g, j, (g * TG + j) % RING)

            def add_tile(g, j, u):
                pe.wait_ge(hotd_ready, j + (g * TG + 1))
                for t in range(NT):
                    ins = pe.matmul(PS[:, t, :], hotd[:, u, t * P:(t + 1) * P],
                                    part[SUM_AT[g]][:, bass.ds(j, 1), :].rearrange("p a d -> p (a d)"),
                                    start=False, stop=True, skip_group_check=True)
                ins.then_inc(tile_summed, 1)

            def sum_group(g):
                pe.wait_ge(path_step, (g + 1) * 2 * PATHS)
                with pe.Fori(0, SIZES[g] // RING) as q:
                    for u in range(RING):
                        add_tile(g, q * RING + u, (g * TG + u) % RING)
                for j in range(SIZES[g] // RING * RING, SIZES[g]):
                    add_tile(g, j, (g * TG + j) % RING)

            pe.wait_ge(srcT_set, SRC_CUT * NT)
            gather_group(0)
            gather_group(1)
            for g in range(GROUPS):
                sum_group(g)
                if g + 2 < GROUPS:
                    gather_group(g + 2)

        @block.vector
        def _(dve):
            steps = Steps(dve, dve_step)
            link = steps.link
            carried = []

            def carry():
                carried.append(0)
                dve.memset(idle[0:1, len(carried):len(carried) + 1], 0.0)

            def newton(y, a, w, o, n):
                for c in range(n):
                    ins = dve.scalar_tensor_tensor(out=a[:, c:c + 1], in0=y[:, c:c + 1], scalar=w[:, c:c + 1],
                                                   in1=y[:, c:c + 1], op0=ALU.mult, op1=ALU.mult)
                link(ins)
                link(dve.tensor_scalar(a, a, -0.5, 1.5, ALU.mult, ALU.add))
                link(dve.tensor_tensor(o, y, a, ALU.mult))

            def stats(t, inp):
                return dve.bn_stats(st[:, t, :], inp[:, t, :])

            def variance(n):
                carry()
                for t in range(NT):
                    ins = dve.bn_aggr(mv[:, t, :], st[:, t, :])
                ins.then_inc(ln_var, 1)
                dve.wait_ge(ln_var, n + 1)
                steps.mark(dve.tensor_scalar(var[:], mv[:, :, 1], LN_EPS, None, ALU.add))

            def refine(n):
                steps.await_marked()
                dve.wait_ge(ln_est, n + 1)
                newton(est[:], nwt[:], var[:], rstd[:], NT)

            def take_stats(inp):
                for t in range(NT):
                    ins = stats(t, inp)
                link(ins)

            def layer_norm(n, inp):
                variance(n)
                refine(n)
                for t in range(NT):
                    dve.tensor_scalar(xn[:, t, :], inp[:, t, :], mv[:, t, 0:1], rstd[:, t:t + 1],
                                      ALU.subtract, ALU.mult).then_inc(ln_out, 1)

            def residual(bank, done, value):
                for t in range(NT):
                    dve.wait_ge(done, value + (t + 1))
                    link(dve.tensor_tensor(h[:, t, :], PS[:, bank + t, :], h[:, t, :], ALU.add))
                    ins = stats(t, h)
                link(ins)

            def add_bias(i, to):
                for t in range(NT):
                    ins = dve.tensor_tensor(to[:, t, :], to[:, t, :], bias_of(i), ALU.add)
                ins.then_inc(bias_added, 1)

            dve.memset(path[:], 0).then_inc(path_clear, 1)
            dve.wait_ge(edges_in, 32)
            dve.tensor_copy(src_f[:], src_i[:]).then_inc(edges_f, 1)
            dve.tensor_copy(dst_f[:], dst_i[:]).then_inc(edges_f, 1)
            dve.tensor_scalar(dst_n[:], dst_i[:], -1.0, None, ALU.mult).then_inc(edges_f, 1)
            dve.tensor_scalar(src_n[:], src_i[:], -1.0, None, ALU.mult).then_inc(edges_f, 1)
            dve.memset(PS[:, 2:4, :], 0.0).then_inc(edges_f, 1)
            dve.wait_ge(edges_f, 5)
            dve.wait_ge(consts_set, CONSTS)

            def hot(tile, k):
                if k < HOT - BY_ACT:
                    dve.tensor_scalar(hot_s[:, k, :], iota_b[:], src_f[:, bass.ds(tile, 1)], None, ALU.is_equal).then_inc(hot_ready, 1)
                dve.tensor_scalar(hot_d[:, k, :], iota_b[:], dst_f[:, bass.ds(tile, 1)], None, ALU.is_equal).then_inc(hot_ready, 1)

            for k in range(HOT):
                hot(k, k)
            with dve.Fori(1, ET // HOT) as i:
                for k in range(HOT):
                    dve.wait_ge(hot_used, i * HOT + (k + 1 - HOT))
                    hot(i * HOT + k, k)
            dve.wait_ge(hot_used, ET)
            for s in range(NT):
                dve.tensor_copy(cnt[:, s, :], PS[:, 2 + s, 0:N]).then_inc(cnt_set, 1)
            dve.wait_ge(cnt_set, NT)
            link(dve.tensor_scalar(mask[:], cnt[:], 0.0, MASKED, ALU.is_equal, ALU.mult))
            link(dve.tensor_reduce(outdeg[:], cnt[:], AX.X, ALU.add))
            link(dve.reciprocal(outrec[:], outdeg[:]))
            dve.wait_ge(cntT_done, 1)
            for t in range(NT):
                dve.tensor_copy(cntT[:, t, :], PS[:, 4 + t, 0:N]).then_inc(cols_set, 1)
            dve.wait_ge(par_turned, 2)
            dve.tensor_copy(cols[:, 0:NCOL_A], PS[:, 0, 0:NCOL_A]).then_inc(cols_set, 1)
            dve.tensor_copy(cols[:, NCOL_A:], PS[:, 1, 0:NCOL_B]).then_inc(cols_set, 1)
            dve.wait_ge(cols_set, 4)

            dve.wait_ge(path_in, 32)
            dve.wait_ge(path_clear, 1)
            table = path[0:1, :].rearrange("a (r k) -> a r k", k=4)
            raw = path_raw[0:1, :].rearrange("a (r k) -> a r k", k=3)
            dve.tensor_scalar(table[:, 0:PATHS, 0:2], raw[:, :, 0:2], EXT, None, ALU.mult)
            link(dve.tensor_scalar(table[:, AHEAD:, 2:3], raw[:, :, 2:3], EXT, None, ALU.mult))
            def vn_product(bank, wT):
                for o in range(CT):
                    ins = dve.tensor_tensor_reduce(out=scrap[:, o, :], in0=PS[:, bank, :], in1=wT[:, o, :], scale=1.0,
                                                   scalar=0.0, op0=ALU.mult, op1=ALU.add, accum_out=vhid[:, o:o + 1])
                link(ins)

            dve.wait_ge(cond_a, 1)
            dve.tensor_scalar(cz, PS[0:NC, 6, 0:N], fb[:, 0:1], None, ALU.add).then_inc(cond_z, 1)

            def layer0(l, first):
                layer_norm(l, x if first else h)
                dve.wait_ge(hT_ready, l * CT + CT)
                if first:
                    link(dve.tensor_copy(vn[:], cols[:, COL["vn_emb"]:COL["vn_emb"] + CT]))
                    dve.tensor_reduce(hmax[:], hT[:], AX.X, ALU.max)
                else:
                    def par(name):
                        return cols[:, bass.ds(l * CT + (COL[name] - CT), CT)]

                    dve.tensor_tensor(vtmp[:], hsum[:], vn[:], ALU.add).then_inc(vn_in, 1)
                    link(dve.tensor_reduce(hmax[:], hT[:], AX.X, ALU.max))
                    dve.wait_ge(vn_spread, l)
                    dve.wait_ge(w1T_set, l * CT)
                    vn_product(2, w1T)
                    link(dve.tensor_tensor(vhid[:], vhid[:], par("vn_b1"), ALU.add))
                    dve.tensor_reduce(vsum[:, 0:1], vhid[:], AX.X, ALU.add).then_inc(vn_sum, 1)
                    dve.wait_ge(vn_mean, l)
                    link(dve.scalar_tensor_tensor(out=vcen[:], in0=PS[:, 0, 0:1].to_broadcast([P, CT]), scalar=-1.0 / D,
                                                  in1=vhid[:], op0=ALU.mult, op1=ALU.add))
                    dve.tensor_tensor_reduce(out=vsq[:], in0=vcen[:], in1=vcen[:], scale=1.0, scalar=0.0,
                                             op0=ALU.mult, op1=ALU.add, accum_out=vsum[:, 1:2]).then_inc(vn_squares, 1)
                    dve.wait_ge(vn_total, l)
                    dve.tensor_scalar(vvar[:, 0:1], PS[:, 1, 0:1], 1.0 / D, LN_EPS, ALU.mult, ALU.add).then_inc(vn_var, 1)
                    dve.wait_ge(vn_est, l)
                    dve.wait_ge(vn_var, l)
                    newton(vvar[:, 2:3], vvar[:, 3:4], vvar[:, 0:1], rstd[:, 0:1], 1)
                    link(dve.scalar_tensor_tensor(out=vhid[:], in0=vcen[:], scalar=rstd[:, 0:1], in1=par("vn_g"),
                                                  op0=ALU.mult, op1=ALU.mult))
                    link(dve.tensor_tensor(vhid[:], vhid[:], par("vn_beta"), ALU.add))
                    dve.tensor_scalar(vhid[:], vhid[:], 0.0, None, ALU.max).then_inc(vn_act, 1)
                    dve.wait_ge(vn_act_spread, l)
                    dve.wait_ge(w2T_set, l * CT)
                    vn_product(3, w2T)
                    link(dve.tensor_tensor(vn[:], vhid[:], par("vn_b2"), ALU.add))
                link(dve.tensor_scalar(vne[:], vn[:], MSG_EPS, None, ALU.add))
                dve.tensor_tensor(mmax[:], hmax[:], vne[:], ALU.add)
                for b in range(2):
                    for c in (2 * b, 2 * b + 1):
                        ins = dve.tensor_scalar(m[:, c, :], hT[:, c, :], vne[:, c:c + 1], MSG_EPS, ALU.add, ALU.max)
                    ins.then_inc(m_ready, 1)
                    dve.wait_ge(m_ready, l * 2 + (b + 1))
                    if b == 0:
                        link(dve.tensor_scalar(mmax[:], mmax[:], MSG_EPS, None, ALU.max))
                    for c in (2 * b, 2 * b + 1):
                        ins = dve.tensor_scalar(md[:, c, :], m[:, c, :], mmax[:, c:c + 1], None, ALU.subtract)
                    ins.then_inc(md_ready, 1)
                for c in range(CT):
                    ins = dve.tensor_scalar(hv[:, c, :], hT[:, c, :], vn[:, c:c + 1], None, ALU.add)
                for b in range(2):
                    half = slice(b * N, (b + 1) * N)
                    dve.wait_ge(mT_done, l * 2 + (b + 1))
                    dve.wait_ge(ex_ready, l * 2 + (b + 1))
                    dve.tensor_tensor(mex[:, :, half], halves(4 + b), ex[:, :, half], ALU.mult).then_inc(mex_ready, 1)
                for b in range(2):
                    two = slice(2 * b, 2 * b + 2)
                    dve.wait_ge(rec_est, l * 2 + (b + 1))
                    link(dve.tensor_tensor(z[:, two, :], chunks(0)[:, two, :], rec[:, two, :], ALU.mult))
                    link(dve.scalar_tensor_tensor(out=z[:, two, :], in0=z[:, two, :], scalar=-2.0,
                                                  in1=rec[:, two, :], op0=ALU.add, op1=ALU.mult))
                    dve.wait_ge(num_done, l * 2 + (b + 1))
                    link(dve.tensor_tensor(z[:, two, :], chunks(2)[:, two, :], z[:, two, :], ALU.mult))
                    dve.tensor_tensor(z[:, two, :], hv[:, two, :], z[:, two, :], ALU.subtract).then_inc(z_ready, 1)
                if first:
                    dve.wait_ge(cond_e, 1)
                    dve.wait_ge(cond_z, 1)
                    link(dve.tensor_scalar(ce, ce, 1.0, None, ALU.add))
                    link(dve.reciprocal(ce, ce))
                    dve.tensor_tensor(cz, cz, ce, ALU.mult).then_inc(cond_s, 1)
                    dve.wait_ge(w_in[0], 32)
                    for t in range(NT):
                        dve.wait_ge(conv_done, t + 1)
                        ins = dve.tensor_tensor(h[:, t, :], PS[:, 4 + t, :], bias_of(0), ALU.add)
                    ins.then_inc(bias_added, 1)
                    dve.wait_ge(bias_added, 1)
                    take_stats(h)
                else:
                    dve.wait_ge(w_in[0], l * 32 + 32)
                    carry()
                    add_bias(0, h)
                    dve.wait_ge(bias_added, l + 1)
                    residual(4, conv_done, l * 2)

            dve.wait_ge(x_in, 16)
            take_stats(x)
            layer0(0, True)
            with dve.Fori(1, LAYERS) as l:
                steps.enter(l - 1, 26)
                layer0(l, False)
            steps.leave(LAYERS - 1)

            layer_norm(LN_L0_LAST, h)
            dve.wait_ge(ln_out, LN_L0_LAST * 2 + 2)
            dve.wait_ge(gb_in, 32)
            for k, op in ((0, ALU.mult), (1, ALU.add)):
                for t in range(NT):
                    ins = dve.tensor_tensor(xn[:, t, :], xn[:, t, :], gb[:, k, :], op)
                link(ins)
            link(dve.tensor_tensor(x[:], x[:], xn[:], ALU.add))
            take_stats(x)
            layer_norm(LN_L1_IN, x)
            dve.wait_ge(ln_out, LN_L1_IN * 2 + 2)
            link(dve.tensor_scalar(h[:], xn[:], 0.0, None, ALU.max))
            take_stats(h)

            def cond_norm(k):
                variance(k + LN_BLOCK)
                for t in range(NT):
                    dve.wait_ge(tab_ready, k * 4 + (t + 1))
                    ins = dve.scalar_tensor_tensor(out=xn[:, t, :], in0=h[:, t, :], scalar=mv[:, t, 0:1],
                                                   in1=tab[:, 0, t, :], op0=ALU.subtract, op1=ALU.mult)
                link(ins)
                refine(k + LN_BLOCK)
                for t in range(NT):
                    dve.wait_ge(tab_ready, k * 4 + (t + 3))
                    dve.scalar_tensor_tensor(out=xn[:, t, :], in0=xn[:, t, :], scalar=rstd[:, t:t + 1],
                                             in1=tab[:, 1, t, :], op0=ALU.mult, op1=ALU.add).then_inc(y_ready, 1)

            with dve.Fori(0, BLOCKS) as b:
                steps.enter(b, 24)
                cond_norm(b * 2)
                dve.wait_ge(w_in[0], b * 32 + (LAYERS + 1) * 32)
                carry()
                add_bias(0, h)
                for hd in range(HEADS):
                    dve.wait_ge(k_done, b * 2 + (hd // 2 + 1))
                    dve.tensor_scalar(kT[:, hd, :], chunks(4)[:, hd, :], cols[:, bass.ds(b * CT + (COL["bk"] + hd), 1)],
                                      None, ALU.add).then_inc(k_ready, 1)
                for t in range(NT):
                    for hd in range(HEADS):
                        k = t * HEADS + hd
                        if hd % 2 == 0:
                            dve.wait_ge(sc_done, b * 4 + (2 * t + hd // 2 + 1))
                            carry()
                        ins = dve.tensor_tensor_reduce(out=prob[:, t, hd, :], in0=chunks(2 * t)[:, hd, :],
                                                       in1=mask[:, t, :], scale=float(DH) ** -0.5, scalar=-3e38,
                                                       op0=ALU.add, op1=ALU.max, accum_out=smax[:, k:k + 1])
                    link(ins)
                    four = slice(t * HEADS, (t + 1) * HEADS)
                    dve.tensor_scalar(nmax[:, four], smax[:, four], -1.0, None, ALU.mult).then_inc(smax_ready, 1)
                for t in range(NT):
                    four = slice(t * HEADS, (t + 1) * HEADS)
                    for hd in range(HEADS):
                        k = t * HEADS + hd
                        dve.wait_ge(exp_ready, b * 8 + (k + 1))
                        ins = dve.tensor_tensor_reduce(out=prob[:, t, hd, :], in0=prob[:, t, hd, :],
                                                       in1=cnt[:, t, :], scale=1.0, scalar=0.0,
                                                       op0=ALU.mult, op1=ALU.add, accum_out=den[:, k:k + 1])
                    link(ins)
                    link(dve.tensor_scalar(den[:, four], den[:, four], TINY, None, ALU.max))
                    link(dve.reciprocal(rden[:, four], den[:, four]))
                    for hd in range(HEADS):
                        k = t * HEADS + hd
                        dve.tensor_scalar(prob[:, t, hd, :], prob[:, t, hd, :], rden[:, k:k + 1], None,
                                          ALU.mult).then_inc(p_ready, 1)
                    if t == 0:
                        dve.wait_ge(w_in[5], b * 32 + 32)
                    dve.wait_ge(v_done, b * 2 + (t + 1))
                    dve.tensor_tensor(v[:, t, :], PS[:, t, :], bias_of(5), ALU.add).then_inc(v_ready, 1)
                for i in range(2):
                    dve.wait_ge(pT_done, b * 4 + (2 * i + 2))
                    dve.tensor_copy(probT[:, 1, 2 * i:2 * i + 2, :], chunks(6)[:, 2 * i:2 * i + 2, :]).then_inc(pT_dve, 1)
                dve.wait_ge(bias_added, b * 2 + (LAYERS + 1))
                residual(2, proj_done, b * 2)
                cond_norm(b * 2 + 1)
                dve.wait_ge(w_in[2], b * 32 + ((LAYERS - 1) * 16 + 32))
                carry()
                add_bias(2, h)
                dve.wait_ge(bias_added, b * 2 + (LAYERS + 2))
                residual(0, down_done, b * 2)
            steps.leave(BLOCKS)
            link(dve.tensor_tensor(x[:], x[:], h[:], ALU.add))

            take_stats(x)
            layer_norm(LN_L2, x)
            dve.wait_ge(ln_out, OUT_L2 * 2 + 2)
            dve.wait_ge(w_in[5], 32 * (BLOCKS + 1))
            add_bias(5, x)
            dve.wait_ge(bias_added, LAYERS + 2 * BLOCKS + 1)
            for t in range(NT):
                dve.wait_ge(alpha_done, t + 1)
                ins = dve.tensor_tensor(x[:, t, :], PS[:, 4 + t, :], x[:, t, :], ALU.add)
            link(ins)
            for t in range(NT):
                dve.wait_ge(gamma_done, t + 1)
                link(dve.scalar_tensor_tensor(out=x[:, t, :], in0=PS[:, 6 + t, :], scalar=outrec[:, t:t + 1],
                                              in1=x[:, t, :], op0=ALU.mult, op1=ALU.add))
                ins = stats(t, x)
            link(ins)
            layer_norm(LN_L3, x)
            dve.wait_ge(ln_out, OUT_L3 * 2 + 2)
            link(dve.tensor_scalar(h[:], xn[:], 0.0, None, ALU.max))
            dve.tensor_copy(hs[:, 0, :, :], h[:]).then_inc(hs_ready, 1)
            dve.wait_ge(hs_ready, 1)
            link(dve.tensor_tensor(h[:], h[:], hs[:, 0, :, :], ALU.subtract))
            dve.tensor_copy(hs[:, 1, :, :], h[:]).then_inc(hs_ready, 1)
            dve.wait_ge(hs_ready, 2)
            dve.tensor_tensor(hs[:, 2, :, :], h[:], hs[:, 1, :, :], ALU.subtract).then_inc(hs_ready, 1)
            dve.memset(PS[:, 0:NT, :], 0.0)

            regs = [[dve.alloc_register(f"path{u}_{k}") for k in range(4)] for u in range(RING)]
            for g in range(GROUPS):
                dve.wait_ge(x2_in[g], 16)
                dve.wait_ge(x1_ready, min((g + 1) * TG, ET))
                n = SIZES[g]
                xs, xe, sums = (part[at[g]][:, 0:n, :] for at in (SOURCE_AT, EDGE_AT, SUM_AT))

                def path_rows(row, lo, n_rows, slot, first_sums=False):
                    dve.load([r for four in regs[0:n_rows] for r in four], path[0:1, bass.ds(row * 4, 4 * n_rows)])
                    for j in range(n_rows):
                        i1, i2, i3 = (dve.snap(r, min_val=0, max_val=(SEGS - 1) * EXT) for r in regs[j][0:3])
                        if j == 0 and first_sums:
                            dve.wait_ge(acc_zero, (g + 1) * 3)
                        if lo + j >= AHEAD:
                            dve.wait_ge(path_step, row * 2 + (g * 2 * PATHS + 2 * j + 1 - 2 * AHEAD))
                            o = sums[:, :, bass.ds(i3, EXT)]
                            dve.tensor_tensor(o, o, prod[:, (slot + j - AHEAD) % RING, 0:n, :], ALU.add).then_inc(path_step, 1)
                        if lo + j < PATHS:
                            dve.scalar_tensor_tensor(
                                out=prod[:, (slot + j) % RING, 0:n, :], in0=xs[:, :, bass.ds(i1, EXT)],
                                scalar=coef[:, bass.ds(row + j, 1)], in1=xe[:, :, bass.ds(i2, EXT)],
                                op0=ALU.mult, op1=ALU.mult).then_inc(path_step, 1)

                path_rows(0, 0, AHEAD, 0)
                dve.memset(part[SUM_AT[g]][:, 0:ZERO_CUT[0], :], 0.0).then_inc(acc_zero, 1)
                path_rows(AHEAD, AHEAD, RING, AHEAD, first_sums=True)
                with dve.Fori(0, PATHS // RING // 2 - 1) as q:
                    for half in range(2):
                        path_rows(q * (2 * RING) + (half * RING + RING + AHEAD), AHEAD, RING, AHEAD)
                last = PATHS - RING + AHEAD
                path_rows(last, last, RING, last % RING)
            for t in range(NT):
                dve.wait_ge(tile_summed, ET)
                dve.tensor_tensor(x[:, t, :], PS[:, t, :], x[:, t, :], ALU.add).then_inc(final, 1)


_OUTS = [((N, D), "float32")]


def kernel(**inputs):
    import numpy as _np
    import concourse.bacc as _bacc
    from concourse import mybir as _mybir
    from concourse.bass_utils import run_bass_kernel_spmd as _run

    nc = _bacc.Bacc("TRN2", target_bir_lowering=False, num_devices=1)
    arrays, args = {}, {}
    for name in inputs:
        a = _np.ascontiguousarray(inputs[name])
        arrays[f"in_{name}_dram"] = a
        args[name] = nc.dram_tensor(f"in_{name}_dram", a.shape, _mybir.dt.from_np(a.dtype), kind="ExternalInput").ap()
    shape, dtype = _OUTS[0]
    out = nc.dram_tensor("out_0_dram", shape, _mybir.dt.from_np(_np.dtype(dtype)), kind="ExternalOutput").ap()
    gnn_stack_kernel(nc, args, out)
    r = _run(nc, [arrays], core_ids=[0])
    return r.results[0]["out_0_dram"]
```
